# Optimizing a Trainium2 kernel written in Bass

```python
import numpy as np
import jax
import jax.numpy as jnp

def _softmax(x, axis=-1):
    return jax.nn.softmax(x, axis=axis)

def _gelu(x):
    return jax.nn.gelu(x, approximate=True)

def _silu(x):
    return jax.nn.silu(x)

def _sigmoid(x):
    return jax.nn.sigmoid(x)

def _layernorm(x, axis=-1, eps=1e-05):
    m = jnp.mean(x, axis=axis, keepdims=True)
    v = jnp.var(x, axis=axis, keepdims=True)
    return (x - m) / jnp.sqrt(v + eps)

def _scatter_add(tgt, idx, src, axis=0):
    return tgt.at[idx].add(src)

def _segment_sum(src, seg, n):
    return jax.ops.segment_sum(src, seg, n)
kernel_name = 'mk_prb_d1_jaxref_r4_df6d34'

def setup_inputs(seed: int=0):
    np.random.seed(seed)
    _w = jnp.asarray

    def _L0_attn_setup():
        import jax, jax.numpy as jnp
        import numpy as np
        EMBED_DIM = 256
        NUM_HEADS = 16
        HEAD_DIM = EMBED_DIM // NUM_HEADS
        BATCH = 2
        SEQ = 512
        NEG_INF = float('-inf')
        key = jax.random.key(seed)
        k1, k2, k3, k4, k5 = jax.random.split(key, 5)
        return {'query': jax.random.normal(k1, (BATCH, SEQ, EMBED_DIM), dtype=jnp.float32), 'key': jax.random.normal(k2, (BATCH, SEQ, EMBED_DIM), dtype=jnp.float32), 'value': jax.random.normal(k3, (BATCH, SEQ, EMBED_DIM), dtype=jnp.float32), 'in_proj_weight': jax.random.normal(k4, (3 * EMBED_DIM, EMBED_DIM), dtype=jnp.float32) * (1.0 / np.sqrt(EMBED_DIM)), 'out_proj_weight': jax.random.normal(k5, (EMBED_DIM, EMBED_DIM), dtype=jnp.float32) * (1.0 / np.sqrt(EMBED_DIM))}
    _L0_attn_in = _L0_attn_setup()

    def _L0_ffn_setup():
        import jax, jax.numpy as jnp
        import numpy as np
        TOP_K = 2
        CAP_FACTOR = 1.25
        EPS = 1.1920929e-07
        key = jax.random.key(seed)
        ks = jax.random.split(key, 6)
        B, S, D, E, H = (8, 512, 256, 8, 1024)
        return {'hidden_states': jax.random.normal(ks[0], (B, S, D), jnp.float32), 'wg': jax.random.normal(ks[1], (D, E), jnp.float32) * 0.02, 'fc1_w': jax.random.normal(ks[2], (E, H, D), jnp.float32) * 0.02, 'fc1_b': jnp.zeros((E, H), jnp.float32), 'fc2_w': jax.random.normal(ks[3], (E, H, D), jnp.float32) * 0.02, 'fc2_b': jnp.zeros((E, D), jnp.float32), 'ln_gamma': jnp.ones((D,), jnp.float32), 'ln_beta': jnp.zeros((D,), jnp.float32)}
    _L0_ffn_in = _L0_ffn_setup()
    _d = {'L0_attn_query': _L0_attn_in['query'], 'L0_attn_key': _L0_attn_in['key'], 'L0_attn_value': _L0_attn_in['value'], 'L0_attn_in_proj_weight': _L0_attn_in['in_proj_weight'], 'L0_attn_out_proj_weight': _L0_attn_in['out_proj_weight'], 'L0_ffn_wg': _L0_ffn_in['wg'], 'L0_ffn_fc1_w': _L0_ffn_in['fc1_w'], 'L0_ffn_fc1_b': _L0_ffn_in['fc1_b'], 'L0_ffn_fc2_w': _L0_ffn_in['fc2_w'], 'L0_ffn_fc2_b': _L0_ffn_in['fc2_b'], 'L0_ffn_ln_gamma': _L0_ffn_in['ln_gamma'], 'L0_ffn_ln_beta': _L0_ffn_in['ln_beta']}
    _x0 = _d['L0_attn_query']
    _d['L0_attn_query'] = jax.random.normal(jax.random.fold_in(jax.random.key(seed), 1), (1, 4096, 256), dtype=_x0.dtype)
    del _x0
    return _d

def reference(L0_attn_query, L0_attn_key, L0_attn_value, L0_attn_in_proj_weight, L0_attn_out_proj_weight, L0_ffn_wg, L0_ffn_fc1_w, L0_ffn_fc1_b, L0_ffn_fc2_w, L0_ffn_fc2_b, L0_ffn_ln_gamma, L0_ffn_ln_beta):

    def _L0_attn_ref(query, key, value, in_proj_weight, out_proj_weight):
        import jax, jax.numpy as jnp
        import numpy as np
        EMBED_DIM = 256
        NUM_HEADS = 16
        HEAD_DIM = EMBED_DIM // NUM_HEADS
        BATCH = 2
        SEQ = 512
        NEG_INF = float('-inf')
        B, T, E = query.shape
        H, D = (NUM_HEADS, HEAD_DIM)
        projected = jnp.einsum('bte,fe->btf', query, in_proj_weight)
        packed = projected.reshape(B, T, 3, H, D).transpose(0, 3, 2, 1, 4)
        q, k, v = (packed[:, :, 0], packed[:, :, 1], packed[:, :, 2])
        q = q / jnp.sqrt(jnp.asarray(D, dtype=q.dtype))
        attention = jnp.einsum('bhtd,bhkd->bhtk', q, k)
        qpos = jnp.arange(T)[:, None]
        kpos = jnp.arange(T)[None, :]
        mask = jnp.where(qpos - kpos >= 0, 0.0, NEG_INF).astype(attention.dtype)
        attention = attention + mask[None, None]
        activation = jax.nn.softmax(attention, axis=-1)
        x = jnp.einsum('bhtk,bhkd->bhtd', activation, v)
        x = x.transpose(0, 2, 1, 3).reshape(B, T, E)
        out = jnp.einsum('bte,fe->btf', x, out_proj_weight)
        return out

    def _L0_ffn_ref(hidden_states, wg, fc1_w, fc1_b, fc2_w, fc2_b, ln_gamma, ln_beta):
        import jax, jax.numpy as jnp
        import numpy as np
        TOP_K = 2
        CAP_FACTOR = 1.25
        EPS = 1.1920929e-07
        B, S, D = hidden_states.shape
        E = wg.shape[1]
        N = B * S
        k = TOP_K
        C = k * int(CAP_FACTOR * ((N + E - 1) // E))
        x = hidden_states.reshape(N, D)
        scores = jax.nn.softmax(x @ wg, axis=-1)
        gates, idx = jax.lax.top_k(scores, k)
        gates = gates / jnp.clip(jnp.sum(gates, -1, keepdims=True), EPS)
        masks = jax.nn.one_hot(idx, E, dtype=jnp.int32)
        counts = masks.sum(0)
        offsets = jnp.concatenate([jnp.zeros((1, E), jnp.int32), jnp.cumsum(counts, 0)[:-1]], 0)
        loc = jnp.cumsum(masks, 0) - 1 + offsets[None]
        loc_sel = (loc * masks).sum(-1)
        keep = loc_sel < C
        gates = gates * keep.astype(gates.dtype)
        pos = jnp.where(keep, idx * C + loc_sel, E * C)
        xk = jnp.broadcast_to(x[:, None, :], (N, k, D)).reshape(N * k, D)
        buf = jnp.zeros((E * C + 1, D), x.dtype).at[pos.reshape(-1)].set(xk)
        disp = buf[:E * C].reshape(E, C, D)
        h = jax.nn.silu(jnp.einsum('ecd,ehd->ech', disp, fc1_w) + fc1_b[:, None, :])
        y = jnp.einsum('ech,ehd->ecd', h, fc2_w) + fc2_b[:, None, :]
        ybuf = jnp.concatenate([y.reshape(E * C, D), jnp.zeros((1, D), y.dtype)], 0)
        combined = jnp.sum(gates[..., None] * ybuf[pos], axis=1)
        res = hidden_states + combined.reshape(B, S, D)
        mu = jnp.mean(res, -1, keepdims=True)
        var = jnp.var(res, -1, keepdims=True)
        return (res - mu) * jax.lax.rsqrt(var + 1e-05) * ln_gamma + ln_beta
    x = L0_attn_query
    xn = _layernorm(x, axis=-1)
    x = x + _L0_attn_ref(xn, L0_attn_key, L0_attn_value, L0_attn_in_proj_weight, L0_attn_out_proj_weight) + _L0_ffn_ref(xn, L0_ffn_wg, L0_ffn_fc1_w, L0_ffn_fc1_b, L0_ffn_fc2_w, L0_ffn_fc2_b, L0_ffn_ln_gamma, L0_ffn_ln_beta)
    return x

_drawn_inputs = setup_inputs


def setup_inputs(seed=0):
    import zlib

    import numpy as np

    out = dict(_drawn_inputs(seed))
    spreads = {'L0_ffn_fc1_b': (0.0, 0.66),
     'L0_ffn_fc2_b': (0.0, 0.1),
     'L0_ffn_ln_gamma': (1.0, 0.2),
     'L0_ffn_ln_beta': (0.0, 0.1)}
    factors = {}
    for name, (base, spread) in spreads.items():
        noise = np.random.default_rng([zlib.crc32(name.encode()), seed]).standard_normal(out[name].shape)
        drawn = base * np.exp(spread * noise) if base else spread * noise
        out[name] = jnp.asarray(drawn.astype(out[name].dtype))
    for name, factor in factors.items():
        out[name] = (out[name] * factor).astype(out[name].dtype)
    return out
```

```python
from contextlib import ExitStack

import concourse.bass as bass
from concourse import mybir

F32 = mybir.dt.float32
BF16 = mybir.dt.bfloat16
I32 = mybir.dt.int32
ACT = mybir.ActivationFunctionType
ALU = mybir.AluOpType
AX = mybir.AxisListType

P = 128
T, D = 4096, 256
NH, DH = 16, 16
E, HID, TOPK = 8, 1024, 2
CAP = TOPK * int(1.25 * ((T + E - 1) // E))
NT = T // P
DC = D // P
CH = 512
NC = T // CH
TPC = CH // P
ROUNDS = E
assert ROUNDS * 2 == NH
Q_PARTS = (0, 0, 1, 1, 0, 2)
K_PARTS = (0, 1, 0, 1, 2, 0)
ROWS = 6 * DH
AUG = ROWS + 2
LN_EPS = 1e-5
GATE_EPS = 1.1920929e-07
MASKED = -1e30
SLABS = 5
SLAB_T = CAP // P // SLABS
BT = TPC
NB = NT // BT
HC = HID // P
VW = 32
OW = DH + 1

M_RING, S_RING, F_RING = 3, 2, 1
P_SLOTS, GROUP = 8, 4


def round_steps():
    experts = []
    for f in range(SLABS):
        if f == 0:
            experts += [("X", 0)] + [("H", 0, 0, s) for s in range(4)]
        for u in range(1, HC // 2):
            experts += [("H", f, u, s) for s in range(4)]
        if f + 1 < SLABS:
            experts += [("X", f + 1)] + [("H", f + 1, 0, s) for s in range(4)]
        experts += [("Y", f, s) for s in range(16)]

    maxima = []
    for c in range(NC):
        maxima += [("M", h, t, j) for t in range(TPC * c, TPC * c + TPC) for j in range(c + 1) for h in range(2)]
        maxima += [("N", c), ("R", c)]
    scored = [("S", c, h, 2 * g + b) for c in range(NC) for g in range(2 * c + 2) for b in range(2) for h in range(2)]
    sums = [("V", c, g, g == 2 * c + 1) for c in range(NC) for g in range(2 * c + 2)]

    hop, row_trip = 120, 2700
    pe = dve = act = pool = 0.0
    m_free, s_free, f_free = [0.0] * M_RING, [0.0] * S_RING, [0.0] * F_RING
    slot_free, bank_v, o_bufs, row_use = [0.0] * (P_SLOTS // GROUP), 0.0, [0.0, 0.0], 0.0
    neg_at, rows_at, prob_at, done = {}, {}, {}, {}
    n_m = n_s = n_f = n_v = 0
    o_due = []
    out = []
    total = 1.1 * (sum(217 for _ in scored) * 2 + 900 * len(sums) + 430 * len(experts))
    spent = 0.0

    def width(x):
        if x[0] == "M":
            return (x[2] % TPC + 1) * P if x[3] == x[2] // TPC else CH
        return CH - max(0, x[3] - TPC * x[1]) * P

    while maxima or scored or sums or experts or o_due:
        choice = []
        if maxima:
            x = maxima[0]
            if x[0] == "M":
                choice.append((m_free[n_m % M_RING], 2, "m", x))
            elif x[0] == "N":
                choice.append((0.0, -1, "m", x))
            else:
                choice.append((max(neg_at[x[1]], row_use), 0, "m", x))
        if scored:
            x = scored[0]
            ready = rows_at.get(x[1])
            ahead = n_m - n_s >= AHEAD * (x[1] + 1) + AHEAD_0 or maxima == []
            if ready is not None and ahead and n_s // GROUP - n_v < P_SLOTS // GROUP:
                choice.append((max(ready, s_free[n_s % S_RING]), 1, "s", x))
        if sums and (n_v + 1) * GROUP <= n_s:
            x = sums[0]
            choice.append((max(prob_at[n_v], bank_v if x[2] == 0 else 0.0), 0.5, "v", x))
        if o_due:
            choice.append((max(o_due[0][0], row_use), 0.7, "o", o_due[0][1]))
        if experts:
            x = experts[0]
            at = 0.0
            if x[0] != "H" or x[3] == 0:
                if x[0] != "Y" or x[2] == 0:
                    at = f_free[n_f % F_RING]
            if x[0] == "H" and x[2] == 0 and x[3] == 0:
                at = max(at, done[("X", x[1])])
            if x[0] == "Y" and x[2] == 0:
                at = max(at, done[("H", x[1], HC // 2 - 1)])
            share = 1 - len(experts) / (SLABS * 33)
            choice.append((at, 0.8 if share < F_PACE * spent / total else 3, "f", x))
        ready = [ch for ch in choice if ch[0] <= pe + 20]
        at, _, stream, x = min(ready, key=lambda ch: ch[1]) if ready else min(choice, key=lambda ch: ch[:2])
        pe = max(pe, at)
        out.append(x)
        cost = 0.0
        if stream == "m":
            maxima.pop(0)
            if x[0] == "M":
                w = width(x)
                cost = w / 2.4 + 3 + (56 if x[3] == x[2] // TPC else 0)
                dve = max(dve, pe + cost + hop) + (w + 62) / 0.96
                m_free[n_m % M_RING] = dve + hop
                n_m += 1
            elif x[0] == "N":
                dve += 700
                neg_at[x[1]] = dve + hop
            else:
                cost = 60
                dve = max(dve, pe + cost + hop) + 250
                row_use = dve + hop
                rows_at[x[1]] = dve + row_trip
        elif stream == "s":
            scored.pop(0)
            w = width(x)
            cost = w / 2.4 + 3 + (56 if x[3] >= TPC * x[1] else 0)
            act = max(act, pe + cost + hop, slot_free[n_s // GROUP % (P_SLOTS // GROUP)]) + (w + 70) / 1.2
            s_free[n_s % S_RING] = act + hop
            prob_at[n_s // GROUP] = act + hop
            n_s += 1
        elif stream == "v":
            sums.pop(0)
            cost = 900
            slot_free[n_v % (P_SLOTS // GROUP)] = pe + cost + hop
            n_v += 1
            if x[3]:
                act = max(act, pe + cost + hop) + 480
                bank_v = act + hop
                o_due.append((act + hop, ("O", x[1])))
        elif stream == "o":
            o_due.pop(0)
            cost = 130
            dve = max(dve, pe + cost + hop) + 600
            row_use = dve + hop
        else:
            experts.pop(0)
            cost = 430
            item = x[:3] if x[0] == "H" else x[:2]
            if x[0] == "X":
                dve = max(dve, pe + cost + hop) + 600
            elif x[0] == "H" and x[3] == 3:
                act = max(act, pe + cost + hop) + 2 * 310
                pool = max(pool, act + hop) + 550
                dve = max(dve, pool + hop) + 800
            elif x[0] == "Y" and x[2] == 15:
                dve = max(dve, pe + cost + hop) + 600
            if x[0] == "X" or x[-1] == (3 if x[0] == "H" else 15):
                f_free[n_f % F_RING] = done[item] = dve + hop
                n_f += 1
        pe += cost
        spent += cost
    round_steps.length = pe
    return out


AHEAD, AHEAD_0, F_PACE = 8, 8, 0.6
STEPS = round_steps()


def numbered(kinds, key=lambda x: x):
    return {key(x): n for n, x in enumerate([x for x in STEPS if x[0] in kinds])}


M_AT = numbered("M")
S_AT = numbered("S")
V_AT = numbered("V")
ROW_AT = numbered("RO")
N_M, N_S, N_V, N_ROW = len(M_AT), len(S_AT), len(V_AT), len(ROW_AT)
ITEMS = [x[:3] if x[0] == "H" else x[:2] for x in STEPS
         if x[0] == "X" or (x[0] in "HY" and x[-1] == 0)]
ITEM_AT = {x: n for n, x in enumerate(ITEMS)}
HIDDEN_AT = {x: n for n, x in enumerate([x for x in ITEMS if x[0] == "H"])}
N_F, N_H = len(ITEMS), len(HIDDEN_AT)


class Waits:

    def __init__(self, engine, sem, per_pass, start=0, wait=None):
        self.wait = wait or engine.wait_ge
        self.engine, self.sem, self.per_pass, self.start, self.at = engine, sem, per_pass, start, start
        self.reg = engine.alloc_register(f"{engine.engine.name}_{sem.name}_{start}_{engine.bass.next_id()}")
        engine.reg_mov(self.reg, start)
        self.waited = False

    def reach(self, value):
        if value > self.at or not self.waited:
            if value > self.at:
                self.engine.reg_add(self.reg, self.reg, value - self.at)
                self.at = value
            self.waited = True
            self.wait(self.sem, self.reg)

    def end_pass(self):
        self.engine.reg_add(self.reg, self.reg, self.per_pass + self.start - self.at)
        self.at = self.start
        self.waited = False


def build(nc, x, wqkv, wo, wg, w1, b1, w2, b2, gamma, beta, out):
    with ExitStack() as ctx:
        def sb(name, shape, dt=F32):
            return ctx.enter_context(nc.sbuf_tensor(name, shape, dt))

        def dram(name, shape, dt=F32):
            return nc.dram_tensor(name, shape, dt, kind="Internal").ap()

        def sem(name):
            return ctx.enter_context(nc.semaphore(name))

        xn_d = dram("xn_d", (T, D))
        qk_d = dram("qk_d", (3, 2 * D, T), BF16)
        slot_d = dram("slot_d", (E * CAP, 1), I32)
        y_d = dram("y_d", (E * CAP + 1, D))
        ao_d = dram("ao_d", (T, D))

        v_all = sb("v_all", [P, NT, D])
        q_op0, k_op0 = sb("q_op0", [P, 2, T], BF16), sb("k_op0", [P, 2, T], BF16)
        zone = sb("zone", [P, 16384])
        v_op = sb("v_op", [P, NT, 2, VW])
        w1_sb = [sb(f"w1_sb{i}", [P, DC, HID]) for i in range(2)]
        w2_sb = [sb(f"w2_sb{i}", [P, HC, D]) for i in range(2)]
        b1_sb = [sb(f"b1_sb{i}", [P, HC]) for i in range(2)]
        b1h_sb = [sb(f"b1h_sb{i}", [P, HC]) for i in range(2)]
        b2_sb = [sb(f"b2_sb{i}", [P, D]) for i in range(2)]
        slab_x = sb("slab_x", [P, SLAB_T, D])
        slab_xt = sb("slab_xt", [P, DC, SLAB_T * P])
        sig = sb("sig", [P, 2, CH])
        y_sb = sb("y_sb", [P, 2, SLAB_T, D])
        o_sb = sb("o_sb", [P, 2, CH])
        ao_sb = sb("ao_sb", [P, 2, TPC, 2 * DH])
        rden = sb("rden", [P, 2, TPC, 2])
        part = sb("part", [P, 2, NT, NC])
        neg = sb("neg", [P, 2, 8])
        negb = sb("negb", [P, 2, 2, 8], BF16)
        rows = sb("rows", [16, 2, P], BF16)
        wo_sb = sb("wo_sb", [P, DC, D])
        gam, bet = sb("gam", [P, D]), sb("bet", [P, D])
        ident, identb = sb("ident", [P, P]), sb("identb", [P, P], BF16)
        mask_m, mask_s = sb("mask_m", [P, P], BF16), sb("mask_s", [P, P], BF16)
        tri, onesb = sb("tri", [P, P], BF16), sb("onesb", [P, P], BF16)
        pick = sb("pick", [P, 2 * OW])
        zeros = sb("zeros", [P, P])
        down = sb("down", [P, E])
        logits = sb("logits", [P, NT, E])
        gate = sb("gate", [P, TOPK, NT])
        pos = sb("pos", [P, TOPK, NT], I32)
        token = sb("token", [P, NT], I32)
        slot_tok = sb("slot_tok", [P, E + 1, CAP // P], I32)
        slot_cur = sb("slot_cur", [P, CAP // P], I32)
        stats = sb("stats", [P, 2, TPC, 6])
        mean_var = sb("mean_var", [P, 2, TPC, 2])
        rstd = sb("rstd", [P, 2, TPC])
        half = sb("half", [P, TPC])
        bpos, bgate = sb("bpos", [P, 2, TOPK, BT], I32), sb("bgate", [P, 2, TOPK, BT])
        ones_row = sb("ones_row", [1, P])

        def view(a, n, dt=F32):
            v = zone[:, a:a + n]
            return v if dt == F32 else v.bitcast(dt)

        q_op = [q_op0[:, :, :], view(0, 4096, BF16).rearrange("p (h t) -> p h t", h=2)]
        k_op = [k_op0[:, :, :], view(4096, 4096, BF16).rearrange("p (h t) -> p h t", h=2)]
        prob = view(8192, P_SLOTS * CH).rearrange("p (s t) -> p s t", s=P_SLOTS)
        hid = [view(12288 + i * 2048, 2048).rearrange("p (c t) -> p c t", c=HC) for i in range(2)]
        x_in = [view(i * 1024, 1024).rearrange("p (j d) -> p j d", j=TPC) for i in range(2)]
        xn = [view(2048 + i * 1024, 1024).rearrange("p (j d) -> p j d", j=TPC) for i in range(2)]
        xt = [view(4096 + i * 1024, 1024).rearrange("p (c t) -> p c t", c=DC) for i in range(2)]
        resid = view(6144, 2048).rearrange("p (w t) -> p w t", w=4)
        split = [view(8192 + i * 3072, 3072, BF16).rearrange("p (s w t) -> p s w t", s=3, w=4)
                 for i in range(2)]
        wq_sb = view(14336, DC * (3 * D + E)).rearrange("p (c f) -> p c f", c=DC)
        r_score = view(0, 256).rearrange("p (i e) -> p i e", e=E)
        r_exp = view(256, 256).rearrange("p (i e) -> p i e", e=E)
        r_tmp = view(512, 256).rearrange("p (i e) -> p i e", e=E)
        r_hot = view(768, 512).rearrange("p (k i e) -> p k i e", k=TOPK, e=E)
        r_hotb = view(1280, 256, BF16).rearrange("p (k i e) -> p k i e", k=TOPK, e=E)
        r_in = view(1536, 512).rearrange("p (k i e) -> p k i e", k=TOPK, e=E)
        r_tot = [view(2048 + i * 512, 512).rearrange("p (k i e) -> p k i e", k=TOPK, e=E) for i in range(2)]
        r_own = view(3072, 512).rearrange("p (k i e) -> p k i e", k=TOPK, e=E)
        r_small = [view(3584 + i * 64, 64).rearrange("p (k i) -> p k i", k=TOPK) for i in range(6)]
        r_one = [view(3968 + i * 32, 32) for i in range(4)]
        bx, bxn, bao, bres, baot, bout = (
            [view((8 * i + n) * BT * D, BT * D).rearrange("p (j d) -> p j d", j=BT) for i in range(2)] for n in range(6))
        g_row = [view((8 * i + 6) * BT * D, TOPK * BT * D).rearrange("p (k j d) -> p k j d", k=TOPK, j=BT) for i in range(2)]

        bank = [ctx.enter_context(nc.psum_tensor(f"bank{i}", [P, CH], F32)) for i in range(8)]
        m_bank, s_bank = bank[0:M_RING], bank[M_RING:M_RING + S_RING]
        f_bank = bank[M_RING + S_RING:6]
        v_bank, row_bank = bank[6], bank[7]
        assert len(f_bank) == F_RING
        row_b16 = row_bank[:, :].bitcast(BF16)

        idle = sem("idle")
        consts, consts2 = sem("consts"), sem("consts2")
        const_dma, x_dma = sem("const_dma"), [sem(f"x_dma{i}") for i in range(2)]
        stat_done, rstd_done, xn_done = sem("stat_done"), sem("rstd_done"), sem("xn_done")
        xn_store = [sem(f"xn_store{i}") for i in range(2)]
        turned, xt_ready, qk_done, part1, resid_done, split_done = (
            sem(n) for n in ("turned", "xt_ready", "qk_done", "part1", "resid_done", "split_done"))
        part2 = sem("part2")
        split_store = [sem(f"split_store{i}") for i in range(2)]
        v_done, v_free = sem("v_done"), sem("v_free")
        rt_dve, rt_act, rt_pe, pos_ready = sem("rt_dve"), sem("rt_act"), sem("rt_pe"), sem("pos_ready")
        zero_dma, scatter, slot_load = sem("zero_dma"), sem("scatter"), sem("slot_load")
        rounds_ready = sem("rounds_ready")
        qk_load, w_load = [sem(f"qk_load{i}") for i in range(2)], [sem(f"w_load{i}") for i in range(2)]
        v_ready, b1h_ready, round_done = sem("v_ready"), sem("b1h_ready"), sem("round_done")
        m_ready, m_free, s_ready, s_done = sem("m_ready"), sem("m_free"), sem("s_ready"), sem("s_done")
        neg_done, negb_done = sem("neg_done"), sem("negb_done")
        row_done, row_free = sem("row_done"), sem("row_free")
        row_dma = [sem(f"row_dma{i}") for i in range(2)]
        pv_done, o_ready, o_used, rden_done = sem("pv_done"), sem("o_ready"), sem("o_used"), sem("rden_done")
        ao_store = [sem(f"ao_store{i}") for i in range(2)]
        idx_ready, slab_dma = sem("idx_ready"), sem("slab_dma")
        f_ready, f_free, tanh_done, sig_done = sem("f_ready"), sem("f_free"), sem("tanh_done"), sem("sig_done")
        y_store = [sem(f"y_store{i}") for i in range(2)]
        b_load, b_gather = [sem(f"b_load{i}") for i in range(2)], [sem(f"b_gather{i}") for i in range(2)]
        b_idx, b_dve, b_rstd, b_turn, b_aot, b_proj, b_out = (
            sem(n) for n in ("b_idx", "b_dve", "b_rstd", "b_turn", "b_aot", "b_proj", "b_out"))
        b_store = [sem(f"b_store{i}") for i in range(2)]

        x_t = x.rearrange("(i p) d -> p i d", p=P)
        xn_t = xn_d.rearrange("(i p) d -> p i d", p=P)
        ao_t = ao_d.rearrange("(i p) d -> p i d", p=P)
        out_t = out.rearrange("(i p) d -> p i d", p=P)
        slot_2d = slot_d.rearrange("(p j) o -> p (j o)", p=P)
        slot_t = slot_d.rearrange("(e p j) o -> p e (j o)", e=E, p=P)
        y_t = y_d[0:E * CAP, :].rearrange("(e p j) d -> e p j d", e=E, p=P)

        N_CONST = 7
        B_DVE = 5

        def chunks(engine, begin, rest):
            begin(0, 0)
            with engine.Fori(0, NC // 2 - 1) as n:
                rest(n, 0, lambda: begin(n, 1))
                rest(n, 1, lambda: begin(n + 1, 0))
            rest(NC // 2 - 1, 0, lambda: begin(NC // 2 - 1, 1))
            rest(NC // 2 - 1, 1, lambda: None)

        block = ctx.enter_context(nc.Block())

        @block.sync
        def _(sp):
            sp.dma_start(wq_sb[:, :, 0:3 * D], wqkv.rearrange("(c p) f -> p c f", p=P)).then_inc(const_dma, 16)
            sp.dma_start(wq_sb[:, :, 3 * D:], wg.rearrange("(c p) f -> p c f", p=P)).then_inc(const_dma, 16)
            sp.dma_start(wo_sb[:, :, :], wo.rearrange("(c p) f -> p c f", p=P)).then_inc(const_dma, 16)
            sp.dma_start(gam[:, :], gamma.rearrange("(a d) -> a d", a=1).broadcast_to([P, D])).then_inc(const_dma, 16)
            sp.dma_start(bet[:, :], beta.rearrange("(a d) -> a d", a=1).broadcast_to([P, D])).then_inc(const_dma, 16)
            sp.wait_ge(consts, 1)
            sp.dma_start(slot_2d, zeros[:, 0:E * CAP // P].bitcast(I32)).then_inc(zero_dma, 16)
            sp.dma_start(y_d[E * CAP:, :].rearrange("a (b d) -> (a b) d", b=2), zeros[0:2, :]).then_inc(zero_dma, 16)

            def load_x(c, par, before=None):
                if before is not None:
                    sp.wait_ge(xn_done, before)
                sp.dma_start(x_in[par], x_t[:, bass.ds(c * TPC, TPC), :]).then_inc(x_dma[par], 16)

            def store_front(c, par):
                sp.wait_ge(xn_done, c + 1)
                sp.dma_start(xn_t[:, bass.ds(c * TPC, TPC), :], xn[par]).then_inc(xn_store[par], 16)
                sp.wait_ge(split_done, 4 * c + 8)
                for s in range(3):
                    sp.dma_start(qk_d[s].rearrange("(w p) t -> p w t", p=P)[:, :, bass.ds(c * CH, CH)],
                                 split[par][:, s]).then_inc(split_store[par], 16)

            load_x(0, 0)
            load_x(1, 1)
            with sp.Fori(0, NC // 2 - 1) as n:
                for par in range(2):
                    load_x(2 * n + 2 + par, par, before=2 * n + par + 1)
                    store_front(2 * n + par, par)
            for par in range(2):
                store_front(NC - 2 + par, par)

            def load_round(r, par):
                for g in range(6):
                    for op, parts, first in ((q_op, Q_PARTS, 0), (k_op, K_PARTS, D)):
                        src = qk_d[parts[g], bass.ds(r * 2 * DH + first, 2 * DH), :]
                        sp.dma_start(op[par][g * DH:(g + 1) * DH],
                                     src.rearrange("(h r) t -> r h t", h=2)).then_inc(qk_load[par], 16)
                sp.dma_start(w1_sb[par][:, :, :],
                             w1[bass.ds(r, 1)].rearrange("o (c p) f -> p (o c) f", p=P)).then_inc(w_load[par], 16)
                sp.dma_start(w2_sb[par][:, :, :],
                             w2[bass.ds(r, 1)].rearrange("o (c p) f -> p (o c) f", p=P)).then_inc(w_load[par], 16)
                sp.dma_start(b1_sb[par][:, :], b1[:, bass.ds(r, 1), :].rearrange("p o c -> p (o c)")).then_inc(w_load[par], 16)
                sp.dma_start(b2_sb[par][:, :], b2[bass.ds(r, 1), :].broadcast_to([P, D])).then_inc(w_load[par], 16)

            def sp_round(n, par, load):
                r = 2 * n + par
                if load:
                    sp.wait_ge(round_done, r + 1)
                    sp.wait_ge(f_free, F_RING + r * N_F)
                    load_round(r + 1, 1 - par)
                for x in STEPS:
                    if x[0] == "R":
                        c = x[1]
                        rows_out.reach(1 + par * N_ROW + ROW_AT[x] + 1)
                        for s in range(2):
                            for h in range(2):
                                a = 8 * s + TPC * h
                                sp.dma_start(q_op[par][ROWS + s:ROWS + s + 1, h, c * CH:(c + 1) * CH]
                                             .rearrange("o (t q) -> o t q", t=TPC),
                                             rows[a:a + TPC, c % 2, :]).then_inc(row_dma[c % 2], 16)
                    elif x[0] == "O":
                        c = x[1]
                        rows_out.reach(1 + par * N_ROW + ROW_AT[x] + 1)
                        sp.sem_inc(idle, 1)
                        sp.dma_start(ao_t[:, c * TPC:(c + 1) * TPC, bass.ds(r * 2 * DH, 2 * DH)],
                                     ao_sb[:, c % 2]).then_inc(ao_store[c % 2], 16)
                    elif x[0] == "Y" and x[2] == 15:
                        f = x[1]
                        buf = (par * SLABS + f) % 2
                        slabs_out.reach(F_RING + par * N_F + ITEM_AT[("Y", f)] + 1)
                        sp.dma_start(y_t[bass.ds(r, 1), :, f * SLAB_T:(f + 1) * SLAB_T, :].rearrange("o p j d -> (o p) j d"),
                                     y_sb[:, buf]).then_inc(y_store[buf], 16)

            for i in range(2):
                sp.wait_ge(split_store[i], 48 * (NC // 2 + 1))
            load_round(0, 0)
            for i in range(2):
                sp.wait_ge(xn_store[i], 16 * (NC // 2 + 1))
            sp.wait_ge(rounds_ready, 1)
            rows_out = Waits(sp, row_free, 2 * N_ROW, 1)
            slabs_out = Waits(sp, f_free, 2 * N_F, F_RING)
            with sp.Fori(0, ROUNDS // 2 - 1) as n:
                for par in range(2):
                    sp_round(n, par, True)
                for w in (rows_out, slabs_out):
                    w.end_pass()
            sp_round(ROUNDS // 2 - 1, 0, True)
            sp_round(ROUNDS // 2 - 1, 1, False)

            sp.wait_ge(round_done, ROUNDS + 1)
            for i in range(2):
                sp.wait_ge(ao_store[i], 16 * (ROUNDS * NC // 2 + 1))

            def load_back(i, par):
                for dst, src in ((bxn, xn_t), (bao, ao_t), (bx, x_t)):
                    sp.dma_start(dst[par], src[:, bass.ds(i * BT, BT), :]).then_inc(b_load[par], 16)

            def store_back(i, par):
                sp.wait_ge(b_out, i + 2)
                sp.dma_start(out_t[:, bass.ds(i * BT, BT), :], bout[par]).then_inc(b_store[par], 16)

            load_back(0, 0)
            load_back(1, 1)
            with sp.Fori(0, NB // 2 - 1) as n:
                for par in range(2):
                    store_back(2 * n + par, par)
                    load_back(2 * n + 2 + par, par)
            for par in range(2):
                store_back(NB - 2 + par, par)
            for i in range(2):
                sp.wait_ge(b_store[i], 16 * (NB // 2 + 1))

        @block.gpsimd
        def _(pool):
            g = nc.gpsimd
            def wait(sem, value):
                pool.wait_ge(sem, value)
                if not isinstance(value, int):
                    pool.sem_inc(idle, 1)

            g.memset(zeros[:, :], 0.0).then_inc(consts, 1)
            g.memset(ident[:, :], 0.0).then_inc(consts, 1)
            g.memset(identb[:, :], 0.0).then_inc(consts, 1)
            g.memset(mask_m[:, :], 0.0).then_inc(consts, 1)
            g.memset(mask_s[:, :], 0.0).then_inc(consts, 1)
            g.memset(onesb[:, :], 1.0).then_inc(consts, 1)
            g.memset(tri[:, :], 1.0).then_inc(consts, 1)
            g.memset(pick[:, :], 0.0).then_inc(consts, 1)
            g.memset(v_op[:, :, :, :], 0.0).then_inc(consts, 1)
            g.memset(slot_tok[:, :, :], 0).then_inc(consts, 1)
            g.memset(half[:, :], -0.5).then_inc(consts, 1)
            g.memset(ones_row[:, :], 1.0).then_inc(consts, 1)
            wait(consts, 12)
            for m in (ident, identb):
                g.affine_select(out=m[:, :], in_=m[:, :], compare_op=ALU.not_equal, fill=1.0, base=0,
                                pattern=[[-1, P]], channel_multiplier=1).then_inc(consts2, 1)
            g.affine_select(out=mask_m[:, :], in_=mask_m[:, :], compare_op=ALU.is_ge, fill=MASKED, base=0,
                            pattern=[[-1, P]], channel_multiplier=1).then_inc(consts2, 1)
            g.affine_select(out=mask_s[:, :], in_=mask_s[:, :], compare_op=ALU.is_ge, fill=MASKED, base=0,
                            pattern=[[1, P]], channel_multiplier=-1).then_inc(consts2, 1)
            g.affine_select(out=tri[:, :], in_=tri[:, :], compare_op=ALU.is_ge, fill=0.0, base=0,
                            pattern=[[1, P]], channel_multiplier=-1).then_inc(consts2, 1)
            for h in range(2):
                for s in range(2):
                    wait(consts2, 5 + 2 * h + s)
                    g.affine_select(out=pick[:, h * OW:(h + 1) * OW], in_=pick[:, h * OW:(h + 1) * OW],
                                    compare_op=ALU.not_equal, fill=1.0, base=-VW * (2 * h + s),
                                    pattern=[[-1, OW]], channel_multiplier=1).then_inc(consts2, 1)
            g.memset(v_op[:, :, :, DH:DH + 1], 1.0).then_inc(consts2, 1)
            g.iota(token[:, :], pattern=[[P, NT]], base=0, channel_multiplier=1).then_inc(consts2, 1)
            for i in range(E):
                g.memset(down[:, i:i + 1], float(E - i)).then_inc(consts2, 1)
            wait(consts2, 9 + 1 + 1 + E)
            g.memset(k_op0[ROWS:ROWS + 2, :, :], 1.0).then_inc(consts2, 1)
            wait(consts2, 9 + 1 + 1 + E + 1)

            pool.sem_inc(split_done, 4)
            def begin_chunk(n, par):
                c = 2 * n + par
                wait(stat_done, 2 * c + 2)
                g.tensor_scalar(rstd[:, par, :], mean_var[:, par, :, 1], LN_EPS, None, ALU.add).then_inc(rstd_done, 1)
                wait(rstd_done, 2 * c + 1)
                g.tensor_tensor(rstd[:, par, :], rstd[:, par, :], half[:, :], ALU.pow).then_inc(rstd_done, 1)

            def split_chunk(n, par, begin_next):
                c = 2 * n + par
                begin_next()
                for w in range(4):
                    wait(part2, 4 * c + w + 1)
                    g.tensor_tensor(split[par][:, 2, w], resid[:, w], split[par][:, 1, w],
                                    ALU.subtract).then_inc(split_done, 1)

            chunks(pool, begin_chunk, split_chunk)

            wait(pos_ready, 1)
            wait(zero_dma, 32)
            for k in range(TOPK):
                for i in range(NT):
                    g.indirect_dma_start(out=slot_d, out_offset=bass.IndirectOffsetOnAxis(ap=pos[:, k, i:i + 1], axis=0),
                                         in_=token[:, i:i + 1], in_offset=None,
                                         bounds_check=E * CAP - 1, oob_is_err=False).then_inc(scatter, 16)
            wait(scatter, 16 * TOPK * NT)
            pool.dma_start(slot_tok[:, 0:E, :], slot_t).then_inc(slot_load, 16)
            wait(slot_load, 16)
            for i in range(2):
                wait(xn_store[i], 16 * (NC // 2 + 1))
                wait(split_store[i], 48 * (NC // 2 + 1))
            g.memset(k_op[1][ROWS:ROWS + 2, :, :], 1.0).then_inc(rounds_ready, 1)
            wait(rounds_ready, 1)

            def gather(e, f, first):
                if first:
                    g.tensor_copy(slot_cur[:, :], slot_tok[:, bass.ds(e, 1), :].rearrange("p o j -> p (o j)")).then_inc(idx_ready, 1)
                    wait(idx_ready, e + 1)
                for j in range(SLAB_T):
                    g.indirect_dma_start(out=slab_x[:, j, :], out_offset=None, in_=xn_d,
                                         in_offset=bass.IndirectOffsetOnAxis(
                                             ap=slot_cur[:, f * SLAB_T + j:f * SLAB_T + j + 1], axis=0)
                                         ).then_inc(slab_dma, 16)

            def pool_round(n, par):
                r = 2 * n + par
                wait(round_done, r + 1)
                g.tensor_copy(v_op[:, :, :, 0:DH], v_all[:, :, bass.ds(r * 2 * DH, 2 * DH)]
                              .rearrange("p i (h d) -> p i h d", h=2)).then_inc(v_ready, 1)
                wait(w_load[par], 64 * (n + 1))
                g.tensor_scalar(b1h_sb[par][:, :], b1_sb[par][:, :], 0.5, None, ALU.mult).then_inc(b1h_ready, 1)
                for x in STEPS:
                    if x[0] == "X":
                        f = x[1]
                        turned_slabs.reach(par * N_F + ITEM_AT[x] + 1)
                        if f + 1 < SLABS:
                            gather(r, f + 1, False)
                        else:
                            slabs_in.reach(32 * (par * SLABS + SLABS))
                            gather(r + 1, 0, True)
                    elif x[0] == "H" and x[3] == 3:
                        k = ITEM_AT[x[:3]]
                        tanhs.reach(par * N_H + HIDDEN_AT[x[:3]] + 1)
                        g.tensor_scalar(sig[:, k % 2], sig[:, k % 2], 0.5, 0.5, ALU.mult, ALU.add).then_inc(sig_done, 1)

            gather(0, 0, True)
            turned_slabs = Waits(pool, f_ready, 2 * N_F, wait=wait)
            slabs_in = Waits(pool, slab_dma, 2 * 32 * SLABS, wait=wait)
            tanhs = Waits(pool, tanh_done, 2 * N_H, wait=wait)
            with pool.Fori(0, ROUNDS // 2) as n:
                for par in range(2):
                    pool_round(n, par)
                for w in (turned_slabs, slabs_in, tanhs):
                    w.end_pass()

            wait(slab_dma, 32 * (ROUNDS * SLABS + 1))
            for i in range(2):
                wait(y_store[i], 16 * (ROUNDS * SLABS // 2 + 1))
            wait(round_done, ROUNDS + 1)

            def pool_gather(i, par):
                g.tensor_copy(bpos[:, par], pos[:, :, bass.ds(i * BT, BT)]).then_inc(b_idx, 1)
                g.tensor_copy(bgate[:, par], gate[:, :, bass.ds(i * BT, BT)]).then_inc(b_idx, 1)
                wait(b_idx, 2 * i + 2)
                for j in range(BT):
                    for k in range(TOPK):
                        g.indirect_dma_start(out=g_row[par][:, k, j], out_offset=None, in_=y_d,
                                             in_offset=bass.IndirectOffsetOnAxis(ap=bpos[:, par, k, j:j + 1], axis=0)
                                             ).then_inc(b_gather[par], 16)

            def pool_rstd(i, par):
                wait(b_dve, B_DVE * i + 4)
                g.tensor_scalar(rstd[:, par, :], mean_var[:, par, :, 1], LN_EPS, None, ALU.add).then_inc(b_rstd, 1)
                wait(b_rstd, 2 * i + 1)
                g.tensor_tensor(rstd[:, par, :], rstd[:, par, :], half[:, :], ALU.pow).then_inc(b_rstd, 1)

            pool_gather(0, 0)
            pool_gather(1, 1)
            with pool.Fori(0, NB // 2 - 1) as n:
                for par in range(2):
                    pool_rstd(2 * n + par, par)
                    pool_gather(2 * n + par + 2, par)
            for par in range(2):
                pool_rstd(NB - 2 + par, par)

        @block.scalar
        def _(act):
            s = nc.scalar
            act.sem_inc(v_free, 2)
            act.sem_inc(xt_ready, 1)
            act.sem_inc(b_aot, 1)
            for i in range(2):
                act.sem_inc(split_store[i], 48)

            def begin_chunk(n, par):
                c = 2 * n + par
                act.wait_ge(turned, c + 1)
                for d in range(DC):
                    last = s.activation(xt[par][:, d], bank[d][:, :], ACT.Copy)
                last.then_inc(xt_ready, 1)

            def act_chunk(n, par, begin_next):
                c = 2 * n + par
                act.wait_ge(split_store[par], 48 * n + 48)
                for w in range(4):
                    act.wait_ge(qk_done, 4 * c + w + 1)
                    s.activation(split[par][:, 0, w], bank[2 + w][:, :], ACT.Copy,
                                 scale=DH ** -0.5 if w < 2 else 1.0).then_inc(part1, 1)
                begin_next()
                for j in range(TPC):
                    act.wait_ge(resid_done, 4 * c + j + 5)
                    s.activation(split[par][:, 1, j], resid[:, j], ACT.Copy).then_inc(part2, 1)
                    act.wait_ge(v_done, 4 * c + j + 1)
                    s.activation(v_all[:, bass.ds(c * TPC + j, 1), :].rearrange("p o d -> p (o d)"),
                                 bank[6 + j % 2][:, 0:D], ACT.Copy)
                    s.activation(logits[:, bass.ds(c * TPC + j, 1), :].rearrange("p o e -> p (o e)"),
                                 bank[6 + j % 2][:, D:D + E], ACT.Copy).then_inc(v_free, 1)

            chunks(act, begin_chunk, act_chunk)

            act.wait_ge(rt_dve, 2)
            s.activation(r_exp, r_tmp, ACT.Exp).then_inc(rt_act, 1)

            act.wait_ge(rounds_ready, 1)

            def act_round(n, par):
                r = 2 * n + par
                act.wait_ge(b1h_ready, r + 1)
                for x in STEPS:
                    if x[0] == "S":
                        _, c, h, b = x
                        k = S_AT[x]
                        off = max(0, b - TPC * c) * P
                        scores.reach(par * N_S + k + 1)
                        if k % GROUP == 0:
                            slots.reach(par * N_V + k // GROUP + 1)
                        s.activation(prob[:, k % P_SLOTS, off:], s_bank[k % S_RING][:, 0:CH - off],
                                     ACT.Exp).then_inc(s_done, 1)
                    elif x[0] == "V" and x[3]:
                        c = x[1]
                        sums.reach(P_SLOTS // GROUP + par * N_V + V_AT[x] + 1)
                        o_bufs.reach(par * NC + c + 1)
                        s.activation(o_sb[:, c % 2], v_bank[:, :], ACT.Copy).then_inc(o_ready, 1)
                    elif x[0] == "H" and x[3] == 3:
                        _, f, u, _ = x
                        k = ITEM_AT[x[:3]]
                        hidden.reach(par * N_F + k + 1)
                        for v in range(2):
                            last = s.activation(sig[:, k % 2, v * D:(v + 1) * D], f_bank[k % F_RING][:, v * D:(v + 1) * D],
                                                ACT.Tanh, bias=b1h_sb[par][:, 2 * u + v:2 * u + v + 1], scale=0.5)
                        last.then_inc(tanh_done, 1)

            act.sem_inc(s_done, S_RING)
            act.sem_inc(o_ready, 1)
            scores = Waits(act, s_ready, 2 * N_S)
            slots = Waits(act, pv_done, 2 * N_V)
            sums = Waits(act, pv_done, 2 * N_V, P_SLOTS // GROUP)
            o_bufs = Waits(act, o_used, 2 * NC)
            hidden = Waits(act, f_ready, 2 * N_F)
            with act.Fori(0, ROUNDS // 2) as n:
                for par in range(2):
                    act_round(n, par)
                for w in (scores, slots, sums, o_bufs, hidden):
                    w.end_pass()

            def act_back(i, par):
                act.wait_ge(b_turn, i + 1)
                act.wait_ge(b_proj, i + 1)
                for h in range(2):
                    last = s.activation(baot[par][:, h * BT // 2:(h + 1) * BT // 2].rearrange("p j d -> p (j d)"),
                                        bank[h][:, :], ACT.Copy)
                last.then_inc(b_aot, 1)

            with act.Fori(0, NB // 2) as n:
                for par in range(2):
                    act_back(2 * n + par, par)

        @block.tensor
        def _(pe):
            t = nc.tensor

            def turn(out_ap, in_ap, unit):
                return t.matmul(out_ap, in_ap, unit, start=True, stop=True, is_transpose=True)

            pe.wait_ge(consts2, 9 + 1 + 1 + E + 1)
            pe.wait_ge(const_dma, 16 * 5)

            def begin_chunk(n, par):
                c = 2 * n + par
                pe.wait_ge(xn_done, c + 1)
                pe.wait_ge(xt_ready, c + 1)
                for j in range(TPC):
                    for d in range(DC):
                        last = turn(bank[d][:, j * P:(j + 1) * P], xn[par][:, j, d * P:(d + 1) * P], ident[:, :])
                last.then_inc(turned, 1)

            def pe_chunk(n, par, begin_next):
                c = 2 * n + par
                pe.wait_ge(xt_ready, c + 2)
                pe.wait_ge(resid_done, 4 * c + 4)
                for w in range(4):
                    for d in range(DC):
                        last = t.matmul(bank[2 + w][:, :], wq_sb[:, d, w * P:(w + 1) * P], xt[par][:, d],
                                        start=d == 0, stop=d == DC - 1)
                    last.then_inc(qk_done, 1)
                begin_next()
                for j in range(TPC):
                    pe.wait_ge(v_free, 4 * c + j + 1)
                    for d in range(DC):
                        last = t.matmul(bank[6 + j % 2][:, 0:D + E], xt[par][:, d, j * P:(j + 1) * P],
                                        wq_sb[:, d, 2 * D:], start=d == 0, stop=d == DC - 1)
                    last.then_inc(v_done, 1)

            chunks(pe, begin_chunk, pe_chunk)

            pe.wait_ge(rt_dve, 17)
            t.matmul(bank[0][:, :], tri[:, :], r_hotb.rearrange("p k i e -> p (k i e)"), start=True, stop=True)
            t.matmul(bank[1][:, :], onesb[:, :], r_hotb.rearrange("p k i e -> p (k i e)"),
                     start=True, stop=True).then_inc(rt_pe, 1)
            pe.wait_ge(pos_ready, 1)

            def pe_round(n, par):
                r = 2 * n + par
                pe.wait_ge(qk_load[par], 192 * (n + 1))
                pe.wait_ge(w_load[par], 64 * (n + 1))
                pe.wait_ge(v_ready, r + 1)
                q, k_ = q_op[par], k_op[par]
                for x in STEPS:
                    kind = x[0]
                    if kind == "M":
                        _, h, i, j = x
                        k = M_AT[x]
                        diag = j == i // TPC
                        w = (i % TPC + 1) * P if diag else CH
                        m_banks.reach(par * N_M + k + 1)
                        o = m_bank[k % M_RING]
                        last = t.matmul(o[:, 0:w], q[0:ROWS, h, i * P:(i + 1) * P], k_[0:ROWS, h, j * CH:j * CH + w],
                                        start=True, stop=True)
                        if diag:
                            last = t.matmul(o[:, w - P:w], identb[:, :], mask_m[:, :], start=False, stop=True,
                                            skip_group_check=True)
                        last.then_inc(m_ready, 1)
                    elif kind == "R":
                        c = x[1]
                        maxima.reach(par * NC + c + 1)
                        row_uses.reach(par * N_ROW + ROW_AT[x] + 1)
                        turn(row_b16[0:16, 0:P], negb[:, c % 2].rearrange("p s n -> p (s n)"),
                                    identb[:, :]).then_inc(row_done, 1)
                    elif kind == "S":
                        _, c, h, b = x
                        k = S_AT[x]
                        off = max(0, b - TPC * c) * P
                        diag = b >= TPC * c
                        if b == 0 and h == 0:
                            row_loads[c % 2].reach(64 * (par * (NC // 2) + c // 2 + 2))
                        s_banks.reach(par * N_S + k + 1)
                        o = s_bank[k % S_RING]
                        last = t.matmul(o[:, 0:CH - off], k_[0:AUG, h, b * P:(b + 1) * P],
                                        q[0:AUG, h, c * CH + off:(c + 1) * CH], start=True, stop=True)
                        if diag:
                            last = t.matmul(o[:, 0:P], identb[:, :], mask_s[:, :], start=False, stop=True,
                                            skip_group_check=True)
                        last.then_inc(s_ready, 1)
                    elif kind == "V":
                        _, c, grp, final = x
                        k = V_AT[x]
                        if grp == 0:
                            o_taken.reach(par * NC + c + 1)
                        probs.reach(S_RING + par * N_S + GROUP * (k + 1))
                        if grp == 0 and c == 0:
                            for h in range(2):
                                t.matmul(v_bank[VW * (2 * h + 1):VW * (2 * h + 2), 0:P], v_op[:, 1, h, :], zeros[:, :],
                                         start=True, stop=False, skip_group_check=True)
                        for b2_ in range(2):
                            for h in range(2):
                                b = 2 * grp + b2_
                                slot = (k * GROUP + 2 * b2_ + h) % P_SLOTS
                                off = max(0, b - TPC * c) * P
                                quad = 2 * h + b2_
                                last = t.matmul(v_bank[VW * quad:VW * (quad + 1), off:], v_op[:, b, h, :],
                                                prob[:, slot, off:], start=grp == 0 and not (c == 0 and b2_ == 1),
                                                stop=final, skip_group_check=True)
                        last.then_inc(pv_done, 1)
                    elif kind == "O":
                        c = x[1]
                        o_copies.reach(1 + par * NC + c + 1)
                        row_uses.reach(par * N_ROW + ROW_AT[x] + 1)
                        for j in range(TPC):
                            last = t.matmul(row_bank[:, j * 2 * OW:(j + 1) * 2 * OW], o_sb[:, c % 2, j * P:(j + 1) * P], pick[:, :],
                                     start=True, stop=True)
                        last.then_inc(o_used, 1)
                    elif kind == "X":
                        f = x[1]
                        k = ITEM_AT[x]
                        slabs.reach(32 * (par * SLABS + f + 1))
                        f_banks.reach(par * N_F + k + 1)
                        for j in range(SLAB_T):
                            for d in range(DC):
                                a = (d * SLAB_T + j) * P
                                last = turn(f_bank[k % F_RING][:, a:a + P], slab_x[:, j, d * P:(d + 1) * P], ident[:, :])
                        last.then_inc(f_ready, 1)
                    elif kind == "H":
                        _, f, u, q4 = x
                        k = ITEM_AT[x[:3]]
                        if q4 == 0:
                            f_banks.reach(par * N_F + k + 1)
                            if u == 0:
                                f_data.reach(F_RING + par * N_F + ITEM_AT[("X", f)] + 1)
                        v, d = q4 // 2, q4 % 2
                        last = t.matmul(f_bank[k % F_RING][:, v * D:(v + 1) * D],
                                        w1_sb[par][:, d, (2 * u + v) * P:(2 * u + v + 1) * P], slab_xt[:, d],
                                        start=d == 0, stop=d == 1, skip_group_check=True)
                        if q4 == 3:
                            last.then_inc(f_ready, 1)
                    elif kind == "Y":
                        _, f, s16 = x
                        k = ITEM_AT[x[:2]]
                        buf = (par * SLABS + f) % 2
                        j, c8 = s16 // HC, s16 % HC
                        if s16 == 0:
                            f_banks.reach(par * N_F + k + 1)
                            f_data.reach(F_RING + par * N_F + ITEM_AT[("H", f, HC // 2 - 1)] + 1)
                        last = t.matmul(f_bank[k % F_RING][:, j * D:(j + 1) * D], hid[buf][:, c8, j * P:(j + 1) * P],
                                        w2_sb[par][:, c8, :], start=c8 == 0, stop=c8 == HC - 1, skip_group_check=True)
                        if s16 == 15:
                            last.then_inc(f_ready, 1)
                pe.wait_ge(o_used, 2 + r * NC + NC)
                pe.wait_ge(f_ready, r * N_F + N_F)
                pe.sem_inc(round_done, 1)

            pe.sem_inc(pv_done, P_SLOTS // GROUP)
            pe.sem_inc(o_used, 2)
            pe.sem_inc(round_done, 1)
            pe.wait_ge(rounds_ready, 1)
            m_banks = Waits(pe, m_free, 2 * N_M)
            s_banks = Waits(pe, s_done, 2 * N_S)
            probs = Waits(pe, s_done, 2 * N_S, S_RING)
            maxima = Waits(pe, negb_done, 2 * NC)
            row_uses = Waits(pe, row_free, 2 * N_ROW)
            row_loads = [Waits(pe, row_dma[i], 64 * NC, 64) for i in range(2)]
            o_taken = Waits(pe, o_ready, 2 * NC)
            o_copies = Waits(pe, o_ready, 2 * NC, 1)
            slabs = Waits(pe, slab_dma, 2 * 32 * SLABS)
            f_banks = Waits(pe, f_free, 2 * N_F)
            f_data = Waits(pe, f_free, 2 * N_F, F_RING)
            with pe.Fori(0, ROUNDS // 2) as n:
                for par in range(2):
                    pe_round(n, par)
                for w in (m_banks, s_banks, probs, maxima, row_uses, *row_loads, o_taken, o_copies, slabs, f_banks, f_data):
                    w.end_pass()

            pe.sem_inc(b_proj, 2)
            pe.wait_ge(m_free, M_RING + ROUNDS * N_M)
            pe.wait_ge(s_done, S_RING + ROUNDS * N_S)
            def pe_back(i, n, par):
                pe.wait_ge(b_load[par], 48 * (n + 1))
                pe.wait_ge(b_aot, i + 1)
                for j in range(BT):
                    for d in range(DC):
                        a = (j * DC + d) % (CH // P) * P
                        last = turn(bank[j * D // CH][:, a:a + P], bao[par][:, j, d * P:(d + 1) * P], ident[:, :])
                last.then_inc(b_turn, 1)
                pe.wait_ge(b_out, i + 1)
                for h in range(2):
                    t.matmul(bank[2 + 2 * par + h][:, :], ident[:, :],
                             bx[par][:, h * BT // 2:(h + 1) * BT // 2].rearrange("p j d -> p (j d)"),
                             start=True, stop=False, skip_group_check=True)
                for j in range(BT):
                    o = bank[2 + 2 * par + j * D // CH][:, j * D % CH:j * D % CH + D]
                    t.matmul(o, ones_row[:, :], bet[0:1, :], start=False, stop=False, skip_group_check=True)
                pe.wait_ge(b_aot, i + 2)
                for j in range(BT):
                    o = bank[2 + 2 * par + j * D // CH][:, j * D % CH:j * D % CH + D]
                    for d in range(DC):
                        last = t.matmul(o, baot[par][:, j, d * P:(d + 1) * P], wo_sb[:, d], start=False, stop=d == 1,
                                        skip_group_check=True)
                last.then_inc(b_proj, 1)

            with pe.Fori(0, NB // 2) as n:
                for par in range(2):
                    pe_back(2 * n + par, n, par)

        @block.vector
        def _(dve):
            v = nc.vector
            for i in range(2):
                dve.sem_inc(row_dma[i], 64)
                dve.sem_inc(ao_store[i], 16)
                dve.sem_inc(y_store[i], 16)
                dve.sem_inc(xn_store[i], 16)
                dve.sem_inc(b_store[i], 16)
            dve.sem_inc(resid_done, 4)
            dve.sem_inc(b_out, 1)
            dve.sem_inc(m_free, M_RING)
            dve.sem_inc(row_free, 1)
            dve.sem_inc(f_free, F_RING)
            v.memset(part[:, :, :, :], 0.0).then_inc(neg_done, 1)

            def begin_chunk(n, par):
                c = 2 * n + par
                dve.wait_ge(x_dma[par], 16 * (n + 1))
                for j in range(TPC):
                    last = v.bn_stats(stats[:, par, j, :], x_in[par][:, j, :])
                last.then_inc(stat_done, 1)
                dve.wait_ge(stat_done, 2 * c + 1)
                dve.sem_inc(idle, 1)
                for j in range(TPC):
                    last = v.bn_aggr(mean_var[:, par, j, :], stats[:, par, j, :])
                last.then_inc(stat_done, 1)
                dve.wait_ge(rstd_done, 2 * c + 2)
                dve.wait_ge(xn_store[par], 16 * n + 16)
                for j in range(TPC):
                    last = v.tensor_scalar(xn[par][:, j, :], x_in[par][:, j, :], mean_var[:, par, j, 0:1],
                                           rstd[:, par, j:j + 1], ALU.subtract, ALU.mult)
                last.then_inc(xn_done, 1)

            def dve_chunk(n, par, begin_next):
                c = 2 * n + par
                begin_next()
                for w in range(4):
                    dve.wait_ge(part1, 4 * c + w + 1)
                    dve.wait_ge(split_done, 4 * c + 4)
                    v.scalar_tensor_tensor(resid[:, w], bank[2 + w][:, :], DH ** -0.5 if w < 2 else 1.0,
                                           split[par][:, 0, w], ALU.mult, ALU.subtract).then_inc(resid_done, 1)

            chunks(dve, begin_chunk, dve_chunk)

            for i in range(2):
                dve.wait_ge(xn_store[i], 16 * (NC // 2 + 1))
            dve.wait_ge(turned, NC)
            dve.wait_ge(v_free, 2 + NT)
            dve.wait_ge(consts2, 9 + 1 + 1 + E + 1)
            steps = [0]

            def chain(ins):
                steps[0] += 1
                ins.then_inc(rt_dve, 1)
                dve.wait_ge(rt_dve, steps[0])

            def over_e(a):
                return a.unsqueeze(2).broadcast_to([P, NT, E])

            down_b = down[:, :].unsqueeze(1).broadcast_to([P, NT, E])
            chain(v.tensor_reduce(r_one[0], logits[:, :, :], AX.X, ALU.max))
            chain(v.tensor_tensor(r_tmp, logits[:, :, :], over_e(r_one[0]), ALU.subtract))
            dve.wait_ge(rt_act, 1)
            chain(v.tensor_reduce(r_one[1], r_exp, AX.X, ALU.add))
            chain(v.reciprocal(r_one[2], r_one[1]))
            chain(v.tensor_tensor(r_score, r_exp, over_e(r_one[2]), ALU.mult))
            best, index = r_small[0], r_small[1]
            for k in range(TOPK):
                src = r_score
                chain(v.tensor_reduce(best[:, k], src, AX.X, ALU.max))
                chain(v.tensor_tensor(r_tmp, src, over_e(best[:, k]), ALU.is_equal))
                chain(v.tensor_tensor(r_tmp, r_tmp, down_b, ALU.mult))
                chain(v.tensor_reduce(index[:, k], r_tmp, AX.X, ALU.max))
                chain(v.tensor_tensor(r_hot[:, k], down_b, over_e(index[:, k]), ALU.is_equal))
                if k == 0:
                    chain(v.scalar_tensor_tensor(r_score.rearrange("p i e -> p (i e)"),
                                                 r_hot[:, 0].rearrange("p i e -> p (i e)"), -2.0,
                                                 r_score.rearrange("p i e -> p (i e)"), ALU.mult, ALU.add))
            assert steps[0] == 16
            chain(v.tensor_copy(r_hotb, r_hot))
            dve.wait_ge(rt_pe, 1)
            flat = "p k i e -> p (k i e)"
            chain(v.tensor_copy(r_in.rearrange(flat), bank[0][:, :]))
            chain(v.tensor_copy(r_tot[0].rearrange(flat), bank[1][:, :]))
            chain(v.tensor_tensor(r_own.rearrange(flat), r_in.rearrange(flat), r_tot[0].rearrange(flat), ALU.subtract))
            src = 0
            for step in (1, 2, 4, 8, 16):
                a, b = r_tot[src], r_tot[1 - src]
                for k in range(TOPK):
                    v.tensor_copy(b[:, k, 0:step], a[:, k, 0:step])
                    last = v.tensor_tensor(b[:, k, step:], a[:, k, step:], a[:, k, 0:NT - step], ALU.add)
                chain(last)
                src = 1 - src
            tot = r_tot[src]
            chain(v.tensor_tensor(r_in.rearrange(flat), r_own.rearrange(flat), tot.rearrange(flat), ALU.add))
            chain(v.tensor_tensor(r_in[:, 1], r_in[:, 1], tot[:, 0, NT - 1:NT, :].broadcast_to([P, NT, E]), ALU.add))
            chain(v.tensor_tensor(r_own.rearrange(flat), r_in.rearrange(flat), r_hot.rearrange(flat), ALU.mult))
            loc, keep, flatpos = r_small[2], r_small[3], r_small[4]
            for k in range(TOPK):
                last = v.tensor_reduce(loc[:, k], r_own[:, k], AX.X, ALU.add)
            chain(last)
            chain(v.tensor_scalar(keep, loc, float(CAP), None, ALU.is_le))
            chain(v.tensor_scalar(flatpos, index, -float(CAP), -1.0, ALU.mult, ALU.add))
            chain(v.tensor_tensor(flatpos, flatpos, loc, ALU.add))
            chain(v.tensor_tensor(flatpos, flatpos, keep, ALU.mult))
            chain(v.tensor_scalar(flatpos, flatpos, float(E * CAP), None, ALU.add))
            chain(v.tensor_copy(pos[:, :, :], flatpos))
            chain(v.tensor_tensor(r_one[0], best[:, 0], best[:, 1], ALU.add))
            chain(v.tensor_scalar(r_one[1], r_one[0], GATE_EPS, None, ALU.max))
            chain(v.reciprocal(r_one[2], r_one[1]))
            chain(v.tensor_tensor(r_small[5], best, r_one[2].unsqueeze(1).broadcast_to([P, TOPK, NT]), ALU.mult))
            v.tensor_tensor(gate[:, :, :], r_small[5], keep, ALU.mult).then_inc(pos_ready, 1)

            dve.wait_ge(rounds_ready, 1)

            def dve_round(n, par):
                r = 2 * n + par
                for x in STEPS:
                    kind = x[0]
                    if kind == "M":
                        _, h, i, j = x
                        k = M_AT[x]
                        w = (i % TPC + 1) * P if j == i // TPC else CH
                        scored.reach(par * N_M + k + 1)
                        v.tensor_reduce(part[:, h, i, j:j + 1], m_bank[k % M_RING][:, 0:w], AX.X, ALU.max).then_inc(m_free, 1)
                    elif kind == "N":
                        c = x[1]
                        last_m = ("M", 1, TPC * c + TPC - 1, c)
                        pieces.reach(M_RING + par * N_M + M_AT[last_m] + 1)
                        b = c % 2
                        v.tensor_reduce(neg[:, b].rearrange("p (h i) -> p h i", h=2),
                                        part[:, :, TPC * c:TPC * c + TPC, 0:c + 1], AX.X, ALU.max,
                                        negate=True).then_inc(neg_done, 1)
                        negs.reach(1 + 2 * (par * NC + c) + 1)
                        v.tensor_copy(negb[:, b, 0], neg[:, b]).then_inc(neg_done, 1)
                        negs.reach(1 + 2 * (par * NC + c) + 2)
                        v.tensor_tensor(negb[:, b, 1], neg[:, b], negb[:, b, 0], ALU.subtract).then_inc(negb_done, 1)
                    elif kind == "R":
                        c = x[1]
                        turned_rows.reach(par * NC + c + 1)
                        row_loads[c % 2].reach(64 * (par * (NC // 2) + c // 2 + 1))
                        v.tensor_copy(rows[:, c % 2, :], row_b16[0:16, 0:P]).then_inc(row_free, 1)
                    elif kind == "O":
                        c = x[1]
                        b = c % 2
                        o = row_bank[:, 0:TPC * 2 * OW].rearrange("p (j h w) -> p j h w", j=TPC, h=2)
                        outputs.reach(2 + par * NC + c + 1)
                        ao_stores[b].reach(16 * (par * (NC // 2) + c // 2 + 1))
                        v.reciprocal(rden[:, b], o[:, :, :, DH]).then_inc(rden_done, 1)
                        rdens.reach(par * NC + c + 1)
                        v.tensor_tensor(ao_sb[:, b].rearrange("p j (h d) -> p j h d", h=2), o[:, :, :, 0:DH],
                                        rden[:, b].unsqueeze(3).broadcast_to([P, TPC, 2, DH]), ALU.mult).then_inc(row_free, 1)
                    elif kind == "X":
                        f = x[1]
                        k = ITEM_AT[x]
                        items.reach(par * N_F + k + 1)
                        v.tensor_copy(slab_xt[:, :, :].rearrange("p c t -> p (c t)"), f_bank[k % F_RING][:, :]).then_inc(f_free, 1)
                    elif kind == "H" and x[3] == 3:
                        _, f, u, _ = x
                        k = ITEM_AT[x[:3]]
                        buf = (par * SLABS + f) % 2
                        sigs.reach(par * N_H + HIDDEN_AT[x[:3]] + 1)
                        for w in range(2):
                            last = v.scalar_tensor_tensor(hid[buf][:, 2 * u + w, :], f_bank[k % F_RING][:, w * D:(w + 1) * D],
                                                          b1_sb[par][:, 2 * u + w:2 * u + w + 1],
                                                          sig[:, k % 2, w * D:(w + 1) * D], ALU.add, ALU.mult)
                        last.then_inc(f_free, 1)
                    elif kind == "Y" and x[2] == 15:
                        f = x[1]
                        k = ITEM_AT[x[:2]]
                        buf = (par * SLABS + f) % 2
                        items.reach(par * N_F + k + 1)
                        y_stores[buf].reach(16 * ((par * SLABS + f) // 2 + 1))
                        v.tensor_tensor(y_sb[:, buf], f_bank[k % F_RING][:, :].rearrange("p (j d) -> p j d", j=SLAB_T),
                                        b2_sb[par][:, :].unsqueeze(1).broadcast_to([P, SLAB_T, D]), ALU.add).then_inc(f_free, 1)

            scored = Waits(dve, m_ready, 2 * N_M)
            pieces = Waits(dve, m_free, 2 * N_M, M_RING)
            negs = Waits(dve, neg_done, 4 * NC, 1)
            turned_rows = Waits(dve, row_done, 2 * NC)
            row_loads = [Waits(dve, row_dma[i], 64 * NC, 64) for i in range(2)]
            outputs = Waits(dve, o_used, 2 * NC, 2)
            ao_stores = [Waits(dve, ao_store[i], 16 * NC, 16) for i in range(2)]
            rdens = Waits(dve, rden_done, 2 * NC)
            items = Waits(dve, f_ready, 2 * N_F)
            sigs = Waits(dve, sig_done, 2 * N_H)
            y_stores = [Waits(dve, y_store[i], 16 * SLABS, 16) for i in range(2)]
            with dve.Fori(0, ROUNDS // 2) as n:
                for par in range(2):
                    dve_round(n, par)
                for w in (scored, pieces, negs, turned_rows, *row_loads, outputs, *ao_stores, rdens, items, sigs, *y_stores):
                    w.end_pass()

            def dve_back(i, n, par):
                dve.wait_ge(b_load[par], 48 * (n + 1))
                dve.wait_ge(b_gather[par], 16 * TOPK * BT * (n + 1))
                dve.wait_ge(b_idx, 2 * i + 2)
                done = [B_DVE * i]

                def stage(op):
                    for j in range(BT):
                        last = op(j)
                    done[0] = done[0] + 1
                    last.then_inc(b_dve, 1)
                    dve.wait_ge(b_dve, done[0])

                stage(lambda j: v.scalar_tensor_tensor(bxn[par][:, j], g_row[par][:, 0, j], bgate[:, par, 0, j:j + 1],
                                                       bxn[par][:, j], ALU.mult, ALU.add))
                stage(lambda j: v.scalar_tensor_tensor(bres[par][:, j], g_row[par][:, 1, j], bgate[:, par, 1, j:j + 1],
                                                       bxn[par][:, j], ALU.mult, ALU.add))
                stage(lambda j: v.bn_stats(stats[:, par, j, :], bres[par][:, j]))
                dve.sem_inc(idle, 1)
                stage(lambda j: v.bn_aggr(mean_var[:, par, j, :], stats[:, par, j, :]))
                stage(lambda j: v.scalar_tensor_tensor(bxn[par][:, j], bres[par][:, j], mean_var[:, par, j, 0:1],
                                                       gam[:, :], ALU.subtract, ALU.mult))
                dve.wait_ge(b_rstd, 2 * i + 2)
                dve.wait_ge(b_proj, i + 3)
                dve.wait_ge(b_store[par], 16 * n + 16)
                for j in range(BT):
                    o = bank[2 + 2 * par + j * D // CH][:, j * D % CH:j * D % CH + D]
                    last = v.scalar_tensor_tensor(bout[par][:, j], bxn[par][:, j], rstd[:, par, j:j + 1], o,
                                                  ALU.mult, ALU.add)
                last.then_inc(b_out, 1)

            with dve.Fori(0, NB // 2) as n:
                for par in range(2):
                    dve_back(2 * n + par, n, par)


def kernel(**inputs):
    import numpy as np
    import concourse.bacc as bacc
    from concourse.bass_utils import run_bass_kernel_spmd

    a = {k: np.asarray(v) for k, v in inputs.items()}
    arrays = {
        "x": a["L0_attn_query"].reshape(T, D),
        "wqkv": a["L0_attn_in_proj_weight"].T,
        "wo": a["L0_attn_out_proj_weight"].T,
        "wg": a["L0_ffn_wg"],
        "w1": a["L0_ffn_fc1_w"].transpose(0, 2, 1),
        "b1": a["L0_ffn_fc1_b"].reshape(E, HC, P).transpose(2, 0, 1),
        "w2": a["L0_ffn_fc2_w"],
        "b2": a["L0_ffn_fc2_b"],
        "gamma": a["L0_ffn_ln_gamma"],
        "beta": a["L0_ffn_ln_beta"],
    }
    arrays = {k: np.ascontiguousarray(v) for k, v in arrays.items()}
    nc = bacc.Bacc("TRN2", target_bir_lowering=False, num_devices=1)
    args = {k: nc.dram_tensor(f"in_{k}", v.shape, mybir.dt.from_np(v.dtype), kind="ExternalInput").ap()
            for k, v in arrays.items()}
    out = nc.dram_tensor("out", (T, D), F32, kind="ExternalOutput").ap()
    build(nc, **args, out=out)
    r = run_bass_kernel_spmd(nc, [{f"in_{k}": v for k, v in arrays.items()}], core_ids=[0])
    return r.results[0]["out"].reshape(1, T, D)
```

```python
from contextlib import ExitStack

import concourse.bass as bass
from concourse import mybir

F32 = mybir.dt.float32
BF16 = mybir.dt.bfloat16
I32 = mybir.dt.int32
ACT = mybir.ActivationFunctionType
ALU = mybir.AluOpType
AX = mybir.AxisListType

P = 128
T, D = 4096, 256
NH, DH = 16, 16
E, HID, TOPK = 8, 1024, 2
CAP = TOPK * int(1.25 * ((T + E - 1) // E))
NT = T // P
DC = D // P
CH = 512
NC = T // CH
TPC = CH // P
ROUNDS = E
assert ROUNDS * 2 == NH
Q_PARTS = (0, 0, 1, 1, 0, 2)
K_PARTS = (0, 1, 0, 1, 2, 0)
ROWS = 6 * DH
AUG = ROWS + 2
LN_EPS = 1e-5
GATE_EPS = 1.1920929e-07
MASKED = -1e30
SLABS = 5
SLAB_T = CAP // P // SLABS
BT = TPC
NB = NT // BT
HC = HID // P
VW = 32
OW = DH + 1

LOADS = 2
SCATTER_NS = 80e3
POOL = 6
M_MOST, S_MOST, F_MOST = 3, 5, 2
P_SLOTS, GROUP = 8, 4


def round_steps(experts_at=0.0):
    experts = []
    for f in range(SLABS):
        if f == 0:
            experts += [("X", 0)] + [("H", 0, 0, s) for s in range(4)]
        for u in range(1, HC // 2):
            experts += [("H", f, u, s) for s in range(4)]
        if f + 1 < SLABS:
            experts += [("X", f + 1)] + [("H", f + 1, 0, s) for s in range(4)]
        experts += [("Y", f, s) for s in range(16)]

    maxima = []
    for c in range(NC):
        maxima += [("M", h, t, j) for t in range(TPC * c, TPC * c + TPC) for j in range(c + 1) for h in range(2)]
        maxima += [("N", c), ("R", c)]
    scored = [("S", c, h, 2 * g + b) for c in range(NC) for g in range(2 * c + 2) for b in range(2) for h in range(2)]
    sums = [("V", c, g, g == 2 * c + 1) for c in range(NC) for g in range(2 * c + 2)]

    hop, row_trip = HOP, ROW_TRIP
    pe = dve = act = 0.0
    m_free, s_free, f_free = [0.0] * M_MOST, [0.0] * S_MOST, [0.0] * F_MOST
    bank_free, bank_user = [0.0] * POOL, [None] * POOL
    bank_of, user_before = {}, {}
    slot_free, bank_v, o_bufs, row_use = [0.0] * (P_SLOTS // GROUP), 0.0, [0.0, 0.0], 0.0
    neg_at, rows_at, prob_at, done = {}, {}, {}, {}
    n_m = n_s = n_f = n_v = n_a = 0
    o_due = []
    out = []
    total = 1.1 * (sum(217 for _ in scored) * 2 + 900 * len(sums) + 430 * len(experts))
    spent = 0.0

    def width(x):
        if x[0] == "M":
            return (x[2] % TPC + 1) * P if x[3] == x[2] // TPC else CH
        return CH - max(0, x[3] - TPC * x[1]) * P

    def take_bank(x, user):
        b = min(range(POOL), key=lambda i: bank_free[i])
        bank_of[x], user_before[x] = b, bank_user[b]
        bank_user[b], bank_free[b] = user, float("inf")
        return b

    while maxima or scored or sums or experts or o_due:
        choice = []
        any_bank = min(bank_free)
        if maxima:
            x = maxima[0]
            if x[0] == "M":
                choice.append((max(m_free[n_m % M_MOST], any_bank), 2, "m", x))
            elif x[0] == "N":
                choice.append((0.0, -1, "m", x))
            else:
                choice.append((max(neg_at[x[1]], row_use), 0, "m", x))
        if scored:
            x = scored[0]
            ready = rows_at.get(x[1])
            ahead = n_m - n_s >= AHEAD * (x[1] + 1) + AHEAD_0 or maxima == []
            if ready is not None and ahead and n_s // GROUP - n_v < P_SLOTS // GROUP:
                choice.append((max(ready, s_free[n_s % S_MOST], any_bank), 1, "s", x))
        if sums and (n_v + 1) * GROUP <= n_s:
            x = sums[0]
            choice.append((max(prob_at[n_v], bank_v if x[2] == 0 else 0.0), 0.5, "v", x))
        if o_due:
            choice.append((max(o_due[0][0], row_use), 0.7, "o", o_due[0][1]))
        if experts:
            x = experts[0]
            at = experts_at
            if x[0] != "H" or x[3] == 0:
                if x[0] != "Y" or x[2] == 0:
                    at = max(at, f_free[n_f % F_MOST], any_bank)
            if x[0] == "H" and x[2] == 0 and x[3] == 0:
                at = max(at, done[("X", x[1])])
            if x[0] == "Y" and x[2] == 0:
                at = max(at, done[("H", x[1], HC // 2 - 1)])
            share = 1 - len(experts) / (SLABS * 33)
            choice.append((at, 0.8 if share < F_PACE * (spent - experts_at) / (total - experts_at) else 3, "f", x))
        ready = [ch for ch in choice if ch[0] <= pe + 20]
        at, _, stream, x = min(ready, key=lambda ch: ch[1]) if ready else min(choice, key=lambda ch: ch[:2])
        pe = max(pe, at)
        out.append(x)
        cost = 0.0
        if stream == "m":
            maxima.pop(0)
            if x[0] == "M":
                w = width(x)
                b = take_bank(x, ("M", n_m))
                cost = w / 2.4 + 3 + (56 if x[3] == x[2] // TPC else 0)
                dve = max(dve, pe + cost + hop) + (w + 62) / 0.96
                m_free[n_m % M_MOST] = bank_free[b] = dve + hop
                n_m += 1
            elif x[0] == "N":
                dve += 700
                neg_at[x[1]] = dve + hop
            else:
                cost = 60
                dve = max(dve, pe + cost + hop) + 250
                row_use = dve + hop
                rows_at[x[1]] = dve + row_trip
        elif stream == "s":
            scored.pop(0)
            w = width(x)
            b = take_bank(x, ("S", n_s))
            cost = w / 2.4 + 3 + (56 if x[3] >= TPC * x[1] else 0)
            act = max(act, pe + cost + hop, slot_free[n_s // GROUP % (P_SLOTS // GROUP)]) + (w + 70) / 1.2
            s_free[n_s % S_MOST] = bank_free[b] = act + hop
            prob_at[n_s // GROUP] = act + hop
            n_s += 1
        elif stream == "v":
            sums.pop(0)
            cost = 930 if x[2] < 2 * x[1] else 850 if not x[3] else 500
            slot_free[n_v % (P_SLOTS // GROUP)] = pe + cost + hop
            n_v += 1
            if x[3]:
                act = max(act, pe + cost + hop) + 480
                bank_v = act + hop
                o_due.append((act + hop, ("O", x[1])))
        elif stream == "o":
            o_due.pop(0)
            cost = 860
            dve = max(dve, pe + cost + hop) + 450
            row_use = dve + hop
        else:
            experts.pop(0)
            cost = 430
            item = x[:3] if x[0] == "H" else x[:2]
            if x[0] == "X" or x[-1] == 0:
                user = ("D", x[1]) if x[0] == "Y" else ("A", n_a)
                n_a += x[0] != "Y"
                f_bank = take_bank(item, user)
            if x[0] == "X":
                act = max(act, pe + cost + hop) + 480
            elif x[0] == "H" and x[3] == 3:
                act = max(act, pe + cost + hop) + 4 * 358
                dve = max(dve, act + hop) + 610
            elif x[0] == "Y" and x[2] == 15:
                dve = max(dve, pe + cost + hop) + 600
            if x[0] == "X" or x[-1] == (3 if x[0] == "H" else 15):
                done[item] = (act if x[0] == "X" else dve) + hop
                f_free[n_f % F_MOST] = bank_free[f_bank] = (dve if x[0] == "Y" else act) + hop
                n_f += 1
        pe += cost
        spent += cost
    round_steps.length = pe
    return out, bank_of, user_before


AHEAD, AHEAD_0, F_PACE, HOP, ROW_TRIP = 9, 16, 0.8, 190, 4500


class Plan:

    def __init__(self, experts_at=0.0):
        self.steps, self.bank, self.before = round_steps(experts_at)
        self.row_at = numbered(self.steps, "RO")


def numbered(steps, kinds):
    return {x: n for n, x in enumerate([x for x in steps if x[0] in kinds])}


FIRST, PLAN = Plan(experts_at=SCATTER_NS), Plan()
M_AT, S_AT, V_AT = (numbered(PLAN.steps, k) for k in "MSV")
N_M, N_S, N_V, N_ROW = len(M_AT), len(S_AT), len(V_AT), len(PLAN.row_at)
ITEMS = [x[:3] if x[0] == "H" else x[:2] for x in PLAN.steps
         if x[0] == "X" or (x[0] in "HY" and x[-1] == 0)]
ITEM_AT = {x: n for n, x in enumerate(ITEMS)}
HIDDEN_AT = {x: n for n, x in enumerate([x for x in ITEMS if x[0] == "H"])}
N_F, N_H = len(ITEMS), len(HIDDEN_AT)
A_AT = {x: n for n, x in enumerate([x for x in ITEMS if x[0] in "XH"])}

N_KIND = {"M": N_M, "S": N_S, "A": len(A_AT), "D": SLABS}


def last_users():
    out = [{} for _ in range(POOL)]
    for plan in (FIRST, PLAN):
        used = {}
        for x in plan.steps:
            key = x[:3] if x[0] == "H" else x[:2] if x[0] == "Y" else x
            if key in plan.bank:
                kind = {"X": "A", "H": "A", "Y": "D"}.get(key[0], key[0])
                at = {"M": M_AT, "S": S_AT, "A": A_AT, "D": {("Y", f): f for f in range(SLABS)}}[kind][key]
                used[plan.bank[key]] = (kind, at)
        for b, (kind, at) in used.items():
            out[b][kind] = max(at, out[b].get(kind, 0))
    return out


LAST_USERS = last_users()
Y_STORES = (SLABS + 1) // 2, SLABS // 2


class Waits:

    def __init__(self, engine, sem, per_round, start=0, wait=None, per_pass=None):
        self.wait = wait or engine.wait_ge
        self.engine, self.sem, self.at = engine, sem, start
        self.base = start + per_round
        self.per_pass = per_pass or 2 * per_round
        self.reg = engine.alloc_register(f"{engine.engine.name}_{sem.name}_{start}_{engine.bass.next_id()}")
        engine.reg_mov(self.reg, start)
        self.waited = False

    def reach(self, value):
        if value > self.at or not self.waited:
            self.move(max(value, self.at))
            self.waited = True
            self.wait(self.sem, self.reg)

    def move(self, value):
        if value != self.at:
            assert value > self.at, (self.sem.name, value, self.at)
            self.engine.reg_add(self.reg, self.reg, value - self.at)
            self.at = value

    def begin_loop(self):
        self.move(self.base)
        self.waited = False

    def end_pass(self):
        self.move(self.base + self.per_pass)
        self.at = self.base
        self.waited = False


def rounds(engine, one, waits):
    one(0, 0, 0, FIRST)
    for w in waits:
        w.begin_loop()
    with engine.Fori(0, ROUNDS // 2 - 1) as n:
        one(2 * n + 1, n, 1, PLAN)
        one(2 * n + 2, n + 1, 2, PLAN)
        for w in waits:
            w.end_pass()
    one(ROUNDS - 1, ROUNDS // 2 - 1, 1, PLAN)


def build(nc, x, wqkv, wo, wg, w1, b1, w2, b2, gamma, beta, out):
    with ExitStack() as ctx:
        def sb(name, shape, dt=F32):
            return ctx.enter_context(nc.sbuf_tensor(name, shape, dt))

        def dram(name, shape, dt=F32):
            return nc.dram_tensor(name, shape, dt, kind="Internal").ap()

        def sem(name):
            return ctx.enter_context(nc.semaphore(name))

        xn_d = dram("xn_d", (T, D))
        qk_d = dram("qk_d", (3, 2 * D, T), BF16)
        slot_d = dram("slot_d", (E * CAP, 1), I32)
        y_d = dram("y_d", (E * CAP + 1, D))
        ao_d = dram("ao_d", (T, D))

        v_all = sb("v_all", [P, NT, D])
        q_op0, k_op0 = sb("q_op0", [P, 2, T], BF16), sb("k_op0", [P, 2, T], BF16)
        zone = sb("zone", [P, 16384])
        v_op = sb("v_op", [P, NT, 2, VW])
        w1_sb = [sb(f"w1_sb{i}", [P, DC, HID]) for i in range(2)]
        w2_sb = [sb(f"w2_sb{i}", [P, HC, D]) for i in range(2)]
        b1_sb = [sb(f"b1_sb{i}", [P, HC]) for i in range(2)]
        b1h_sb = [sb(f"b1h_sb{i}", [P, HC]) for i in range(2)]
        b2_sb = [sb(f"b2_sb{i}", [P, D]) for i in range(2)]
        slab_x = sb("slab_x", [P, SLAB_T, D])
        slab_xt = sb("slab_xt", [P, DC, SLAB_T * P])
        tanh = sb("tanh", [P, 2, CH])
        y_sb = sb("y_sb", [P, 2, SLAB_T, D])
        o_sb = sb("o_sb", [P, 2, CH])
        ao_sb = sb("ao_sb", [P, 2, TPC, 2 * DH])
        rden = sb("rden", [P, 2, TPC, 2])
        part = sb("part", [P, 2, NT, NC])
        neg = sb("neg", [P, 2, 8])
        negb = sb("negb", [P, 2, 2, 8], BF16)
        rows = sb("rows", [16, 2, P], BF16)
        wo_sb = sb("wo_sb", [P, DC, D])
        gam, bet = sb("gam", [P, D]), sb("bet", [P, D])
        ident, identb = sb("ident", [P, P]), sb("identb", [P, P], BF16)
        mask_m, mask_s = sb("mask_m", [P, P], BF16), sb("mask_s", [P, P], BF16)
        tri, onesb = sb("tri", [P, P], BF16), sb("onesb", [P, P], BF16)
        pick = sb("pick", [P, 2 * OW])
        zeros = sb("zeros", [P, P])
        down = sb("down", [P, E])
        logits = sb("logits", [P, NT, E])
        gate = sb("gate", [P, TOPK, NT])
        pos = sb("pos", [P, TOPK, NT], I32)
        token = sb("token", [P, NT], I32)
        slot_tok = sb("slot_tok", [P, E + 1, CAP // P], I32)
        slot_cur = sb("slot_cur", [P, CAP // P], I32)
        stats = sb("stats", [P, 2, TPC, 6])
        mean_var = sb("mean_var", [P, 2, TPC, 2])
        rstd = sb("rstd", [P, 2, TPC])
        half = sb("half", [P, TPC])
        bpos, bgate = sb("bpos", [P, 2, TOPK, BT], I32), sb("bgate", [P, 2, TOPK, BT])
        ones_row = sb("ones_row", [1, P])

        def view(a, n, dt=F32):
            v = zone[:, a:a + n]
            return v if dt == F32 else v.bitcast(dt)

        q_op = [q_op0[:, :, :], view(0, 4096, BF16).rearrange("p (h t) -> p h t", h=2)]
        k_op = [k_op0[:, :, :], view(4096, 4096, BF16).rearrange("p (h t) -> p h t", h=2)]
        prob = view(8192, P_SLOTS * CH).rearrange("p (s t) -> p s t", s=P_SLOTS)
        hid = [view(12288 + i * 2048, 2048).rearrange("p (c t) -> p c t", c=HC) for i in range(2)]
        x_in = [view(i * 1024, 1024).rearrange("p (j d) -> p j d", j=TPC) for i in range(2)]
        xn = [view(2048 + i * 1024, 1024).rearrange("p (j d) -> p j d", j=TPC) for i in range(2)]
        xt = [view(4096 + i * 1024, 1024).rearrange("p (c t) -> p c t", c=DC) for i in range(2)]
        resid = view(6144, 2048).rearrange("p (w t) -> p w t", w=4)
        split = [view(8192 + i * 3072, 3072, BF16).rearrange("p (s w t) -> p s w t", s=3, w=4)
                 for i in range(2)]
        wq_sb = view(14336, DC * (3 * D + E)).rearrange("p (c f) -> p c f", c=DC)
        r_score = view(0, 256).rearrange("p (i e) -> p i e", e=E)
        r_exp = view(256, 256).rearrange("p (i e) -> p i e", e=E)
        r_tmp = view(512, 256).rearrange("p (i e) -> p i e", e=E)
        r_hot = view(768, 512).rearrange("p (k i e) -> p k i e", k=TOPK, e=E)
        r_hotb = view(1280, 256, BF16).rearrange("p (k i e) -> p k i e", k=TOPK, e=E)
        r_own = view(3072, 512).rearrange("p (k i e) -> p k i e", k=TOPK, e=E)
        r_small = [view(3584 + i * 64, 64).rearrange("p (k i) -> p k i", k=TOPK) for i in range(6)]
        r_one = [view(3968 + i * 32, 32) for i in range(4)]
        bx, bxn, bao, bres, baot, bout = (
            [view((8 * i + n) * BT * D, BT * D).rearrange("p (j d) -> p j d", j=BT) for i in range(2)] for n in range(6))
        g_row = [view((8 * i + 6) * BT * D, TOPK * BT * D).rearrange("p (k j d) -> p k j d", k=TOPK, j=BT) for i in range(2)]

        bank = [ctx.enter_context(nc.psum_tensor(f"bank{i}", [P, CH], F32)) for i in range(8)]
        v_bank, row_bank = bank[POOL], bank[POOL + 1]
        row_b16 = row_bank[:, :].bitcast(BF16)

        idle = sem("idle")
        consts, consts2 = sem("consts"), sem("consts2")
        const_dma, x_dma = sem("const_dma"), [sem(f"x_dma{i}") for i in range(2)]
        stat_done, rstd_done, xn_done = sem("stat_done"), sem("rstd_done"), sem("xn_done")
        xn_store = [sem(f"xn_store{i}") for i in range(2)]
        turned, xt_ready, qk_done, part1, resid_done, split_done = (
            sem(n) for n in ("turned", "xt_ready", "qk_done", "part1", "resid_done", "split_done"))
        part2 = sem("part2")
        split_store = [sem(f"split_store{i}") for i in range(2)]
        v_done, v_free = sem("v_done"), sem("v_free")
        rt_dve, rt_act, rt_hot, rt_pe, pos_ready = (sem(n) for n in ("rt_dve", "rt_act", "rt_hot", "rt_pe", "pos_ready"))
        zero_dma, scatter, slot_load = sem("zero_dma"), sem("scatter"), sem("slot_load")
        rounds_ready = sem("rounds_ready")
        qk_load, w_load = [sem(f"qk_load{i}") for i in range(2)], [sem(f"w_load{i}") for i in range(2)]
        v_ready, b1h_ready, round_done = sem("v_ready"), sem("b1h_ready"), sem("round_done")
        m_ready, m_free, s_ready, s_done = sem("m_ready"), sem("m_free"), sem("s_ready"), sem("s_done")
        neg_done, negb_done = sem("neg_done"), sem("negb_done")
        row_done, row_free = sem("row_done"), sem("row_free")
        row_dma = [sem(f"row_dma{i}") for i in range(2)]
        pv_done, o_ready, o_used, rden_done = sem("pv_done"), sem("o_ready"), sem("o_used"), sem("rden_done")
        ao_store = [sem(f"ao_store{i}") for i in range(2)]
        idx_ready, slab_dma = sem("idx_ready"), sem("slab_dma")
        f_ready, hid_done = sem("f_ready"), sem("hid_done")
        f_act, f_dve = sem("f_act"), sem("f_dve")
        y_store = [sem(f"y_store{i}") for i in range(2)]
        b_load, b_gather = [sem(f"b_load{i}") for i in range(2)], [sem(f"b_gather{i}") for i in range(2)]
        b_idx, b_dve, b_rstd, b_turn, b_aot, b_proj, b_out = (
            sem(n) for n in ("b_idx", "b_dve", "b_rstd", "b_turn", "b_aot", "b_proj", "b_out"))
        b_store = [sem(f"b_store{i}") for i in range(2)]

        x_t = x.rearrange("(i p) d -> p i d", p=P)
        xn_t = xn_d.rearrange("(i p) d -> p i d", p=P)
        ao_t = ao_d.rearrange("(i p) d -> p i d", p=P)
        out_t = out.rearrange("(i p) d -> p i d", p=P)
        slot_2d = slot_d.rearrange("(p j) o -> p (j o)", p=P)
        slot_t = slot_d.rearrange("(e p j) o -> p e (j o)", e=E, p=P)
        y_t = y_d[0:E * CAP, :].rearrange("(e p j) d -> e p j d", e=E, p=P)

        N_CONST = 7
        B_DVE = 5

        def chunks(engine, begin, rest):
            begin(0, 0)
            with engine.Fori(0, NC // 2 - 1) as n:
                rest(n, 0, lambda: begin(n, 1))
                rest(n, 1, lambda: begin(n + 1, 0))
            rest(NC // 2 - 1, 0, lambda: begin(NC // 2 - 1, 1))
            rest(NC // 2 - 1, 1, lambda: None)

        block = ctx.enter_context(nc.Block())

        @block.sync
        def _(sp):
            sp.dma_start(wq_sb[:, :, 0:3 * D], wqkv.rearrange("(c p) f -> p c f", p=P)).then_inc(const_dma, 16)
            sp.dma_start(wq_sb[:, :, 3 * D:], wg.rearrange("(c p) f -> p c f", p=P)).then_inc(const_dma, 16)
            sp.dma_start(wo_sb[:, :, :], wo.rearrange("(c p) f -> p c f", p=P)).then_inc(const_dma, 16)
            sp.dma_start(gam[:, :], gamma.rearrange("(a d) -> a d", a=1).broadcast_to([P, D])).then_inc(const_dma, 16)
            sp.dma_start(bet[:, :], beta.rearrange("(a d) -> a d", a=1).broadcast_to([P, D])).then_inc(const_dma, 16)
            sp.wait_ge(consts, 1)
            sp.dma_start(slot_2d, zeros[:, 0:E * CAP // P].bitcast(I32)).then_inc(zero_dma, 16)
            sp.dma_start(y_d[E * CAP:, :].rearrange("a (b d) -> (a b) d", b=2), zeros[0:2, :]).then_inc(zero_dma, 16)

            def load_x(c, par, before=None):
                if before is not None:
                    sp.wait_ge(xn_done, before)
                sp.dma_start(x_in[par], x_t[:, bass.ds(c * TPC, TPC), :]).then_inc(x_dma[par], 16)

            def store_front(c, par):
                sp.wait_ge(xn_done, c + 1)
                sp.dma_start(xn_t[:, bass.ds(c * TPC, TPC), :], xn[par]).then_inc(xn_store[par], 16)
                sp.wait_ge(split_done, 4 * c + 8)
                for s in range(3):
                    sp.dma_start(qk_d[s].rearrange("(w p) t -> p w t", p=P)[:, :, bass.ds(c * CH, CH)],
                                 split[par][:, s]).then_inc(split_store[par], 16)

            load_x(0, 0)
            load_x(1, 1)
            with sp.Fori(0, NC // 2 - 1) as n:
                for par in range(2):
                    load_x(2 * n + 2 + par, par, before=2 * n + par + 1)
                    store_front(2 * n + par, par)
            for par in range(2):
                store_front(NC - 2 + par, par)

            def loads(r, par):
                def load(dst, src, done):
                    return lambda: sp.dma_start(dst, src).then_inc(done, 16)

                out = []
                for g in range(6):
                    for op, parts, first in ((q_op, Q_PARTS, 0), (k_op, K_PARTS, D)):
                        src = qk_d[parts[g], bass.ds(r * 2 * DH + first, 2 * DH), :]
                        out.append(load(op[par][g * DH:(g + 1) * DH], src.rearrange("(h r) t -> r h t", h=2), qk_load[par]))
                for w, src in ((w1_sb, w1), (w2_sb, w2)):
                    out.append(load(w[par][:, :, :], src[bass.ds(r, 1)].rearrange("o (c p) f -> p (o c) f", p=P), w_load[par]))
                out.append(load(b1_sb[par][:, :], b1[:, bass.ds(r, 1), :].rearrange("p o c -> p (o c)"), w_load[par]))
                out.append(load(b2_sb[par][:, :], b2[bass.ds(r, 1), :].broadcast_to([P, D]), w_load[par]))
                return out

            def sp_round(r, half, nth, plan):
                par = nth % 2
                last = isinstance(r, int) and r == ROUNDS - 1
                due = [] if last else loads(r + 1, 1 - par)
                if due:
                    sp.wait_ge(round_done, r + 1)
                    if nth > 0:
                        sp.sem_inc(idle, 1)
                        sp.wait_ge(f_dve, r * SLABS)
                    sp.sem_inc(idle, 1)
                for x in plan.steps:
                    if x[0] == "R":
                        c = x[1]
                        rows_out.reach(1 + nth * N_ROW + plan.row_at[x] + 1)
                        for s in range(2):
                            for h in range(2):
                                a = 8 * s + TPC * h
                                sp.dma_start(q_op[par][ROWS + s:ROWS + s + 1, h, c * CH:(c + 1) * CH]
                                             .rearrange("o (t q) -> o t q", t=TPC),
                                             rows[a:a + TPC, c % 2, :]).then_inc(row_dma[c % 2], 16)
                    elif x[0] == "O":
                        c = x[1]
                        rows_out.reach(1 + nth * N_ROW + plan.row_at[x] + 1)
                        sp.sem_inc(idle, 1)
                        sp.dma_start(ao_t[:, c * TPC:(c + 1) * TPC, bass.ds(r * 2 * DH, 2 * DH)],
                                     ao_sb[:, c % 2]).then_inc(ao_store[c % 2], 16)
                    elif x[0] == "Y" and x[2] == 15:
                        f = x[1]
                        buf = (nth * SLABS + f) % 2
                        slabs_out.reach(nth * SLABS + f + 1)
                        sp.sem_inc(idle, 1)
                        sp.dma_start(y_t[bass.ds(r, 1), :, f * SLAB_T:(f + 1) * SLAB_T, :].rearrange("o p j d -> (o p) j d"),
                                     y_sb[:, buf]).then_inc(y_store[buf], 16)
                    if x[0] in "RO":
                        for load in due[:LOADS]:
                            load()
                        due = due[LOADS:]

            for i in range(2):
                sp.wait_ge(split_store[i], 48 * (NC // 2 + 1))
            for load in loads(0, 0):
                load()
            for i in range(2):
                sp.wait_ge(xn_store[i], 16 * (NC // 2 + 1))
            sp.wait_ge(rounds_ready, 1)
            sp.wait_ge(pos_ready, 1)
            rows_out = Waits(sp, row_free, N_ROW, 1)
            slabs_out = Waits(sp, f_dve, SLABS)
            rounds(sp, sp_round, (rows_out, slabs_out))

            sp.wait_ge(round_done, ROUNDS + 1)
            for i in range(2):
                sp.wait_ge(ao_store[i], 16 * (ROUNDS * NC // 2 + 1))

            def load_back(i, par):
                for dst, src in ((bxn, xn_t), (bao, ao_t), (bx, x_t)):
                    sp.dma_start(dst[par], src[:, bass.ds(i * BT, BT), :]).then_inc(b_load[par], 16)

            def store_back(i, par):
                sp.wait_ge(b_out, i + 2)
                sp.dma_start(out_t[:, bass.ds(i * BT, BT), :], bout[par]).then_inc(b_store[par], 16)

            load_back(0, 0)
            load_back(1, 1)
            with sp.Fori(0, NB // 2 - 1) as n:
                for par in range(2):
                    store_back(2 * n + par, par)
                    load_back(2 * n + 2 + par, par)
            for par in range(2):
                store_back(NB - 2 + par, par)
            for i in range(2):
                sp.wait_ge(b_store[i], 16 * (NB // 2 + 1))

        @block.gpsimd
        def _(pool):
            g = nc.gpsimd
            def wait(sem, value):
                pool.wait_ge(sem, value)
                if not isinstance(value, int):
                    pool.sem_inc(idle, 1)

            g.memset(zeros[:, :], 0.0).then_inc(consts, 1)
            g.memset(ident[:, :], 0.0).then_inc(consts, 1)
            g.memset(identb[:, :], 0.0).then_inc(consts, 1)
            g.memset(mask_m[:, :], 0.0).then_inc(consts, 1)
            g.memset(mask_s[:, :], 0.0).then_inc(consts, 1)
            g.memset(onesb[:, :], 1.0).then_inc(consts, 1)
            g.memset(tri[:, :], 1.0).then_inc(consts, 1)
            g.memset(pick[:, :], 0.0).then_inc(consts, 1)
            g.memset(v_op[:, :, :, :], 0.0).then_inc(consts, 1)
            g.memset(slot_tok[:, :, :], 0).then_inc(consts, 1)
            g.memset(half[:, :], -0.5).then_inc(consts, 1)
            g.memset(ones_row[:, :], 1.0).then_inc(consts, 1)
            wait(consts, 12)
            for m in (ident, identb):
                g.affine_select(out=m[:, :], in_=m[:, :], compare_op=ALU.not_equal, fill=1.0, base=0,
                                pattern=[[-1, P]], channel_multiplier=1).then_inc(consts2, 1)
            g.affine_select(out=mask_m[:, :], in_=mask_m[:, :], compare_op=ALU.is_ge, fill=MASKED, base=0,
                            pattern=[[-1, P]], channel_multiplier=1).then_inc(consts2, 1)
            g.affine_select(out=mask_s[:, :], in_=mask_s[:, :], compare_op=ALU.is_ge, fill=MASKED, base=0,
                            pattern=[[1, P]], channel_multiplier=-1).then_inc(consts2, 1)
            g.affine_select(out=tri[:, :], in_=tri[:, :], compare_op=ALU.is_ge, fill=0.0, base=0,
                            pattern=[[1, P]], channel_multiplier=-1).then_inc(consts2, 1)
            for h in range(2):
                for s in range(2):
                    wait(consts2, 5 + 2 * h + s)
                    g.affine_select(out=pick[:, h * OW:(h + 1) * OW], in_=pick[:, h * OW:(h + 1) * OW],
                                    compare_op=ALU.not_equal, fill=1.0, base=-VW * (2 * h + s),
                                    pattern=[[-1, OW]], channel_multiplier=1).then_inc(consts2, 1)
            g.memset(v_op[:, :, :, DH:DH + 1], 1.0).then_inc(consts2, 1)
            g.iota(token[:, :], pattern=[[P, NT]], base=0, channel_multiplier=1).then_inc(consts2, 1)
            for i in range(E):
                g.memset(down[:, i:i + 1], float(E - i)).then_inc(consts2, 1)
            wait(consts2, 9 + 1 + 1 + E)
            g.memset(k_op0[ROWS:ROWS + 2, :, :], 1.0).then_inc(consts2, 1)
            wait(consts2, 9 + 1 + 1 + E + 1)

            pool.sem_inc(split_done, 4)
            def begin_chunk(n, par):
                c = 2 * n + par
                wait(stat_done, 2 * c + 2)
                g.tensor_scalar(rstd[:, par, :], mean_var[:, par, :, 1], LN_EPS, None, ALU.add).then_inc(rstd_done, 1)
                wait(rstd_done, 2 * c + 1)
                g.tensor_tensor(rstd[:, par, :], rstd[:, par, :], half[:, :], ALU.pow).then_inc(rstd_done, 1)

            def split_chunk(n, par, begin_next):
                c = 2 * n + par
                begin_next()
                for w in range(4):
                    wait(part2, 4 * c + w + 1)
                    g.tensor_tensor(split[par][:, 2, w], resid[:, w], split[par][:, 1, w],
                                    ALU.subtract).then_inc(split_done, 1)

            chunks(pool, begin_chunk, split_chunk)

            def v_operand(r):
                wait(round_done, r + 1)
                g.tensor_copy(v_op[:, :, :, 0:DH], v_all[:, :, bass.ds(r * 2 * DH, 2 * DH)]
                              .rearrange("p i (h d) -> p i h d", h=2)).then_inc(v_ready, 1)

            def half_bias(half, par):
                wait(w_load[par], 64 * (half + 1))
                g.tensor_scalar(b1h_sb[par][:, :], b1_sb[par][:, :], 0.5, None, ALU.mult).then_inc(b1h_ready, 1)

            wait(v_free, 2 + NT)
            wait(split_done, 4 + 4 * NC)
            g.memset(k_op[1][ROWS:ROWS + 2, :, :], 1.0).then_inc(rounds_ready, 1)
            wait(rounds_ready, 1)
            v_operand(0)

            wait(pos_ready, 1)
            wait(zero_dma, 32)
            for k in range(TOPK):
                for i in range(NT):
                    g.indirect_dma_start(out=slot_d, out_offset=bass.IndirectOffsetOnAxis(ap=pos[:, k, i:i + 1], axis=0),
                                         in_=token[:, i:i + 1], in_offset=None,
                                         bounds_check=E * CAP - 1, oob_is_err=False).then_inc(scatter, 16)
            wait(scatter, 16 * TOPK * NT)
            pool.dma_start(slot_tok[:, 0:E, :], slot_t).then_inc(slot_load, 16)
            wait(slot_load, 16)
            for i in range(2):
                wait(xn_store[i], 16 * (NC // 2 + 1))
            half_bias(0, 0)

            def gather(e, f, first):
                if first:
                    g.tensor_copy(slot_cur[:, :], slot_tok[:, bass.ds(e, 1), :].rearrange("p o j -> p (o j)")).then_inc(idx_ready, 1)
                    wait(idx_ready, e + 1)
                for j in range(SLAB_T):
                    g.indirect_dma_start(out=slab_x[:, j, :], out_offset=None, in_=xn_d,
                                         in_offset=bass.IndirectOffsetOnAxis(
                                             ap=slot_cur[:, f * SLAB_T + j:f * SLAB_T + j + 1], axis=0)
                                         ).then_inc(slab_dma, 16)

            def pool_round(r, half, nth, plan):
                par = nth % 2
                if nth > 0:
                    v_operand(r)
                    half_bias(half, par)
                for x in plan.steps:
                    if x[0] == "X":
                        f = x[1]
                        turned_slabs.reach(nth * N_F + ITEM_AT[x] + 1)
                        if f + 1 < SLABS:
                            gather(r, f + 1, False)
                        else:
                            slabs_in.reach(32 * (nth * SLABS + SLABS))
                            gather(r + 1, 0, True)

            gather(0, 0, True)
            turned_slabs = Waits(pool, f_ready, N_F, wait=wait)
            slabs_in = Waits(pool, slab_dma, 32 * SLABS, wait=wait)
            rounds(pool, pool_round, (turned_slabs, slabs_in))

            wait(slab_dma, 32 * (ROUNDS * SLABS + 1))
            for i in range(2):
                wait(y_store[i], 16 * (ROUNDS * SLABS // 2 + 1))
            wait(round_done, ROUNDS + 1)

            def pool_gather(i, par):
                g.tensor_copy(bpos[:, par], pos[:, :, bass.ds(i * BT, BT)]).then_inc(b_idx, 1)
                g.tensor_copy(bgate[:, par], gate[:, :, bass.ds(i * BT, BT)]).then_inc(b_idx, 1)
                wait(b_idx, 2 * i + 2)
                for j in range(BT):
                    for k in range(TOPK):
                        g.indirect_dma_start(out=g_row[par][:, k, j], out_offset=None, in_=y_d,
                                             in_offset=bass.IndirectOffsetOnAxis(ap=bpos[:, par, k, j:j + 1], axis=0)
                                             ).then_inc(b_gather[par], 16)

            def pool_rstd(i, par):
                wait(b_dve, B_DVE * i + 4)
                g.tensor_scalar(rstd[:, par, :], mean_var[:, par, :, 1], LN_EPS, None, ALU.add).then_inc(b_rstd, 1)
                wait(b_rstd, 2 * i + 1)
                g.tensor_tensor(rstd[:, par, :], rstd[:, par, :], half[:, :], ALU.pow).then_inc(b_rstd, 1)

            pool_gather(0, 0)
            pool_gather(1, 1)
            with pool.Fori(0, NB // 2 - 1) as n:
                for par in range(2):
                    pool_rstd(2 * n + par, par)
                    pool_gather(2 * n + par + 2, par)
            for par in range(2):
                pool_rstd(NB - 2 + par, par)

        @block.scalar
        def _(act):
            s = nc.scalar
            act.sem_inc(v_free, 2)
            act.sem_inc(xt_ready, 1)
            act.sem_inc(b_aot, 1)
            for i in range(2):
                act.sem_inc(split_store[i], 48)

            def begin_chunk(n, par):
                c = 2 * n + par
                act.wait_ge(turned, c + 1)
                for d in range(DC):
                    last = s.activation(xt[par][:, d], bank[d][:, :], ACT.Copy)
                last.then_inc(xt_ready, 1)

            def act_chunk(n, par, begin_next):
                c = 2 * n + par
                act.wait_ge(split_store[par], 48 * n + 48)
                for w in range(4):
                    act.wait_ge(qk_done, 4 * c + w + 1)
                    s.activation(split[par][:, 0, w], bank[2 + w][:, :], ACT.Copy,
                                 scale=DH ** -0.5 if w < 2 else 1.0).then_inc(part1, 1)
                begin_next()
                for j in range(TPC):
                    act.wait_ge(resid_done, 4 * c + j + 5)
                    s.activation(split[par][:, 1, j], resid[:, j], ACT.Copy).then_inc(part2, 1)
                    act.wait_ge(v_done, 4 * c + j + 1)
                    s.activation(v_all[:, bass.ds(c * TPC + j, 1), :].rearrange("p o d -> p (o d)"),
                                 bank[6 + j % 2][:, 0:D], ACT.Copy)
                    s.activation(logits[:, bass.ds(c * TPC + j, 1), :].rearrange("p o e -> p (o e)"),
                                 bank[6 + j % 2][:, D:D + E], ACT.Copy).then_inc(v_free, 1)

            chunks(act, begin_chunk, act_chunk)

            act.wait_ge(rt_dve, 2)
            s.activation(r_exp, r_tmp, ACT.Exp).then_inc(rt_act, 1)

            for i in range(2):
                act.wait_ge(split_store[i], 48 * (NC // 2 + 1))

            def act_round(r, half, nth, plan):
                par = nth % 2
                for x in plan.steps:
                    if x[0] == "S":
                        _, c, h, b = x
                        k = S_AT[x]
                        off = max(0, b - TPC * c) * P
                        scores.reach(nth * N_S + k + 1)
                        if k % GROUP == 0:
                            slots.reach(nth * N_V + k // GROUP + 1)
                        s.activation(prob[:, k % P_SLOTS, off:], bank[plan.bank[x]][:, 0:CH - off],
                                     ACT.Exp).then_inc(s_done, 1)
                    elif x[0] == "V" and x[3]:
                        c = x[1]
                        sums.reach(P_SLOTS // GROUP + nth * N_V + V_AT[x] + 1)
                        o_bufs.reach(nth * NC + c + 1)
                        s.activation(o_sb[:, c % 2], v_bank[:, :], ACT.Copy).then_inc(o_ready, 1)
                    elif x[0] == "H" and x[3] == 3:
                        _, f, u, _ = x
                        hidden.reach(nth * N_F + ITEM_AT[x[:3]] + 1)
                        z = bank[plan.bank[x[:3]]]
                        if f == 0 and u == 0:
                            act.wait_ge(b1h_ready, r + 1)
                        m = HIDDEN_AT[x[:3]]
                        tanhs.reach(nth * N_H + m + 1)
                        for v in range(2):
                            s.activation(hid[(nth * SLABS + f) % 2][:, 2 * u + v, :], z[:, v * D:(v + 1) * D],
                                         ACT.Identity, bias=b1h_sb[par][:, 2 * u + v:2 * u + v + 1], scale=0.5)
                        for v in range(2):
                            last = s.activation(tanh[:, m % 2, v * D:(v + 1) * D], z[:, v * D:(v + 1) * D],
                                                ACT.Tanh, bias=b1h_sb[par][:, 2 * u + v:2 * u + v + 1], scale=0.5)
                        last.then_inc(f_act, 1)
                    elif x[0] == "X":
                        hidden.reach(nth * N_F + ITEM_AT[x] + 1)
                        s.activation(slab_xt[:, :, :].rearrange("p c t -> p (c t)"), bank[plan.bank[x]][:, :],
                                     ACT.Copy).then_inc(f_act, 1)

            act.sem_inc(hid_done, 2)
            act.sem_inc(o_ready, 1)
            scores = Waits(act, s_ready, N_S)
            slots = Waits(act, pv_done, N_V)
            sums = Waits(act, pv_done, N_V, P_SLOTS // GROUP)
            o_bufs = Waits(act, o_used, NC)
            hidden = Waits(act, f_ready, N_F)
            tanhs = Waits(act, hid_done, N_H)
            rounds(act, act_round, (scores, slots, sums, o_bufs, hidden, tanhs))

            def act_back(i, par):
                act.wait_ge(b_turn, i + 1)
                act.wait_ge(b_proj, i + 1)
                for h in range(2):
                    last = s.activation(baot[par][:, h * BT // 2:(h + 1) * BT // 2].rearrange("p j d -> p (j d)"),
                                        bank[h][:, :], ACT.Copy)
                last.then_inc(b_aot, 1)

            with act.Fori(0, NB // 2) as n:
                for par in range(2):
                    act_back(2 * n + par, par)

        @block.tensor
        def _(pe):
            t = nc.tensor

            def turn(out_ap, in_ap, unit):
                return t.matmul(out_ap, in_ap, unit, start=True, stop=True, is_transpose=True)

            pe.wait_ge(consts2, 9 + 1 + 1 + E + 1)
            pe.wait_ge(const_dma, 16 * 5)

            def begin_chunk(n, par):
                c = 2 * n + par
                pe.wait_ge(xn_done, c + 1)
                pe.wait_ge(xt_ready, c + 1)
                for j in range(TPC):
                    for d in range(DC):
                        last = turn(bank[d][:, j * P:(j + 1) * P], xn[par][:, j, d * P:(d + 1) * P], ident[:, :])
                last.then_inc(turned, 1)

            def pe_chunk(n, par, begin_next):
                c = 2 * n + par
                pe.wait_ge(xt_ready, c + 2)
                pe.wait_ge(resid_done, 4 * c + 4)
                for w in range(4):
                    for d in range(DC):
                        last = t.matmul(bank[2 + w][:, :], wq_sb[:, d, w * P:(w + 1) * P], xt[par][:, d],
                                        start=d == 0, stop=d == DC - 1)
                    last.then_inc(qk_done, 1)
                begin_next()
                for j in range(TPC):
                    pe.wait_ge(v_free, 4 * c + j + 1)
                    for d in range(DC):
                        last = t.matmul(bank[6 + j % 2][:, 0:D + E], xt[par][:, d, j * P:(j + 1) * P],
                                        wq_sb[:, d, 2 * D:], start=d == 0, stop=d == DC - 1)
                    last.then_inc(v_done, 1)

            chunks(pe, begin_chunk, pe_chunk)

            def count(k, unit, source, tile, first, start=False):
                hot = r_hotb[:, source, tile:tile + 1, :].broadcast_to([P, NT - first, E])
                return t.matmul(bank[k][:, first * E:NT * E].rearrange("p (i e) -> p i e", e=E), unit[:, :], hot,
                                start=start, stop=False, skip_group_check=True)

            for k in range(TOPK):
                pe.wait_ge(rt_hot, k + 1)
                last = t.matmul(bank[k][:, 0:NT * E], tri[:, :], r_hotb[:, k].rearrange("p i e -> p (i e)"),
                                start=k == 0, stop=False, skip_group_check=True)
                for i in range(NT - 1):
                    last = count(k, onesb, k, i, i + 1)
                if k == 0:
                    for i in range(NT):
                        count(1, onesb, 0, i, 0, start=i == 0)
            last.then_inc(rt_pe, 1)
            pe.wait_ge(rt_dve, 18)

            def take_bank(key, plan, nth):
                before = plan.before[key]
                if before is not None:
                    by_kind[before[0]].reach(nth * N_KIND[before[0]] + before[1] + 1)
                elif nth > 0:
                    for kind, at in LAST_USERS[plan.bank[key]].items():
                        by_kind[kind].reach((nth - 1) * N_KIND[kind] + at + 1)
                return bank[plan.bank[key]]

            def pe_round(r, half, nth, plan):
                par = nth % 2
                pe.wait_ge(qk_load[par], 192 * (half + 1))
                q, k_ = q_op[par], k_op[par]
                for x in plan.steps:
                    kind = x[0]
                    if kind == "M":
                        _, h, i, j = x
                        diag = j == i // TPC
                        w = (i % TPC + 1) * P if diag else CH
                        o = take_bank(x, plan, nth)
                        last = t.matmul(o[:, 0:w], q[0:ROWS, h, i * P:(i + 1) * P], k_[0:ROWS, h, j * CH:j * CH + w],
                                        start=True, stop=True)
                        if diag:
                            last = t.matmul(o[:, w - P:w], identb[:, :], mask_m[:, :], start=False, stop=True,
                                            skip_group_check=True)
                        last.then_inc(m_ready, 1)
                    elif kind == "R":
                        c = x[1]
                        maxima.reach(nth * NC + c + 1)
                        row_uses.reach(nth * N_ROW + plan.row_at[x] + 1)
                        turn(row_b16[0:16, 0:P], negb[:, c % 2].rearrange("p s n -> p (s n)"),
                                    identb[:, :]).then_inc(row_done, 1)
                    elif kind == "S":
                        _, c, h, b = x
                        k = S_AT[x]
                        off = max(0, b - TPC * c) * P
                        diag = b >= TPC * c
                        if b == 0 and h == 0:
                            row_loads[c % 2].reach(64 * (nth * (NC // 2) + c // 2 + 2))
                        o = take_bank(x, plan, nth)
                        last = t.matmul(o[:, 0:CH - off], k_[0:AUG, h, b * P:(b + 1) * P],
                                        q[0:AUG, h, c * CH + off:(c + 1) * CH], start=True, stop=True)
                        if diag:
                            last = t.matmul(o[:, 0:P], identb[:, :], mask_s[:, :], start=False, stop=True,
                                            skip_group_check=True)
                        last.then_inc(s_ready, 1)
                    elif kind == "V":
                        _, c, grp, final = x
                        k = V_AT[x]
                        if grp == 0:
                            o_taken.reach(nth * NC + c + 1)
                        exps.reach(nth * N_S + GROUP * (k + 1))
                        if grp == 0 and c == 0:
                            pe.wait_ge(v_ready, r + 1)
                            for h in range(2):
                                t.matmul(v_bank[VW * (2 * h + 1):VW * (2 * h + 2), 0:P], v_op[:, 1, h, :], zeros[:, :],
                                         start=True, stop=False, skip_group_check=True)
                        for b2_ in range(2):
                            for h in range(2):
                                b = 2 * grp + b2_
                                slot = (k * GROUP + 2 * b2_ + h) % P_SLOTS
                                off = max(0, b - TPC * c) * P
                                quad = 2 * h + b2_
                                last = t.matmul(v_bank[VW * quad:VW * (quad + 1), off:], v_op[:, b, h, :],
                                                prob[:, slot, off:], start=grp == 0 and not (c == 0 and b2_ == 1),
                                                stop=final, skip_group_check=True)
                        last.then_inc(pv_done, 1)
                    elif kind == "O":
                        c = x[1]
                        o_copies.reach(1 + nth * NC + c + 1)
                        row_uses.reach(nth * N_ROW + plan.row_at[x] + 1)
                        for j in range(TPC):
                            last = t.matmul(row_bank[:, j * 2 * OW:(j + 1) * 2 * OW], o_sb[:, c % 2, j * P:(j + 1) * P], pick[:, :],
                                     start=True, stop=True)
                        last.then_inc(o_used, 1)
                    elif kind == "X":
                        f = x[1]
                        slabs.reach(32 * (nth * SLABS + f + 1))
                        o = take_bank(x, plan, nth)
                        for j in range(SLAB_T):
                            for d in range(DC):
                                a = (d * SLAB_T + j) * P
                                last = turn(o[:, a:a + P], slab_x[:, j, d * P:(d + 1) * P], ident[:, :])
                        last.then_inc(f_ready, 1)
                    elif kind == "H":
                        _, f, u, q4 = x
                        if q4 == 0:
                            take_bank(x[:3], plan, nth)
                            if f == 0 and u == 0:
                                pe.wait_ge(w_load[par], 64 * (half + 1))
                            if u == 0:
                                by_kind["A"].reach(nth * N_KIND["A"] + A_AT[("X", f)] + 1)
                        v, d = q4 // 2, q4 % 2
                        last = t.matmul(bank[plan.bank[x[:3]]][:, v * D:(v + 1) * D],
                                        w1_sb[par][:, d, (2 * u + v) * P:(2 * u + v + 1) * P], slab_xt[:, d],
                                        start=d == 0, stop=d == 1, skip_group_check=True)
                        if q4 == 3:
                            last.then_inc(f_ready, 1)
                    elif kind == "Y":
                        _, f, s16 = x
                        buf = (nth * SLABS + f) % 2
                        j, c8 = s16 // HC, s16 % HC
                        if s16 == 0:
                            take_bank(x[:2], plan, nth)
                            hids.reach(2 + nth * N_H + HIDDEN_AT[("H", f, HC // 2 - 1)] + 1)
                        last = t.matmul(bank[plan.bank[x[:2]]][:, j * D:(j + 1) * D], hid[buf][:, c8, j * P:(j + 1) * P],
                                        w2_sb[par][:, c8, :], start=c8 == 0, stop=c8 == HC - 1, skip_group_check=True)
                        if s16 == 15:
                            last.then_inc(f_ready, 1)
                pe.wait_ge(o_used, 2 + r * NC + NC)
                pe.wait_ge(f_ready, r * N_F + N_F)
                pe.sem_inc(round_done, 1)

            pe.sem_inc(pv_done, P_SLOTS // GROUP)
            pe.sem_inc(o_used, 2)
            pe.sem_inc(round_done, 1)
            pe.wait_ge(rounds_ready, 1)
            exps = Waits(pe, s_done, N_S)
            by_kind = {"M": Waits(pe, m_free, N_M), "S": exps, "A": Waits(pe, f_act, N_KIND["A"]), "D": Waits(pe, f_dve, SLABS)}
            maxima = Waits(pe, negb_done, NC)
            row_uses = Waits(pe, row_free, N_ROW)
            row_loads = [Waits(pe, row_dma[i], 32 * NC, 64) for i in range(2)]
            o_taken = Waits(pe, o_ready, NC)
            o_copies = Waits(pe, o_ready, NC, 1)
            slabs = Waits(pe, slab_dma, 32 * SLABS)
            hids = Waits(pe, hid_done, N_H, 2)
            rounds(pe, pe_round, (*by_kind.values(), maxima, row_uses, *row_loads, o_taken, o_copies, slabs, hids))

            pe.sem_inc(b_proj, 2)
            pe.wait_ge(m_free, ROUNDS * N_M)
            pe.wait_ge(s_done, ROUNDS * N_S)
            pe.wait_ge(f_act, ROUNDS * N_KIND["A"])
            pe.wait_ge(f_dve, ROUNDS * SLABS)
            def pe_back(i, n, par):
                pe.wait_ge(b_load[par], 48 * (n + 1))
                pe.wait_ge(b_aot, i + 1)
                for j in range(BT):
                    for d in range(DC):
                        a = (j * DC + d) % (CH // P) * P
                        last = turn(bank[j * D // CH][:, a:a + P], bao[par][:, j, d * P:(d + 1) * P], ident[:, :])
                last.then_inc(b_turn, 1)
                pe.wait_ge(b_out, i + 1)
                for h in range(2):
                    t.matmul(bank[2 + 2 * par + h][:, :], ident[:, :],
                             bx[par][:, h * BT // 2:(h + 1) * BT // 2].rearrange("p j d -> p (j d)"),
                             start=True, stop=False, skip_group_check=True)
                for j in range(BT):
                    o = bank[2 + 2 * par + j * D // CH][:, j * D % CH:j * D % CH + D]
                    t.matmul(o, ones_row[:, :], bet[0:1, :], start=False, stop=False, skip_group_check=True)
                pe.wait_ge(b_aot, i + 2)
                for j in range(BT):
                    o = bank[2 + 2 * par + j * D // CH][:, j * D % CH:j * D % CH + D]
                    for d in range(DC):
                        last = t.matmul(o, baot[par][:, j, d * P:(d + 1) * P], wo_sb[:, d], start=False, stop=d == 1,
                                        skip_group_check=True)
                last.then_inc(b_proj, 1)

            with pe.Fori(0, NB // 2) as n:
                for par in range(2):
                    pe_back(2 * n + par, n, par)

        @block.vector
        def _(dve):
            v = nc.vector
            for i in range(2):
                dve.sem_inc(row_dma[i], 64)
                dve.sem_inc(ao_store[i], 16)
                dve.sem_inc(y_store[i], 16)
                dve.sem_inc(xn_store[i], 16)
                dve.sem_inc(b_store[i], 16)
            dve.sem_inc(resid_done, 4)
            dve.sem_inc(b_out, 1)
            dve.sem_inc(row_free, 1)
            v.memset(part[:, :, :, :], 0.0).then_inc(neg_done, 1)

            def begin_chunk(n, par):
                c = 2 * n + par
                dve.wait_ge(x_dma[par], 16 * (n + 1))
                for j in range(TPC):
                    last = v.bn_stats(stats[:, par, j, :], x_in[par][:, j, :])
                last.then_inc(stat_done, 1)
                dve.wait_ge(stat_done, 2 * c + 1)
                dve.sem_inc(idle, 1)
                for j in range(TPC):
                    last = v.bn_aggr(mean_var[:, par, j, :], stats[:, par, j, :])
                last.then_inc(stat_done, 1)
                dve.wait_ge(rstd_done, 2 * c + 2)
                dve.wait_ge(xn_store[par], 16 * n + 16)
                for j in range(TPC):
                    last = v.tensor_scalar(xn[par][:, j, :], x_in[par][:, j, :], mean_var[:, par, j, 0:1],
                                           rstd[:, par, j:j + 1], ALU.subtract, ALU.mult)
                last.then_inc(xn_done, 1)

            def dve_chunk(n, par, begin_next):
                c = 2 * n + par
                begin_next()
                for w in range(4):
                    dve.wait_ge(part1, 4 * c + w + 1)
                    dve.wait_ge(split_done, 4 * c + 4)
                    v.scalar_tensor_tensor(resid[:, w], bank[2 + w][:, :], DH ** -0.5 if w < 2 else 1.0,
                                           split[par][:, 0, w], ALU.mult, ALU.subtract).then_inc(resid_done, 1)

            chunks(dve, begin_chunk, dve_chunk)

            for i in range(2):
                dve.wait_ge(xn_store[i], 16 * (NC // 2 + 1))
            dve.wait_ge(turned, NC)
            dve.wait_ge(v_free, 2 + NT)
            dve.wait_ge(consts2, 9 + 1 + 1 + E + 1)
            steps = [0]

            def chain(ins):
                steps[0] += 1
                ins.then_inc(rt_dve, 1)
                dve.wait_ge(rt_dve, steps[0])

            def over_e(a):
                return a.unsqueeze(2).broadcast_to([P, NT, E])

            down_b = down[:, :].unsqueeze(1).broadcast_to([P, NT, E])
            chain(v.tensor_reduce(r_one[0], logits[:, :, :], AX.X, ALU.max))
            chain(v.tensor_tensor(r_tmp, logits[:, :, :], over_e(r_one[0]), ALU.subtract))
            dve.wait_ge(rt_act, 1)
            chain(v.tensor_reduce(r_one[1], r_exp, AX.X, ALU.add))
            chain(v.reciprocal(r_one[2], r_one[1]))
            chain(v.tensor_tensor(r_score, r_exp, over_e(r_one[2]), ALU.mult))
            best, index = r_small[0], r_small[1]
            for k in range(TOPK):
                src = r_score
                chain(v.tensor_reduce(best[:, k], src, AX.X, ALU.max))
                chain(v.tensor_tensor(r_tmp, src, over_e(best[:, k]), ALU.is_equal))
                chain(v.tensor_tensor(r_tmp, r_tmp, down_b, ALU.mult))
                chain(v.tensor_reduce(index[:, k], r_tmp, AX.X, ALU.max))
                chain(v.tensor_tensor(r_hot[:, k], down_b, over_e(index[:, k]), ALU.is_equal))
                v.tensor_copy(r_hotb[:, k], r_hot[:, k]).then_inc(rt_hot, 1)
                if k == 0:
                    chain(v.scalar_tensor_tensor(r_score.rearrange("p i e -> p (i e)"),
                                                 r_hot[:, 0].rearrange("p i e -> p (i e)"), -2.0,
                                                 r_score.rearrange("p i e -> p (i e)"), ALU.mult, ALU.add))
            dve.wait_ge(rt_pe, 1)
            for k in range(TOPK):
                chain(v.tensor_tensor(r_own[:, k], bank[k][:, 0:NT * E].rearrange("p (i e) -> p i e", e=E), r_hot[:, k], ALU.mult))
            assert steps[0] == 18
            loc, keep, flatpos = r_small[2], r_small[3], r_small[4]
            for k in range(TOPK):
                last = v.tensor_reduce(loc[:, k], r_own[:, k], AX.X, ALU.add)
            chain(last)
            chain(v.tensor_scalar(keep, loc, float(CAP), None, ALU.is_le))
            chain(v.tensor_scalar(flatpos, index, -float(CAP), -1.0, ALU.mult, ALU.add))
            chain(v.tensor_tensor(flatpos, flatpos, loc, ALU.add))
            chain(v.tensor_tensor(flatpos, flatpos, keep, ALU.mult))
            chain(v.tensor_scalar(flatpos, flatpos, float(E * CAP), None, ALU.add))
            chain(v.tensor_copy(pos[:, :, :], flatpos))
            chain(v.tensor_tensor(r_one[0], best[:, 0], best[:, 1], ALU.add))
            chain(v.tensor_scalar(r_one[1], r_one[0], GATE_EPS, None, ALU.max))
            chain(v.reciprocal(r_one[2], r_one[1]))
            chain(v.tensor_tensor(r_small[5], best, r_one[2].unsqueeze(1).broadcast_to([P, TOPK, NT]), ALU.mult))
            v.tensor_tensor(gate[:, :, :], r_small[5], keep, ALU.mult).then_inc(pos_ready, 1)


            def dve_round(r, half, nth, plan):
                par = nth % 2
                for x in plan.steps:
                    kind = x[0]
                    if kind == "M":
                        _, h, i, j = x
                        k = M_AT[x]
                        w = (i % TPC + 1) * P if j == i // TPC else CH
                        scored.reach(nth * N_M + k + 1)
                        v.tensor_reduce(part[:, h, i, j:j + 1], bank[plan.bank[x]][:, 0:w], AX.X, ALU.max).then_inc(m_free, 1)
                    elif kind == "N":
                        c = x[1]
                        last_m = ("M", 1, TPC * c + TPC - 1, c)
                        pieces.reach(nth * N_M + M_AT[last_m] + 1)
                        b = c % 2
                        v.tensor_reduce(neg[:, b].rearrange("p (h i) -> p h i", h=2),
                                        part[:, :, TPC * c:TPC * c + TPC, 0:c + 1], AX.X, ALU.max,
                                        negate=True).then_inc(neg_done, 1)
                        negs.reach(1 + 2 * (nth * NC + c) + 1)
                        v.tensor_copy(negb[:, b, 0], neg[:, b]).then_inc(neg_done, 1)
                        negs.reach(1 + 2 * (nth * NC + c) + 2)
                        v.tensor_tensor(negb[:, b, 1], neg[:, b], negb[:, b, 0], ALU.subtract).then_inc(negb_done, 1)
                    elif kind == "R":
                        c = x[1]
                        turned_rows.reach(nth * NC + c + 1)
                        row_loads[c % 2].reach(64 * (nth * (NC // 2) + c // 2 + 1))
                        v.tensor_copy(rows[:, c % 2, :], row_b16[0:16, 0:P]).then_inc(row_free, 1)
                    elif kind == "O":
                        c = x[1]
                        b = c % 2
                        o = row_bank[:, 0:TPC * 2 * OW].rearrange("p (j h w) -> p j h w", j=TPC, h=2)
                        outputs.reach(2 + nth * NC + c + 1)
                        ao_stores[b].reach(16 * (nth * (NC // 2) + c // 2 + 1))
                        v.reciprocal(rden[:, b], o[:, :, :, DH]).then_inc(rden_done, 1)
                        rdens.reach(nth * NC + c + 1)
                        v.tensor_tensor(ao_sb[:, b].rearrange("p j (h d) -> p j h d", h=2), o[:, :, :, 0:DH],
                                        rden[:, b].unsqueeze(3).broadcast_to([P, TPC, 2, DH]), ALU.mult).then_inc(row_free, 1)
                    elif kind == "H" and x[3] == 3:
                        _, f, u, _ = x
                        buf = (nth * SLABS + f) % 2
                        halves.reach(nth * N_KIND["A"] + A_AT[x[:3]] + 1)
                        z = hid[buf][:, 2 * u:2 * u + 2, :].rearrange("p c t -> p (c t)")
                        v.scalar_tensor_tensor(z, tanh[:, HIDDEN_AT[x[:3]] % 2], 1.0, z, ALU.add, ALU.mult).then_inc(hid_done, 1)
                    elif kind == "Y" and x[2] == 15:
                        f = x[1]
                        k = ITEM_AT[x[:2]]
                        buf = (nth * SLABS + f) % 2
                        items.reach(nth * N_F + k + 1)
                        y_stores[buf].reach(16 * ((nth * SLABS + f) // 2 + 1))
                        v.tensor_tensor(y_sb[:, buf], bank[plan.bank[x[:2]]][:, :].rearrange("p (j d) -> p j d", j=SLAB_T),
                                        b2_sb[par][:, :].unsqueeze(1).broadcast_to([P, SLAB_T, D]), ALU.add).then_inc(f_dve, 1)

            scored = Waits(dve, m_ready, N_M)
            pieces = Waits(dve, m_free, N_M)
            negs = Waits(dve, neg_done, 2 * NC, 1)
            turned_rows = Waits(dve, row_done, NC)
            row_loads = [Waits(dve, row_dma[i], 32 * NC, 64) for i in range(2)]
            outputs = Waits(dve, o_used, NC, 2)
            ao_stores = [Waits(dve, ao_store[i], 8 * NC, 16) for i in range(2)]
            rdens = Waits(dve, rden_done, NC)
            items = Waits(dve, f_ready, N_F)
            halves = Waits(dve, f_act, N_KIND["A"])
            y_stores = [Waits(dve, y_store[i], 16 * Y_STORES[i], 16, per_pass=16 * SLABS) for i in range(2)]
            rounds(dve, dve_round, (scored, pieces, negs, turned_rows, *row_loads, outputs, *ao_stores, rdens, items, halves, *y_stores))

            def dve_back(i, n, par):
                dve.wait_ge(b_load[par], 48 * (n + 1))
                dve.wait_ge(b_gather[par], 16 * TOPK * BT * (n + 1))
                dve.wait_ge(b_idx, 2 * i + 2)
                done = [B_DVE * i]

                def stage(op):
                    for j in range(BT):
                        last = op(j)
                    done[0] = done[0] + 1
                    last.then_inc(b_dve, 1)
                    dve.wait_ge(b_dve, done[0])

                stage(lambda j: v.scalar_tensor_tensor(bxn[par][:, j], g_row[par][:, 0, j], bgate[:, par, 0, j:j + 1],
                                                       bxn[par][:, j], ALU.mult, ALU.add))
                stage(lambda j: v.scalar_tensor_tensor(bres[par][:, j], g_row[par][:, 1, j], bgate[:, par, 1, j:j + 1],
                                                       bxn[par][:, j], ALU.mult, ALU.add))
                stage(lambda j: v.bn_stats(stats[:, par, j, :], bres[par][:, j]))
                dve.sem_inc(idle, 1)
                stage(lambda j: v.bn_aggr(mean_var[:, par, j, :], stats[:, par, j, :]))
                stage(lambda j: v.scalar_tensor_tensor(bxn[par][:, j], bres[par][:, j], mean_var[:, par, j, 0:1],
                                                       gam[:, :], ALU.subtract, ALU.mult))
                dve.wait_ge(b_rstd, 2 * i + 2)
                dve.wait_ge(b_proj, i + 3)
                dve.wait_ge(b_store[par], 16 * n + 16)
                for j in range(BT):
                    o = bank[2 + 2 * par + j * D // CH][:, j * D % CH:j * D % CH + D]
                    last = v.scalar_tensor_tensor(bout[par][:, j], bxn[par][:, j], rstd[:, par, j:j + 1], o,
                                                  ALU.mult, ALU.add)
                last.then_inc(b_out, 1)

            with dve.Fori(0, NB // 2) as n:
                for par in range(2):
                    dve_back(2 * n + par, n, par)


def kernel(**inputs):
    import numpy as np
    import concourse.bacc as bacc
    from concourse.bass_utils import run_bass_kernel_spmd

    a = {k: np.asarray(v) for k, v in inputs.items()}
    arrays = {
        "x": a["L0_attn_query"].reshape(T, D),
        "wqkv": a["L0_attn_in_proj_weight"].T,
        "wo": a["L0_attn_out_proj_weight"].T,
        "wg": a["L0_ffn_wg"],
        "w1": a["L0_ffn_fc1_w"].transpose(0, 2, 1),
        "b1": a["L0_ffn_fc1_b"].reshape(E, HC, P).transpose(2, 0, 1),
        "w2": a["L0_ffn_fc2_w"],
        "b2": a["L0_ffn_fc2_b"],
        "gamma": a["L0_ffn_ln_gamma"],
        "beta": a["L0_ffn_ln_beta"],
    }
    arrays = {k: np.ascontiguousarray(v) for k, v in arrays.items()}
    nc = bacc.Bacc("TRN2", target_bir_lowering=False, num_devices=1)
    args = {k: nc.dram_tensor(f"in_{k}", v.shape, mybir.dt.from_np(v.dtype), kind="ExternalInput").ap()
            for k, v in arrays.items()}
    out = nc.dram_tensor("out", (T, D), F32, kind="ExternalOutput").ap()
    build(nc, **args, out=out)
    r = run_bass_kernel_spmd(nc, [{f"in_{k}": v for k, v in arrays.items()}], core_ids=[0])
    return r.results[0]["out"].reshape(1, T, D)
```

```python
from contextlib import ExitStack

import concourse.bass as bass
from concourse import mybir

F32 = mybir.dt.float32
BF16 = mybir.dt.bfloat16
I32 = mybir.dt.int32
ACT = mybir.ActivationFunctionType
ALU = mybir.AluOpType
AX = mybir.AxisListType

P = 128
T, D = 4096, 256
NH, DH = 16, 16
E, HID, TOPK = 8, 1024, 2
CAP = TOPK * int(1.25 * ((T + E - 1) // E))
NT = T // P
DC = D // P
CH = 512
NC = T // CH
TPC = CH // P
ROUNDS = E
assert ROUNDS * 2 == NH
Q_PARTS = (0, 0, 1, 1, 0, 2)
K_PARTS = (0, 1, 0, 1, 2, 0)
ROWS = 6 * DH
AUG = ROWS + 2
LN_EPS = 1e-5
GATE_EPS = 1.1920929e-07
MASKED = -1e30
SLABS = 5
SLAB_T = CAP // P // SLABS
BT = TPC
NB = NT // BT
HC = HID // P
VW = 32
OW = DH + 1

LAST_PACE = 1.5
EARLY = 8
LOADS = 2
SCATTER_NS = 74e3
POOL = 6
M_MOST, S_MOST, F_MOST = 3, 5, 2
P_SLOTS, GROUP = 8, 4


def round_steps(experts_at=0.0, pace=None):
    experts = []
    for f in range(SLABS):
        if f == 0:
            experts += [("X", 0)] + [("H", 0, 0, s) for s in range(4)]
        for u in range(1, HC // 2):
            experts += [("H", f, u, s) for s in range(4)]
        if f + 1 < SLABS:
            experts += [("X", f + 1)] + [("H", f + 1, 0, s) for s in range(4)]
        experts += [("Y", f, s) for s in range(16)]

    maxima = []
    for c in range(NC):
        maxima += [("M", h, t, j) for t in range(TPC * c, TPC * c + TPC) for j in range(c + 1) for h in range(2)]
        maxima += [("N", c), ("R", c)]
    scored = [("S", c, h, 2 * g + b) for c in range(NC) for g in range(2 * c + 2) for b in range(2) for h in range(2)]
    sums = [("V", c, g, g == 2 * c + 1) for c in range(NC) for g in range(2 * c + 2)]

    hop, row_trip = HOP, ROW_TRIP
    pe = dve = act = 0.0
    m_free, s_free, f_free = [0.0] * M_MOST, [0.0] * S_MOST, [0.0] * F_MOST
    bank_free, bank_user = [0.0] * POOL, [None] * POOL
    bank_of, user_before = {}, {}
    slot_free, bank_v, row_use = [0.0] * (P_SLOTS // GROUP), 0.0, 0.0
    neg_at, rows_at, prob_at, done = {}, {}, {}, {}
    n_m = n_s = n_f = n_v = n_a = 0
    o_due = []
    out = []
    total = 1.1 * (sum(217 for _ in scored) * 2 + 900 * len(sums) + 430 * len(experts))
    spent = 0.0

    def width(x):
        if x[0] == "M":
            return (x[2] % TPC + 1) * P if x[3] == x[2] // TPC else CH
        return CH - max(0, x[3] - TPC * x[1]) * P

    def take_bank(x, user):
        b = min(range(POOL), key=lambda i: bank_free[i])
        bank_of[x], user_before[x] = b, bank_user[b]
        bank_user[b], bank_free[b] = user, float("inf")
        return b

    while maxima or scored or sums or experts or o_due:
        choice = []
        any_bank = min(bank_free)
        if maxima:
            x = maxima[0]
            if x[0] == "M":
                choice.append((max(m_free[n_m % M_MOST], any_bank), 2, "m", x))
            elif x[0] == "N":
                choice.append((0.0, -1, "m", x))
            else:
                choice.append((max(neg_at[x[1]], row_use), 0, "m", x))
        if scored:
            x = scored[0]
            ready = rows_at.get(x[1])
            ahead = n_m - n_s >= AHEAD * (x[1] + 1) + AHEAD_0 or maxima == []
            if ready is not None and ahead and n_s // GROUP - n_v < P_SLOTS // GROUP:
                choice.append((max(ready, s_free[n_s % S_MOST], any_bank), 1, "s", x))
        if sums and (n_v + 1) * GROUP <= n_s and not (sums[0][3] and o_due):
            x = sums[0]
            choice.append((max(prob_at[n_v], bank_v if x[2] == 0 else 0.0), 2.5, "v", x))
        if o_due:
            choice.append((max(o_due[0][0], row_use), 3.5, "o", o_due[0][1]))
        if experts:
            x = experts[0]
            at = experts_at
            if x[0] != "H" or x[3] == 0:
                if x[0] != "Y" or x[2] == 0:
                    at = max(at, f_free[n_f % F_MOST], any_bank)
            if x[0] == "H" and x[2] == 0 and x[3] == 0:
                at = max(at, done[("X", x[1])])
            if x[0] == "Y" and x[2] == 0:
                at = max(at, done[("H", x[1], HC // 2 - 1)])
            share = 1 - len(experts) / (SLABS * 33)
            choice.append((at, 0.4 if share < (pace or F_PACE) * (spent - experts_at) / (total - experts_at) else 3, "f", x))
        ready = [ch for ch in choice if ch[0] <= pe + 40]
        at, _, stream, x = min(ready, key=lambda ch: ch[1]) if ready else min(choice, key=lambda ch: ch[:2])
        pe = max(pe, at)
        out.append(x)
        cost = 0.0
        if stream == "m":
            maxima.pop(0)
            if x[0] == "M":
                w = width(x)
                b = take_bank(x, ("M", n_m))
                cost = w / 2.4 + 3 + (56 if x[3] == x[2] // TPC else 0)
                dve = max(dve, pe + cost + hop) + (w + 62) / 0.96
                m_free[n_m % M_MOST] = bank_free[b] = dve + hop
                n_m += 1
            elif x[0] == "N":
                dve += 700
                neg_at[x[1]] = dve + hop
            else:
                cost = 60
                dve = max(dve, pe + cost + hop) + 250
                row_use = dve + hop
                rows_at[x[1]] = dve + row_trip
        elif stream == "s":
            scored.pop(0)
            w = width(x)
            b = take_bank(x, ("S", n_s))
            cost = w / 2.4 + 3 + (56 if x[3] >= TPC * x[1] else 0)
            act = max(act, pe + cost + hop, slot_free[n_s // GROUP % (P_SLOTS // GROUP)]) + (w + 70) / 1.2
            s_free[n_s % S_MOST] = bank_free[b] = act + hop
            prob_at[n_s // GROUP] = act + hop
            n_s += 1
        elif stream == "v":
            sums.pop(0)
            cost = 930 if x[2] < 2 * x[1] else 850 if not x[3] else 500
            slot_free[n_v % (P_SLOTS // GROUP)] = pe + cost + hop
            n_v += 1
            if x[3]:
                act = max(act, pe + cost + hop) + 480
                bank_v = act + hop
                o_due.append((act + hop, ("O", x[1])))
        elif stream == "o":
            o_due.pop(0)
            cost = 430
            dve = max(dve, pe + cost + hop) + 900
            row_use = dve + hop
        else:
            experts.pop(0)
            cost = 430
            item = x[:3] if x[0] == "H" else x[:2]
            if x[0] == "X" or x[-1] == 0:
                user = ("D", x[1]) if x[0] == "Y" else ("A", n_a)
                n_a += x[0] != "Y"
                f_bank = take_bank(item, user)
            if x[0] == "X":
                act = max(act, pe + cost + hop) + 480
            elif x[0] == "H" and x[3] == 3:
                act = max(act, pe + cost + hop) + 4 * 358
                dve = max(dve, act + hop) + 610
            elif x[0] == "Y" and x[2] == 15:
                dve = max(dve, pe + cost + hop) + 600
            if x[0] == "X" or x[-1] == (3 if x[0] == "H" else 15):
                done[item] = (act if x[0] == "X" else dve) + hop
                f_free[n_f % F_MOST] = bank_free[f_bank] = (dve if x[0] == "Y" else act) + hop
                n_f += 1
        pe += cost
        spent += cost
    return out, bank_of, user_before


AHEAD, AHEAD_0, F_PACE, HOP, ROW_TRIP = 9, 8, 1.1, 190, 4500


class Plan:

    def __init__(self, experts_at=0.0, pace=None):
        self.steps, self.bank, self.before = round_steps(experts_at, pace)
        self.row_at = numbered(self.steps, "RO")


def numbered(steps, kinds):
    return {x: n for n, x in enumerate([x for x in steps if x[0] in kinds])}


FIRST, PLAN = Plan(experts_at=SCATTER_NS), Plan()
LAST = Plan(pace=LAST_PACE)
after = max(LAST.steps.index(x) for x in (("R", NC - 1), ("O", NC - 2), ("Y", SLABS - 1, 15))) + 1
GROUPS = [("T", 0), ("T", 1)] + [x for i in range(NB - 2) for x in (("T", i + 2), ("U", i))] + [("U", NB - 2), ("U", NB - 1)]
LAST.steps[after:after] = GROUPS[:EARLY]
LATE = []
for x in GROUPS[EARLY:]:
    LATE.append(x)
    if x[0] == "U":
        LATE.append(("F", sum(y[0] == "F" for y in LATE)))
LATE += [("F", i) for i in range(sum(y[0] == "F" for y in LATE), NB)]
M_AT, S_AT, V_AT = (numbered(PLAN.steps, k) for k in "MSV")
N_M, N_S, N_V, N_ROW = len(M_AT), len(S_AT), len(V_AT), len(PLAN.row_at)
ITEMS = [x[:3] if x[0] == "H" else x[:2] for x in PLAN.steps
         if x[0] == "X" or (x[0] in "HY" and x[-1] == 0)]
ITEM_AT = {x: n for n, x in enumerate(ITEMS)}
HIDDEN_AT = {x: n for n, x in enumerate([x for x in ITEMS if x[0] == "H"])}
N_F, N_H = len(ITEMS), len(HIDDEN_AT)
A_AT = {x: n for n, x in enumerate([x for x in ITEMS if x[0] in "XH"])}

N_KIND = {"M": N_M, "S": N_S, "A": len(A_AT), "D": SLABS}


def last_users():
    out = [{} for _ in range(POOL)]
    for plan in (FIRST, PLAN):
        used = {}
        for x in plan.steps:
            key = x[:3] if x[0] == "H" else x[:2] if x[0] == "Y" else x
            if key in plan.bank:
                kind = {"X": "A", "H": "A", "Y": "D"}.get(key[0], key[0])
                at = {"M": M_AT, "S": S_AT, "A": A_AT, "D": {("Y", f): f for f in range(SLABS)}}[kind][key]
                used[plan.bank[key]] = (kind, at)
        for b, (kind, at) in used.items():
            out[b][kind] = max(at, out[b].get(kind, 0))
    return out


LAST_USERS = last_users()
Y_STORES = (SLABS + 1) // 2, SLABS // 2


class Waits:

    def __init__(self, engine, sem, per_round, start=0, wait=None, per_pass=None):
        self.wait = wait or engine.wait_ge
        self.engine, self.sem, self.at = engine, sem, start
        self.base = start + per_round
        self.per_pass = per_pass or 2 * per_round
        self.reg = engine.alloc_register(f"{engine.engine.name}_{sem.name}_{start}_{engine.bass.next_id()}")
        engine.reg_mov(self.reg, start)
        self.waited = False

    def reach(self, value):
        if value > self.at or not self.waited:
            self.move(max(value, self.at))
            self.waited = True
            self.wait(self.sem, self.reg)

    def move(self, value):
        if value != self.at:
            assert value > self.at, (self.sem.name, value, self.at)
            self.engine.reg_add(self.reg, self.reg, value - self.at)
            self.at = value

    def begin_loop(self):
        self.move(self.base)
        self.waited = False

    def end_pass(self):
        self.move(self.base + self.per_pass)
        self.at = self.base
        self.waited = False


def rounds(engine, one, waits):
    one(0, 0, 0, FIRST)
    for w in waits:
        w.begin_loop()
    with engine.Fori(0, ROUNDS // 2 - 1) as n:
        one(2 * n + 1, n, 1, PLAN)
        one(2 * n + 2, n + 1, 2, PLAN)
        for w in waits:
            w.end_pass()
    one(ROUNDS - 1, ROUNDS // 2 - 1, 1, LAST)


def build(nc, x, wqkv, wo, wg, w1, b1, w2, b2, gamma, beta, out):
    with ExitStack() as ctx:
        def sb(name, shape, dt=F32):
            return ctx.enter_context(nc.sbuf_tensor(name, shape, dt))

        def dram(name, shape, dt=F32):
            return nc.dram_tensor(name, shape, dt, kind="Internal").ap()

        def sem(name):
            return ctx.enter_context(nc.semaphore(name))

        xn_d = dram("xn_d", (T, D))
        qk_d = dram("qk_d", (3, 2 * D, T), BF16)
        slot_d = dram("slot_d", (E * CAP, 1), I32)
        y_d = dram("y_d", (E * CAP + 1, D))
        ao_d = dram("ao_d", (T, D))

        keep = sb("keep", [P, NT * D + 2 * T])
        v_all = keep[:, 0:NT * D].rearrange("p (i d) -> p i d", i=NT)
        q_op0, k_op0 = (keep[:, NT * D + i * T:NT * D + (i + 1) * T].bitcast(BF16).rearrange("p (h t) -> p h t", h=2)
                        for i in range(2))
        rows_g = keep[:, :].rearrange("p (i k j d) -> p i k j d", i=NB, k=TOPK, j=BT)
        zone = sb("zone", [P, 16384])
        v_op = sb("v_op", [P, NT, 2, VW])
        w1_sb = [sb(f"w1_sb{i}", [P, DC, HID]) for i in range(2)]
        w2_sb = [sb(f"w2_sb{i}", [P, HC, D]) for i in range(2)]
        b1_sb = [sb(f"b1_sb{i}", [P, HC]) for i in range(2)]
        b1h_sb = [sb(f"b1h_sb{i}", [P, HC]) for i in range(2)]
        b2_sb = [sb(f"b2_sb{i}", [P, D]) for i in range(2)]
        slab_x = sb("slab_x", [P, SLAB_T, D])
        slab_xt = sb("slab_xt", [P, DC, SLAB_T * P])
        tanh = sb("tanh", [P, 2, CH])
        y_sb = sb("y_sb", [P, 2, SLAB_T, D])
        o_sb = sb("o_sb", [P, 2, CH])
        ao_sb = sb("ao_sb", [P, 2, TPC, 2 * DH])
        o_sum = sb("o_sum", [P, TPC, 2, OW])
        rden = sb("rden", [P, 2, TPC, 2])
        part = sb("part", [P, 2, NT, NC])
        neg = sb("neg", [P, 2, 8])
        negb = sb("negb", [P, 2, 2, 8], BF16)
        rows = sb("rows", [16, 2, P], BF16)
        wo_sb = sb("wo_sb", [P, DC, D])
        gam, bet = sb("gam", [P, D]), sb("bet", [P, D])
        ident, identb = sb("ident", [P, P]), sb("identb", [P, P], BF16)
        mask_m, mask_s = sb("mask_m", [P, P], BF16), sb("mask_s", [P, P], BF16)
        tri, onesb = sb("tri", [P, P], BF16), sb("onesb", [P, P], BF16)
        zeros = sb("zeros", [P, P])
        down = sb("down", [P, E])
        logits = sb("logits", [P, NT, E])
        gate = sb("gate", [P, TOPK, NT])
        pos = sb("pos", [P, TOPK, NT], I32)
        token = sb("token", [P, NT], I32)
        slot_tok = sb("slot_tok", [P, E + 1, CAP // P], I32)
        slot_cur = sb("slot_cur", [P, CAP // P], I32)
        stats = sb("stats", [P, 2, TPC, 6])
        mean_var = sb("mean_var", [P, 2, TPC, 2])
        rstd = sb("rstd", [P, 2, TPC])
        half = sb("half", [P, TPC])
        b_mean_var, b_dev = sb("b_mean_var", [P, NB, BT, 2]), sb("b_dev", [P, NB, BT])

        def view(a, n, dt=F32):
            v = zone[:, a:a + n]
            return v if dt == F32 else v.bitcast(dt)

        q_op = [q_op0[:, :, :], view(0, 4096, BF16).rearrange("p (h t) -> p h t", h=2)]
        k_op = [k_op0[:, :, :], view(4096, 4096, BF16).rearrange("p (h t) -> p h t", h=2)]
        prob = view(8192, P_SLOTS * CH).rearrange("p (s t) -> p s t", s=P_SLOTS)
        hid = [view(12288 + i * 2048, 2048).rearrange("p (c t) -> p c t", c=HC) for i in range(2)]
        x_in = [view(i * 1024, 1024).rearrange("p (j d) -> p j d", j=TPC) for i in range(2)]
        xn = [view(2048 + i * 1024, 1024).rearrange("p (j d) -> p j d", j=TPC) for i in range(2)]
        xt = [view(4096 + i * 1024, 1024).rearrange("p (c t) -> p c t", c=DC) for i in range(2)]
        resid = view(6144, 2048).rearrange("p (w t) -> p w t", w=4)
        split = [view(8192 + i * 3072, 3072, BF16).rearrange("p (s w t) -> p s w t", s=3, w=4)
                 for i in range(2)]
        wq_sb = view(14336, DC * (3 * D + E)).rearrange("p (c f) -> p c f", c=DC)
        r_score = view(0, 256).rearrange("p (i e) -> p i e", e=E)
        r_exp = view(256, 256).rearrange("p (i e) -> p i e", e=E)
        r_tmp = view(512, 256).rearrange("p (i e) -> p i e", e=E)
        r_hot = view(768, 512).rearrange("p (k i e) -> p k i e", k=TOPK, e=E)
        r_hotb = view(1280, 256, BF16).rearrange("p (k i e) -> p k i e", k=TOPK, e=E)
        r_own = view(3072, 512).rearrange("p (k i e) -> p k i e", k=TOPK, e=E)
        r_small = [view(3584 + i * 64, 64).rearrange("p (k i) -> p k i", k=TOPK) for i in range(6)]
        r_one = [view(3968 + i * 32, 32) for i in range(4)]
        baot, bout, bx, bao = (
            [view(a + i * BT * D, BT * D).rearrange("p (j d) -> p j d", j=BT) for i in range(2)]
            for a in (0, 2048, 12288, 14336))
        bxn = [w1_sb[0][:, i, :].rearrange("p (j d) -> p j d", j=BT) for i in range(2)]

        bank = [ctx.enter_context(nc.psum_tensor(f"bank{i}", [P, CH], F32)) for i in range(8)]
        v_bank, row_bank = bank[POOL], bank[POOL + 1]
        row_b16 = row_bank[:, :].bitcast(BF16)

        idle = sem("idle")
        consts, consts2, ones_done = sem("consts"), sem("consts2"), sem("ones_done")
        const_dma, x_dma = sem("const_dma"), [sem(f"x_dma{i}") for i in range(2)]
        stat_done, rstd_done, xn_done = sem("stat_done"), sem("rstd_done"), sem("xn_done")
        xn_store = [sem(f"xn_store{i}") for i in range(2)]
        turned, xt_ready, qk_done, part1, resid_done, split_done = (
            sem(n) for n in ("turned", "xt_ready", "qk_done", "part1", "resid_done", "split_done"))
        part2 = sem("part2")
        split_store = [sem(f"split_store{i}") for i in range(2)]
        v_done, v_free = sem("v_done"), sem("v_free")
        rt_dve, rt_act, rt_hot, rt_pe, pos_ready = (sem(n) for n in ("rt_dve", "rt_act", "rt_hot", "rt_pe", "pos_ready"))
        zero_dma, scatter, slot_load = sem("zero_dma"), sem("scatter"), sem("slot_load")
        rounds_ready = sem("rounds_ready")
        qk_load, w_load = [sem(f"qk_load{i}") for i in range(2)], [sem(f"w_load{i}") for i in range(2)]
        v_ready, b1h_ready, round_done = sem("v_ready"), sem("b1h_ready"), sem("round_done")
        m_ready, m_free, s_ready, s_done = sem("m_ready"), sem("m_free"), sem("s_ready"), sem("s_done")
        neg_done, negb_done = sem("neg_done"), sem("negb_done")
        row_done, row_free = sem("row_done"), sem("row_free")
        row_dma = [sem(f"row_dma{i}") for i in range(2)]
        pv_done, o_ready, o_used, rden_done = sem("pv_done"), sem("o_ready"), sem("o_used"), sem("rden_done")
        ao_store = [sem(f"ao_store{i}") for i in range(2)]
        idx_ready, slab_dma = sem("idx_ready"), sem("slab_dma")
        f_ready, hid_done = sem("f_ready"), sem("hid_done")
        f_act, f_dve = sem("f_act"), sem("f_dve")
        y_store = [sem(f"y_store{i}") for i in range(2)]
        b_load, b_gather = [sem(f"b_load{i}") for i in range(2)], [sem(f"b_gather{i}") for i in range(NB)]
        b_res, b_norm, b_beta, b_rstd, b_turn, b_aot, b_proj, b_out = (
            sem(n) for n in ("b_res", "b_norm", "b_beta", "b_rstd", "b_turn", "b_aot", "b_proj", "b_out"))
        b_xn = [sem(f"b_xn{i}") for i in range(2)]
        b_store = [sem(f"b_store{i}") for i in range(2)]

        x_t = x.rearrange("(i p) d -> p i d", p=P)
        xn_t = xn_d.rearrange("(i p) d -> p i d", p=P)
        ao_t = ao_d.rearrange("(i p) d -> p i d", p=P)
        out_t = out.rearrange("(i p) d -> p i d", p=P)
        slot_2d = slot_d.rearrange("(p j) o -> p (j o)", p=P)
        slot_t = slot_d.rearrange("(e p j) o -> p e (j o)", e=E, p=P)
        y_t = y_d[0:E * CAP, :].rearrange("(e p j) d -> e p j d", e=E, p=P)

        N_RES = 4

        def chunks(engine, begin, rest, between=None):
            begin(0, 0)
            if between:
                between()
            with engine.Fori(0, NC // 2 - 1) as n:
                rest(n, 0, lambda: begin(n, 1))
                rest(n, 1, lambda: begin(n + 1, 0))
            rest(NC // 2 - 1, 0, lambda: begin(NC // 2 - 1, 1))
            rest(NC // 2 - 1, 1, lambda: None)

        block = ctx.enter_context(nc.Block())

        @block.sync
        def _(sp):
            def load_x(c, par, before=None):
                if before is not None:
                    sp.wait_ge(xn_done, before)
                sp.dma_start(x_in[par], x_t[:, bass.ds(c * TPC, TPC), :]).then_inc(x_dma[par], 16)

            load_x(0, 0)
            sp.dma_start(wq_sb[:, :, 0:3 * D], wqkv.rearrange("(c p) f -> p c f", p=P)).then_inc(const_dma, 16)
            sp.dma_start(wq_sb[:, :, 3 * D:], wg.rearrange("(c p) f -> p c f", p=P)).then_inc(const_dma, 16)
            sp.dma_start(wo_sb[:, :, :], wo.rearrange("(c p) f -> p c f", p=P)).then_inc(const_dma, 16)
            sp.dma_start(gam[:, :], gamma.rearrange("(a d) -> a d", a=1).broadcast_to([P, D])).then_inc(const_dma, 16)
            sp.dma_start(bet[:, :], beta.rearrange("(a d) -> a d", a=1).broadcast_to([P, D])).then_inc(const_dma, 16)
            sp.wait_ge(consts, 1)
            sp.dma_start(slot_2d, zeros[:, 0:E * CAP // P].bitcast(I32)).then_inc(zero_dma, 16)
            sp.dma_start(y_d[E * CAP:, :].rearrange("a (b d) -> (a b) d", b=2), zeros[0:2, :]).then_inc(zero_dma, 16)

            def store_front(c, par):
                sp.wait_ge(xn_done, c + 1)
                sp.dma_start(xn_t[:, bass.ds(c * TPC, TPC), :], xn[par]).then_inc(xn_store[par], 16)
                sp.wait_ge(split_done, 4 * c + 8)
                for s in range(3):
                    sp.dma_start(qk_d[s].rearrange("(w p) t -> p w t", p=P)[:, :, bass.ds(c * CH, CH)],
                                 split[par][:, s]).then_inc(split_store[par], 16)

            load_x(1, 1)
            with sp.Fori(0, NC // 2 - 1) as n:
                for par in range(2):
                    load_x(2 * n + 2 + par, par, before=2 * n + par + 1)
                    store_front(2 * n + par, par)
            for par in range(2):
                store_front(NC - 2 + par, par)

            def loads(r, par):
                def load(dst, src, done):
                    return lambda: sp.dma_start(dst, src).then_inc(done, 16)

                out = []
                for g in range(6):
                    for op, parts, first in ((q_op, Q_PARTS, 0), (k_op, K_PARTS, D)):
                        src = qk_d[parts[g], bass.ds(r * 2 * DH + first, 2 * DH), :]
                        out.append(load(op[par][g * DH:(g + 1) * DH], src.rearrange("(h r) t -> r h t", h=2), qk_load[par]))
                for w, src in ((w1_sb, w1), (w2_sb, w2)):
                    out.append(load(w[par][:, :, :], src[bass.ds(r, 1)].rearrange("o (c p) f -> p (o c) f", p=P), w_load[par]))
                out.append(load(b1_sb[par][:, :], b1[:, bass.ds(r, 1), :].rearrange("p o c -> p (o c)"), w_load[par]))
                out.append(load(b2_sb[par][:, :], b2[bass.ds(r, 1), :].broadcast_to([P, D]), w_load[par]))
                return out

            def load_xn(i):
                sp.dma_start(bxn[i % 2], xn_t[:, i * BT:(i + 1) * BT, :]).then_inc(b_xn[i % 2], 16)

            def reload_xn(i):
                if i + 2 < NB:
                    sp.wait_ge(b_res, N_RES * (i + 1))
                    load_xn(i + 2)

            def load_ao(i):
                sp.wait_ge(ao_store[i % 2], 16 * ((ROUNDS - 1) * NC // 2 + i // 2 + 2))
                for dst, src in ((bao, ao_t), (bx, x_t)):
                    sp.dma_start(dst[i % 2], src[:, i * BT:(i + 1) * BT, :]).then_inc(b_load[i % 2], 16)

            def sp_round(r, half, nth, plan):
                par = nth % 2
                last = plan is LAST
                due = [] if last else loads(r + 1, 1 - par)
                sp.wait_ge(round_done, r + 1)
                if nth > 0:
                    sp.sem_inc(idle, 1)
                    sp.wait_ge(f_dve, r * SLABS)
                sp.sem_inc(idle, 1)
                if last:
                    for i in range(2):
                        load_xn(i)
                for x in plan.steps:
                    if x == ("T", 0):
                        sp.wait_ge(f_dve, ROUNDS * SLABS)
                        load_ao(0)
                        load_ao(1)
                    if x[0] == "T":
                        reload_xn(x[1])
                    if x[0] == "R":
                        c = x[1]
                        rows_out.reach(1 + nth * N_ROW + plan.row_at[x] + 1)
                        for s in range(2):
                            for h in range(2):
                                a = 8 * s + TPC * h
                                sp.dma_start(q_op[par][ROWS + s:ROWS + s + 1, h, c * CH:(c + 1) * CH]
                                             .rearrange("o (t q) -> o t q", t=TPC),
                                             rows[a:a + TPC, c % 2, :]).then_inc(row_dma[c % 2], 16)
                    elif x[0] == "O":
                        c = x[1]
                        rows_out.reach(1 + nth * N_ROW + plan.row_at[x] + 1)
                        sp.sem_inc(idle, 1)
                        sp.dma_start(ao_t[:, c * TPC:(c + 1) * TPC, bass.ds(r * 2 * DH, 2 * DH)],
                                     ao_sb[:, c % 2]).then_inc(ao_store[c % 2], 16)
                    elif x[0] == "Y" and x[2] == 15:
                        f = x[1]
                        buf = (nth * SLABS + f) % 2
                        slabs_out.reach(nth * SLABS + f + 1)
                        sp.sem_inc(idle, 1)
                        sp.dma_start(y_t[bass.ds(r, 1), :, f * SLAB_T:(f + 1) * SLAB_T, :].rearrange("o p j d -> (o p) j d"),
                                     y_sb[:, buf]).then_inc(y_store[buf], 16)
                    if x[0] in "RO":
                        for load in due[:LOADS]:
                            load()
                        due = due[LOADS:]

            for i in range(2):
                sp.wait_ge(split_store[i], 48 * (NC // 2 + 1))
            for load in loads(0, 0):
                load()
            for i in range(2):
                sp.wait_ge(xn_store[i], 16 * (NC // 2 + 1))
            sp.wait_ge(rounds_ready, 1)
            sp.wait_ge(pos_ready, 1)
            rows_out = Waits(sp, row_free, N_ROW, 1)
            slabs_out = Waits(sp, f_dve, SLABS)
            rounds(sp, sp_round, (rows_out, slabs_out))

            def store_back(i, par):
                sp.wait_ge(b_out, i + 2)
                sp.dma_start(out_t[:, i * BT:(i + 1) * BT, :], bout[par]).then_inc(b_store[par], 16)

            for x in LATE:
                if x[0] == "T":
                    reload_xn(x[1])
                elif x[0] == "F":
                    store_back(x[1], x[1] % 2)
                    if x[1] + 2 < NB:
                        load_ao(x[1] + 2)
            for i in range(2):
                sp.wait_ge(b_store[i], 16 * (NB // 2 + 1))

        @block.gpsimd
        def _(pool):
            g = nc.gpsimd
            def wait(sem, value):
                pool.wait_ge(sem, value)
                if not isinstance(value, int):
                    pool.sem_inc(idle, 1)

            g.memset(zeros[:, :], 0.0).then_inc(consts, 1)
            g.memset(ident[:, :], 0.0).then_inc(consts, 1)
            g.memset(identb[:, :], 0.0).then_inc(consts, 1)
            g.memset(mask_m[:, :], 0.0).then_inc(consts, 1)
            g.memset(mask_s[:, :], 0.0).then_inc(consts, 1)
            g.memset(onesb[:, :], 1.0).then_inc(consts, 1)
            g.memset(tri[:, :], 1.0).then_inc(consts, 1)
            g.memset(v_op[:, :, :, :], 0.0).then_inc(consts, 1)
            g.memset(slot_tok[:, :, :], 0).then_inc(consts, 1)
            g.memset(half[:, :], -0.5).then_inc(consts, 1)
            wait(consts, 10)
            for m in (ident, identb):
                g.affine_select(out=m[:, :], in_=m[:, :], compare_op=ALU.not_equal, fill=1.0, base=0,
                                pattern=[[-1, P]], channel_multiplier=1).then_inc(consts2, 1)
            g.affine_select(out=mask_m[:, :], in_=mask_m[:, :], compare_op=ALU.is_ge, fill=MASKED, base=0,
                            pattern=[[-1, P]], channel_multiplier=1).then_inc(consts2, 1)
            g.affine_select(out=mask_s[:, :], in_=mask_s[:, :], compare_op=ALU.is_ge, fill=MASKED, base=0,
                            pattern=[[1, P]], channel_multiplier=-1).then_inc(consts2, 1)
            g.affine_select(out=tri[:, :], in_=tri[:, :], compare_op=ALU.is_ge, fill=0.0, base=0,
                            pattern=[[1, P]], channel_multiplier=-1).then_inc(consts2, 1)
            g.memset(v_op[:, :, :, DH:DH + 1], 1.0).then_inc(consts2, 1)
            g.iota(token[:, :], pattern=[[P, NT]], base=0, channel_multiplier=1).then_inc(consts2, 1)
            for i in range(E):
                g.memset(down[:, i:i + 1], float(E - i)).then_inc(consts2, 1)
            wait(consts2, 5 + 1 + 1 + E)

            pool.sem_inc(split_done, 4)
            def begin_chunk(n, par):
                c = 2 * n + par
                wait(stat_done, 2 * c + 2)
                g.tensor_scalar(rstd[:, par, :], mean_var[:, par, :, 1], LN_EPS, None, ALU.add).then_inc(rstd_done, 1)
                wait(rstd_done, 2 * c + 1)
                g.tensor_tensor(rstd[:, par, :], rstd[:, par, :], half[:, :], ALU.pow).then_inc(rstd_done, 1)

            def split_chunk(n, par, begin_next):
                c = 2 * n + par
                begin_next()
                for w in range(4):
                    wait(part2, 4 * c + w + 1)
                    g.tensor_tensor(split[par][:, 2, w], resid[:, w], split[par][:, 1, w],
                                    ALU.subtract).then_inc(split_done, 1)

            def ones_rows():
                wait(rstd_done, 2)
                g.memset(k_op0[ROWS:ROWS + 2, :, :], 1.0).then_inc(ones_done, 1)
                wait(ones_done, 1)

            chunks(pool, begin_chunk, split_chunk, between=ones_rows)

            def v_operand(r):
                wait(round_done, r + 1)
                g.tensor_copy(v_op[:, :, :, 0:DH], v_all[:, :, bass.ds(r * 2 * DH, 2 * DH)]
                              .rearrange("p i (h d) -> p i h d", h=2)).then_inc(v_ready, 1)

            def half_bias(half, par):
                wait(w_load[par], 64 * (half + 1))
                g.tensor_scalar(b1h_sb[par][:, :], b1_sb[par][:, :], 0.5, None, ALU.mult).then_inc(b1h_ready, 1)

            wait(v_free, 2 + NT)
            wait(split_done, 4 + 4 * NC)
            g.memset(k_op[1][ROWS:ROWS + 2, :, :], 1.0).then_inc(rounds_ready, 1)
            wait(rounds_ready, 1)
            v_operand(0)

            wait(pos_ready, 1)
            wait(zero_dma, 32)
            for k in range(TOPK):
                for i in range(NT):
                    g.indirect_dma_start(out=slot_d, out_offset=bass.IndirectOffsetOnAxis(ap=pos[:, k, i:i + 1], axis=0),
                                         in_=token[:, i:i + 1], in_offset=None,
                                         bounds_check=E * CAP - 1, oob_is_err=False).then_inc(scatter, 16)
            wait(scatter, 16 * TOPK * NT)
            pool.dma_start(slot_tok[:, 0:E, :], slot_t).then_inc(slot_load, 16)
            wait(slot_load, 16)
            for i in range(2):
                wait(xn_store[i], 16 * (NC // 2 + 1))
            half_bias(0, 0)

            def gather(e, f, first):
                if first:
                    g.tensor_copy(slot_cur[:, :], slot_tok[:, bass.ds(e, 1), :].rearrange("p o j -> p (o j)")).then_inc(idx_ready, 1)
                    wait(idx_ready, e + 1)
                for j in range(SLAB_T):
                    g.indirect_dma_start(out=slab_x[:, j, :], out_offset=None, in_=xn_d,
                                         in_offset=bass.IndirectOffsetOnAxis(
                                             ap=slot_cur[:, f * SLAB_T + j:f * SLAB_T + j + 1], axis=0)
                                         ).then_inc(slab_dma, 16)

            def pool_round(r, half, nth, plan):
                par = nth % 2
                if nth > 0:
                    v_operand(r)
                    half_bias(half, par)
                for x in plan.steps:
                    if x[0] == "X":
                        f = x[1]
                        turned_slabs.reach(nth * N_F + ITEM_AT[x] + 1)
                        if f + 1 < SLABS:
                            gather(r, f + 1, False)
                        else:
                            slabs_in.reach(32 * (nth * SLABS + SLABS))
                            gather(r + 1, 0, True)

            gather(0, 0, True)
            turned_slabs = Waits(pool, f_ready, N_F, wait=wait)
            slabs_in = Waits(pool, slab_dma, 32 * SLABS, wait=wait)
            rounds(pool, pool_round, (turned_slabs, slabs_in))

            wait(slab_dma, 32 * (ROUNDS * SLABS + 1))
            for i in range(2):
                wait(y_store[i], 16 * (ROUNDS * SLABS // 2 + 1))
            wait(v_ready, ROUNDS)

            def pool_gather(i):
                for j in range(BT):
                    for k in range(TOPK):
                        g.indirect_dma_start(out=rows_g[:, i, k, j], out_offset=None, in_=y_d,
                                             in_offset=bass.IndirectOffsetOnAxis(ap=pos[:, k, i * BT + j:i * BT + j + 1], axis=0)
                                             ).then_inc(b_gather[i], 16)

            def pool_rstd(i):
                wait(b_res, N_RES * i + N_RES)
                g.tensor_scalar(b_dev[:, i], b_mean_var[:, i, :, 1], LN_EPS, None, ALU.add).then_inc(b_rstd, 1)
                wait(b_rstd, 2 * i + 1)
                g.tensor_tensor(b_dev[:, i], b_dev[:, i], half[:, :], ALU.pow).then_inc(b_rstd, 1)

            def add_beta(i):
                wait(b_load[i % 2], 32 * (i // 2 + 1))
                g.tensor_tensor(bx[i % 2], bx[i % 2], bet[:, :].unsqueeze(1).broadcast_to([P, BT, D]), ALU.add).then_inc(b_beta, 1)

            for i in range(NB):
                pool_gather(i)
            add_beta(0)
            add_beta(1)
            for i in range(NB):
                pool_rstd(i)
                if i >= 3:
                    add_beta(i - 1)
            add_beta(NB - 1)

        @block.scalar
        def _(act):
            s = nc.scalar
            act.sem_inc(v_free, 2)
            act.sem_inc(xt_ready, 1)
            act.sem_inc(b_aot, 1)
            for i in range(2):
                act.sem_inc(split_store[i], 48)

            def begin_chunk(n, par):
                c = 2 * n + par
                act.wait_ge(turned, c + 1)
                for d in range(DC):
                    last = s.activation(xt[par][:, d], bank[d][:, :], ACT.Copy)
                last.then_inc(xt_ready, 1)

            def act_chunk(n, par, begin_next):
                c = 2 * n + par
                act.wait_ge(split_store[par], 48 * n + 48)
                for w in range(4):
                    act.wait_ge(qk_done, 4 * c + w + 1)
                    s.activation(split[par][:, 0, w], bank[2 + w][:, :], ACT.Copy,
                                 scale=DH ** -0.5 if w < 2 else 1.0).then_inc(part1, 1)
                begin_next()
                for j in range(TPC):
                    act.wait_ge(resid_done, 4 * c + j + 5)
                    s.activation(split[par][:, 1, j], resid[:, j], ACT.Copy).then_inc(part2, 1)
                    act.wait_ge(v_done, 4 * c + j + 1)
                    s.activation(v_all[:, bass.ds(c * TPC + j, 1), :].rearrange("p o d -> p (o d)"),
                                 bank[6 + j % 2][:, 0:D], ACT.Copy)
                    s.activation(logits[:, bass.ds(c * TPC + j, 1), :].rearrange("p o e -> p (o e)"),
                                 bank[6 + j % 2][:, D:D + E], ACT.Copy).then_inc(v_free, 1)

            chunks(act, begin_chunk, act_chunk)

            act.wait_ge(rt_dve, 2)
            s.activation(r_exp, r_tmp, ACT.Exp).then_inc(rt_act, 1)

            for i in range(2):
                act.wait_ge(split_store[i], 48 * (NC // 2 + 1))

            def act_round(r, half, nth, plan):
                par = nth % 2
                for x in plan.steps:
                    if x[0] == "S":
                        _, c, h, b = x
                        k = S_AT[x]
                        off = max(0, b - TPC * c) * P
                        scores.reach(nth * N_S + k + 1)
                        if k % GROUP == 0:
                            slots.reach(nth * N_V + k // GROUP + 1)
                        s.activation(prob[:, k % P_SLOTS, off:], bank[plan.bank[x]][:, 0:CH - off],
                                     ACT.Exp).then_inc(s_done, 1)
                    elif x[0] == "V" and x[3]:
                        c = x[1]
                        sums.reach(P_SLOTS // GROUP + nth * N_V + V_AT[x] + 1)
                        o_bufs.reach(nth * NC + c + 1)
                        s.activation(o_sb[:, c % 2], v_bank[:, :], ACT.Copy).then_inc(o_ready, 1)
                    elif x[0] == "H" and x[3] == 3:
                        _, f, u, _ = x
                        hidden.reach(nth * N_F + ITEM_AT[x[:3]] + 1)
                        z = bank[plan.bank[x[:3]]]
                        if f == 0 and u == 0:
                            act.wait_ge(b1h_ready, r + 1)
                        m = HIDDEN_AT[x[:3]]
                        tanhs.reach(nth * N_H + m + 1)
                        for v in range(2):
                            s.activation(hid[(nth * SLABS + f) % 2][:, 2 * u + v, :], z[:, v * D:(v + 1) * D],
                                         ACT.Identity, bias=b1h_sb[par][:, 2 * u + v:2 * u + v + 1], scale=0.5)
                        for v in range(2):
                            last = s.activation(tanh[:, m % 2, v * D:(v + 1) * D], z[:, v * D:(v + 1) * D],
                                                ACT.Tanh, bias=b1h_sb[par][:, 2 * u + v:2 * u + v + 1], scale=0.5)
                        last.then_inc(f_act, 1)
                    elif x[0] == "X":
                        hidden.reach(nth * N_F + ITEM_AT[x] + 1)
                        s.activation(slab_xt[:, :, :].rearrange("p c t -> p (c t)"), bank[plan.bank[x]][:, :],
                                     ACT.Copy).then_inc(f_act, 1)

            act.sem_inc(hid_done, 2)
            act.sem_inc(o_ready, 1)
            scores = Waits(act, s_ready, N_S)
            slots = Waits(act, pv_done, N_V)
            sums = Waits(act, pv_done, N_V, P_SLOTS // GROUP)
            o_bufs = Waits(act, o_used, NC)
            hidden = Waits(act, f_ready, N_F)
            tanhs = Waits(act, hid_done, N_H)
            rounds(act, act_round, (scores, slots, sums, o_bufs, hidden, tanhs))

            def act_back(i, par):
                act.wait_ge(b_turn, i + 1)
                act.wait_ge(b_proj, i + 1)
                for h in range(2):
                    last = s.activation(baot[par][:, h * BT // 2:(h + 1) * BT // 2].rearrange("p j d -> p (j d)"),
                                        bank[h][:, :], ACT.Copy)
                last.then_inc(b_aot, 1)

            with act.Fori(0, NB // 2) as n:
                for par in range(2):
                    act_back(2 * n + par, par)

        @block.tensor
        def _(pe):
            t = nc.tensor

            def turn(out_ap, in_ap, unit):
                return t.matmul(out_ap, in_ap, unit, start=True, stop=True, is_transpose=True)

            pe.wait_ge(consts2, 5 + 1 + 1 + E)
            pe.wait_ge(const_dma, 16 * 5)

            def begin_chunk(n, par):
                c = 2 * n + par
                pe.wait_ge(xn_done, c + 1)
                pe.wait_ge(xt_ready, c + 1)
                for j in range(TPC):
                    for d in range(DC):
                        last = turn(bank[d][:, j * P:(j + 1) * P], xn[par][:, j, d * P:(d + 1) * P], ident[:, :])
                last.then_inc(turned, 1)

            def pe_chunk(n, par, begin_next):
                c = 2 * n + par
                pe.wait_ge(xt_ready, c + 2)
                pe.wait_ge(resid_done, 4 * c + 4)
                for w in range(4):
                    for d in range(DC):
                        last = t.matmul(bank[2 + w][:, :], wq_sb[:, d, w * P:(w + 1) * P], xt[par][:, d],
                                        start=d == 0, stop=d == DC - 1)
                    last.then_inc(qk_done, 1)
                begin_next()
                for j in range(TPC):
                    pe.wait_ge(v_free, 4 * c + j + 1)
                    for d in range(DC):
                        last = t.matmul(bank[6 + j % 2][:, 0:D + E], xt[par][:, d, j * P:(j + 1) * P],
                                        wq_sb[:, d, 2 * D:], start=d == 0, stop=d == DC - 1)
                    last.then_inc(v_done, 1)

            chunks(pe, begin_chunk, pe_chunk)

            def count(k, unit, source, tile, first, start=False):
                hot = r_hotb[:, source, tile:tile + 1, :].broadcast_to([P, NT - first, E])
                return t.matmul(bank[k][:, first * E:NT * E].rearrange("p (i e) -> p i e", e=E), unit[:, :], hot,
                                start=start, stop=False, skip_group_check=True)

            for k in range(TOPK):
                pe.wait_ge(rt_hot, k + 1)
                last = t.matmul(bank[k][:, 0:NT * E], tri[:, :], r_hotb[:, k].rearrange("p i e -> p (i e)"),
                                start=k == 0, stop=False, skip_group_check=True)
                for i in range(NT - 1):
                    last = count(k, onesb, k, i, i + 1)
                if k == 0:
                    for i in range(NT):
                        count(1, onesb, 0, i, 0, start=i == 0)
            last.then_inc(rt_pe, 1)
            pe.wait_ge(rt_dve, 18)

            def take_bank(key, plan, nth):
                before = plan.before[key]
                if before is not None:
                    by_kind[before[0]].reach(nth * N_KIND[before[0]] + before[1] + 1)
                elif nth > 0:
                    for kind, at in LAST_USERS[plan.bank[key]].items():
                        by_kind[kind].reach((nth - 1) * N_KIND[kind] + at + 1)
                return bank[plan.bank[key]]

            def pe_round(r, half, nth, plan):
                par = nth % 2
                pe.wait_ge(qk_load[par], 192 * (half + 1))
                q, k_ = q_op[par], k_op[par]
                for x in plan.steps:
                    kind = x[0]
                    if kind == "M":
                        _, h, i, j = x
                        diag = j == i // TPC
                        w = (i % TPC + 1) * P if diag else CH
                        o = take_bank(x, plan, nth)
                        last = t.matmul(o[:, 0:w], q[0:ROWS, h, i * P:(i + 1) * P], k_[0:ROWS, h, j * CH:j * CH + w],
                                        start=True, stop=True)
                        if diag:
                            last = t.matmul(o[:, w - P:w], identb[:, :], mask_m[:, :], start=False, stop=True,
                                            skip_group_check=True)
                        last.then_inc(m_ready, 1)
                    elif kind == "R":
                        c = x[1]
                        maxima.reach(nth * NC + c + 1)
                        row_uses.reach(nth * N_ROW + plan.row_at[x] + 1)
                        turn(row_b16[0:16, 0:P], negb[:, c % 2].rearrange("p s n -> p (s n)"),
                                    identb[:, :]).then_inc(row_done, 1)
                    elif kind == "S":
                        _, c, h, b = x
                        k = S_AT[x]
                        off = max(0, b - TPC * c) * P
                        diag = b >= TPC * c
                        if b == 0 and h == 0:
                            row_loads[c % 2].reach(64 * (nth * (NC // 2) + c // 2 + 2))
                        o = take_bank(x, plan, nth)
                        last = t.matmul(o[:, 0:CH - off], k_[0:AUG, h, b * P:(b + 1) * P],
                                        q[0:AUG, h, c * CH + off:(c + 1) * CH], start=True, stop=True)
                        if diag:
                            last = t.matmul(o[:, 0:P], identb[:, :], mask_s[:, :], start=False, stop=True,
                                            skip_group_check=True)
                        last.then_inc(s_ready, 1)
                    elif kind == "V":
                        _, c, grp, final = x
                        k = V_AT[x]
                        if grp == 0:
                            o_taken.reach(nth * NC + c + 1)
                        exps.reach(nth * N_S + GROUP * (k + 1))
                        if grp == 0 and c == 0:
                            pe.wait_ge(v_ready, r + 1)
                            for h in range(2):
                                t.matmul(v_bank[VW * (2 * h + 1):VW * (2 * h + 2), 0:P], v_op[:, 1, h, :], zeros[:, :],
                                         start=True, stop=False, skip_group_check=True)
                        for b2_ in range(2):
                            for h in range(2):
                                b = 2 * grp + b2_
                                slot = (k * GROUP + 2 * b2_ + h) % P_SLOTS
                                off = max(0, b - TPC * c) * P
                                quad = 2 * h + b2_
                                last = t.matmul(v_bank[VW * quad:VW * (quad + 1), off:], v_op[:, b, h, :],
                                                prob[:, slot, off:], start=grp == 0 and not (c == 0 and b2_ == 1),
                                                stop=final, skip_group_check=True)
                        last.then_inc(pv_done, 1)
                    elif kind == "O":
                        c = x[1]
                        o_copies.reach(1 + nth * NC + c + 1)
                        row_uses.reach(nth * N_ROW + plan.row_at[x] + 1)
                        for j in range(TPC):
                            last = turn(row_bank[:, j * P:(j + 1) * P], o_sb[:, c % 2, j * P:(j + 1) * P], ident[:, :])
                        last.then_inc(o_used, 1)
                    elif kind == "X":
                        f = x[1]
                        slabs.reach(32 * (nth * SLABS + f + 1))
                        o = take_bank(x, plan, nth)
                        for j in range(SLAB_T):
                            for d in range(DC):
                                a = (d * SLAB_T + j) * P
                                last = turn(o[:, a:a + P], slab_x[:, j, d * P:(d + 1) * P], ident[:, :])
                        last.then_inc(f_ready, 1)
                    elif kind == "H":
                        _, f, u, q4 = x
                        if q4 == 0:
                            take_bank(x[:3], plan, nth)
                            if f == 0 and u == 0:
                                pe.wait_ge(w_load[par], 64 * (half + 1))
                            if u == 0:
                                by_kind["A"].reach(nth * N_KIND["A"] + A_AT[("X", f)] + 1)
                        v, d = q4 // 2, q4 % 2
                        last = t.matmul(bank[plan.bank[x[:3]]][:, v * D:(v + 1) * D],
                                        w1_sb[par][:, d, (2 * u + v) * P:(2 * u + v + 1) * P], slab_xt[:, d],
                                        start=d == 0, stop=d == 1, skip_group_check=True)
                        if q4 == 3:
                            last.then_inc(f_ready, 1)
                    elif kind == "Y":
                        _, f, s16 = x
                        buf = (nth * SLABS + f) % 2
                        j, c8 = s16 // HC, s16 % HC
                        if s16 == 0:
                            take_bank(x[:2], plan, nth)
                            hids.reach(2 + nth * N_H + HIDDEN_AT[("H", f, HC // 2 - 1)] + 1)
                        last = t.matmul(bank[plan.bank[x[:2]]][:, j * D:(j + 1) * D], hid[buf][:, c8, j * P:(j + 1) * P],
                                        w2_sb[par][:, c8, :], start=c8 == 0, stop=c8 == HC - 1, skip_group_check=True)
                        if s16 == 15:
                            last.then_inc(f_ready, 1)
                pe.wait_ge(o_used, 2 + r * NC + NC)
                pe.wait_ge(f_ready, r * N_F + N_F)
                pe.sem_inc(round_done, 1)

            pe.sem_inc(pv_done, P_SLOTS // GROUP)
            pe.sem_inc(o_used, 2)
            pe.sem_inc(round_done, 1)
            pe.wait_ge(ones_done, 1)
            pe.wait_ge(rounds_ready, 1)
            exps = Waits(pe, s_done, N_S)
            by_kind = {"M": Waits(pe, m_free, N_M), "S": exps, "A": Waits(pe, f_act, N_KIND["A"]), "D": Waits(pe, f_dve, SLABS)}
            maxima = Waits(pe, negb_done, NC)
            row_uses = Waits(pe, row_free, N_ROW)
            row_loads = [Waits(pe, row_dma[i], 32 * NC, 64) for i in range(2)]
            o_taken = Waits(pe, o_ready, NC)
            o_copies = Waits(pe, o_ready, NC, 1)
            slabs = Waits(pe, slab_dma, 32 * SLABS)
            hids = Waits(pe, hid_done, N_H, 2)
            rounds(pe, pe_round, (*by_kind.values(), maxima, row_uses, *row_loads, o_taken, o_copies, slabs, hids))

            pe.sem_inc(b_proj, 2)
            pe.wait_ge(m_free, ROUNDS * N_M)
            pe.wait_ge(s_done, ROUNDS * N_S)
            pe.wait_ge(f_act, ROUNDS * N_KIND["A"])
            pe.wait_ge(f_dve, ROUNDS * SLABS)
            def pe_back(i, n, par):
                pe.wait_ge(b_load[par], 32 * (n + 1))
                pe.wait_ge(b_aot, i + 1)
                for j in range(BT):
                    for d in range(DC):
                        a = (j * DC + d) % (CH // P) * P
                        last = turn(bank[j * D // CH][:, a:a + P], bao[par][:, j, d * P:(d + 1) * P], ident[:, :])
                last.then_inc(b_turn, 1)
                pe.wait_ge(b_out, i + 1)
                pe.wait_ge(b_beta, i + 1)
                for h in range(2):
                    t.matmul(bank[2 + 2 * par + h][:, :], ident[:, :],
                             bx[par][:, h * BT // 2:(h + 1) * BT // 2].rearrange("p j d -> p (j d)"),
                             start=True, stop=False, skip_group_check=True)
                pe.wait_ge(b_aot, i + 2)
                for j in range(BT):
                    o = bank[2 + 2 * par + j * D // CH][:, j * D % CH:j * D % CH + D]
                    for d in range(DC):
                        last = t.matmul(o, baot[par][:, j, d * P:(d + 1) * P], wo_sb[:, d], start=False, stop=d == 1,
                                        skip_group_check=True)
                last.then_inc(b_proj, 1)

            with pe.Fori(0, NB // 2) as n:
                for par in range(2):
                    pe_back(2 * n + par, n, par)

        @block.vector
        def _(dve):
            v = nc.vector
            for i in range(2):
                dve.sem_inc(row_dma[i], 64)
                dve.sem_inc(ao_store[i], 16)
                dve.sem_inc(y_store[i], 16)
                dve.sem_inc(xn_store[i], 16)
                dve.sem_inc(b_store[i], 16)
            dve.sem_inc(resid_done, 4)
            dve.sem_inc(b_out, 1)
            dve.sem_inc(row_free, 1)
            v.memset(part[:, :, :, :], 0.0).then_inc(neg_done, 1)

            def begin_chunk(n, par):
                c = 2 * n + par
                dve.wait_ge(x_dma[par], 16 * (n + 1))
                for j in range(TPC):
                    last = v.bn_stats(stats[:, par, j, :], x_in[par][:, j, :])
                last.then_inc(stat_done, 1)
                dve.wait_ge(stat_done, 2 * c + 1)
                dve.sem_inc(idle, 1)
                for j in range(TPC):
                    last = v.bn_aggr(mean_var[:, par, j, :], stats[:, par, j, :])
                last.then_inc(stat_done, 1)
                dve.wait_ge(rstd_done, 2 * c + 2)
                dve.wait_ge(xn_store[par], 16 * n + 16)
                for j in range(TPC):
                    last = v.tensor_scalar(xn[par][:, j, :], x_in[par][:, j, :], mean_var[:, par, j, 0:1],
                                           rstd[:, par, j:j + 1], ALU.subtract, ALU.mult)
                last.then_inc(xn_done, 1)

            def dve_chunk(n, par, begin_next):
                c = 2 * n + par
                begin_next()
                for w in range(4):
                    dve.wait_ge(part1, 4 * c + w + 1)
                    dve.wait_ge(split_done, 4 * c + 4)
                    v.scalar_tensor_tensor(resid[:, w], bank[2 + w][:, :], DH ** -0.5 if w < 2 else 1.0,
                                           split[par][:, 0, w], ALU.mult, ALU.subtract).then_inc(resid_done, 1)

            chunks(dve, begin_chunk, dve_chunk)

            for i in range(2):
                dve.wait_ge(xn_store[i], 16 * (NC // 2 + 1))
            dve.wait_ge(turned, NC)
            dve.wait_ge(v_free, 2 + NT)
            dve.wait_ge(consts2, 5 + 1 + 1 + E)
            steps = [0]

            def chain(ins):
                steps[0] += 1
                ins.then_inc(rt_dve, 1)
                dve.wait_ge(rt_dve, steps[0])

            def over_e(a):
                return a.unsqueeze(2).broadcast_to([P, NT, E])

            down_b = down[:, :].unsqueeze(1).broadcast_to([P, NT, E])
            chain(v.tensor_reduce(r_one[0], logits[:, :, :], AX.X, ALU.max))
            chain(v.tensor_tensor(r_tmp, logits[:, :, :], over_e(r_one[0]), ALU.subtract))
            dve.wait_ge(rt_act, 1)
            chain(v.tensor_reduce(r_one[1], r_exp, AX.X, ALU.add))
            chain(v.reciprocal(r_one[2], r_one[1]))
            chain(v.tensor_tensor(r_score, r_exp, over_e(r_one[2]), ALU.mult))
            best, index = r_small[0], r_small[1]
            for k in range(TOPK):
                src = r_score
                chain(v.tensor_reduce(best[:, k], src, AX.X, ALU.max))
                chain(v.tensor_tensor(r_tmp, src, over_e(best[:, k]), ALU.is_equal))
                chain(v.tensor_tensor(r_tmp, r_tmp, down_b, ALU.mult))
                chain(v.tensor_reduce(index[:, k], r_tmp, AX.X, ALU.max))
                chain(v.tensor_tensor(r_hot[:, k], down_b, over_e(index[:, k]), ALU.is_equal))
                v.tensor_copy(r_hotb[:, k], r_hot[:, k]).then_inc(rt_hot, 1)
                if k == 0:
                    chain(v.scalar_tensor_tensor(r_score.rearrange("p i e -> p (i e)"),
                                                 r_hot[:, 0].rearrange("p i e -> p (i e)"), -2.0,
                                                 r_score.rearrange("p i e -> p (i e)"), ALU.mult, ALU.add))
            dve.wait_ge(rt_pe, 1)
            for k in range(TOPK):
                chain(v.tensor_tensor(r_own[:, k], bank[k][:, 0:NT * E].rearrange("p (i e) -> p i e", e=E), r_hot[:, k], ALU.mult))
            assert steps[0] == 18
            loc, keep, flatpos = r_small[2], r_small[3], r_small[4]
            for k in range(TOPK):
                last = v.tensor_reduce(loc[:, k], r_own[:, k], AX.X, ALU.add)
            chain(last)
            chain(v.tensor_scalar(keep, loc, float(CAP), None, ALU.is_le))
            chain(v.tensor_scalar(flatpos, index, -float(CAP), -1.0, ALU.mult, ALU.add))
            chain(v.tensor_tensor(flatpos, flatpos, loc, ALU.add))
            chain(v.tensor_tensor(flatpos, flatpos, keep, ALU.mult))
            chain(v.tensor_scalar(flatpos, flatpos, float(E * CAP), None, ALU.add))
            chain(v.tensor_copy(pos[:, :, :], flatpos))
            chain(v.tensor_tensor(r_one[0], best[:, 0], best[:, 1], ALU.add))
            chain(v.tensor_scalar(r_one[1], r_one[0], GATE_EPS, None, ALU.max))
            chain(v.reciprocal(r_one[2], r_one[1]))
            chain(v.tensor_tensor(r_small[5], best, r_one[2].unsqueeze(1).broadcast_to([P, TOPK, NT]), ALU.mult))
            v.tensor_tensor(gate[:, :, :], r_small[5], keep, ALU.mult).then_inc(pos_ready, 1)


            def stage(op, done, value):
                for j in range(BT):
                    last = op(j)
                last.then_inc(done, 1)
                dve.wait_ge(done, value)

            def group_residual(i, n, par):
                g = rows_g[:, i]
                dve.wait_ge(b_xn[par], 16 * (n + 1))
                dve.wait_ge(b_gather[i], 16 * TOPK * BT)
                stage(lambda j: v.scalar_tensor_tensor(g[:, 0, j], g[:, 0, j], gate[:, 0, i * BT + j:i * BT + j + 1],
                                                       bxn[par][:, j], ALU.mult, ALU.add), b_res, N_RES * i + 1)
                stage(lambda j: v.scalar_tensor_tensor(g[:, 1, j], g[:, 1, j], gate[:, 1, i * BT + j:i * BT + j + 1],
                                                       g[:, 0, j], ALU.mult, ALU.add), b_res, N_RES * i + 2)
                stage(lambda j: v.bn_stats(stats[:, par, j, :], g[:, 1, j]), b_res, N_RES * i + 3)
                stage(lambda j: v.bn_aggr(b_mean_var[:, i, j, :], stats[:, par, j, :]), b_res, N_RES * i + 4)

            def group_norm(i):
                g = rows_g[:, i]
                stage(lambda j: v.scalar_tensor_tensor(g[:, 0, j], g[:, 1, j], b_mean_var[:, i, j, 0:1],
                                                       gam[:, :], ALU.subtract, ALU.mult), b_norm, i + 1)

            def dve_round(r, half, nth, plan):
                par = nth % 2
                for x in plan.steps:
                    kind = x[0]
                    if kind == "M":
                        _, h, i, j = x
                        k = M_AT[x]
                        w = (i % TPC + 1) * P if j == i // TPC else CH
                        scored.reach(nth * N_M + k + 1)
                        v.tensor_reduce(part[:, h, i, j:j + 1], bank[plan.bank[x]][:, 0:w], AX.X, ALU.max).then_inc(m_free, 1)
                    elif kind == "N":
                        c = x[1]
                        last_m = ("M", 1, TPC * c + TPC - 1, c)
                        pieces.reach(nth * N_M + M_AT[last_m] + 1)
                        b = c % 2
                        v.tensor_reduce(neg[:, b].rearrange("p (h i) -> p h i", h=2),
                                        part[:, :, TPC * c:TPC * c + TPC, 0:c + 1], AX.X, ALU.max,
                                        negate=True).then_inc(neg_done, 1)
                        negs.reach(1 + 2 * (nth * NC + c) + 1)
                        v.tensor_copy(negb[:, b, 0], neg[:, b]).then_inc(neg_done, 1)
                        negs.reach(1 + 2 * (nth * NC + c) + 2)
                        v.tensor_tensor(negb[:, b, 1], neg[:, b], negb[:, b, 0], ALU.subtract).then_inc(negb_done, 1)
                    elif kind == "R":
                        c = x[1]
                        turned_rows.reach(nth * NC + c + 1)
                        row_loads[c % 2].reach(64 * (nth * (NC // 2) + c // 2 + 1))
                        v.tensor_copy(rows[:, c % 2, :], row_b16[0:16, 0:P]).then_inc(row_free, 1)
                    elif kind == "O":
                        c = x[1]
                        b = c % 2
                        o = row_bank[:, :].rearrange("p (j s w) -> p j w s", s=2, w=VW)[:, :, 0:OW, :]
                        outputs.reach(2 + nth * NC + c + 1)
                        ao_stores[b].reach(16 * (nth * (NC // 2) + c // 2 + 1))
                        v.tensor_reduce(o_sum[:, :, :, :].rearrange("p j h w -> p (j h) w"), o, AX.X, ALU.add).then_inc(rden_done, 1)
                        rdens.reach(2 * (nth * NC + c) + 1)
                        v.reciprocal(rden[:, b], o_sum[:, :, :, DH]).then_inc(rden_done, 1)
                        rdens.reach(2 * (nth * NC + c) + 2)
                        v.tensor_tensor(ao_sb[:, b].rearrange("p j (h d) -> p j h d", h=2), o_sum[:, :, :, 0:DH],
                                        rden[:, b].unsqueeze(3).broadcast_to([P, TPC, 2, DH]), ALU.mult).then_inc(row_free, 1)
                    elif kind == "T":
                        group_residual(x[1], x[1] // 2, x[1] % 2)
                    elif kind == "U":
                        group_norm(x[1])
                    elif kind == "H" and x[3] == 3:
                        _, f, u, _ = x
                        buf = (nth * SLABS + f) % 2
                        halves.reach(nth * N_KIND["A"] + A_AT[x[:3]] + 1)
                        z = hid[buf][:, 2 * u:2 * u + 2, :].rearrange("p c t -> p (c t)")
                        v.scalar_tensor_tensor(z, tanh[:, HIDDEN_AT[x[:3]] % 2], 1.0, z, ALU.add, ALU.mult).then_inc(hid_done, 1)
                    elif kind == "Y" and x[2] == 15:
                        f = x[1]
                        k = ITEM_AT[x[:2]]
                        buf = (nth * SLABS + f) % 2
                        items.reach(nth * N_F + k + 1)
                        y_stores[buf].reach(16 * ((nth * SLABS + f) // 2 + 1))
                        v.tensor_tensor(y_sb[:, buf], bank[plan.bank[x[:2]]][:, :].rearrange("p (j d) -> p j d", j=SLAB_T),
                                        b2_sb[par][:, :].unsqueeze(1).broadcast_to([P, SLAB_T, D]), ALU.add).then_inc(f_dve, 1)

            scored = Waits(dve, m_ready, N_M)
            pieces = Waits(dve, m_free, N_M)
            negs = Waits(dve, neg_done, 2 * NC, 1)
            turned_rows = Waits(dve, row_done, NC)
            row_loads = [Waits(dve, row_dma[i], 32 * NC, 64) for i in range(2)]
            outputs = Waits(dve, o_used, NC, 2)
            ao_stores = [Waits(dve, ao_store[i], 8 * NC, 16) for i in range(2)]
            rdens = Waits(dve, rden_done, 2 * NC)
            items = Waits(dve, f_ready, N_F)
            halves = Waits(dve, f_act, N_KIND["A"])
            y_stores = [Waits(dve, y_store[i], 16 * Y_STORES[i], 16, per_pass=16 * SLABS) for i in range(2)]
            rounds(dve, dve_round, (scored, pieces, negs, turned_rows, *row_loads, outputs, *ao_stores, rdens, items, halves, *y_stores))

            def dve_back(i):
                n, par = i // 2, i % 2
                dve.wait_ge(b_proj, i + 3)
                dve.wait_ge(b_store[par], 16 * n + 16)
                dve.wait_ge(b_rstd, 2 * i + 2)
                for j in range(BT):
                    o = bank[2 + 2 * par + j * D // CH][:, j * D % CH:j * D % CH + D]
                    last = v.scalar_tensor_tensor(bout[par][:, j], rows_g[:, i, 0, j], b_dev[:, i, j:j + 1], o,
                                                  ALU.mult, ALU.add)
                last.then_inc(b_out, 1)

            for x in LATE:
                if x[0] == "T":
                    group_residual(x[1], x[1] // 2, x[1] % 2)
                elif x[0] == "U":
                    group_norm(x[1])
                else:
                    dve_back(x[1])


def kernel(**inputs):
    import numpy as np
    import concourse.bacc as bacc
    from concourse.bass_utils import run_bass_kernel_spmd

    a = {k: np.asarray(v) for k, v in inputs.items()}
    arrays = {
        "x": a["L0_attn_query"].reshape(T, D),
        "wqkv": a["L0_attn_in_proj_weight"].T,
        "wo": a["L0_attn_out_proj_weight"].T,
        "wg": a["L0_ffn_wg"],
        "w1": a["L0_ffn_fc1_w"].transpose(0, 2, 1),
        "b1": a["L0_ffn_fc1_b"].reshape(E, HC, P).transpose(2, 0, 1),
        "w2": a["L0_ffn_fc2_w"],
        "b2": a["L0_ffn_fc2_b"],
        "gamma": a["L0_ffn_ln_gamma"],
        "beta": a["L0_ffn_ln_beta"],
    }
    arrays = {k: np.ascontiguousarray(v) for k, v in arrays.items()}
    nc = bacc.Bacc("TRN2", target_bir_lowering=False, num_devices=1)
    args = {k: nc.dram_tensor(f"in_{k}", v.shape, mybir.dt.from_np(v.dtype), kind="ExternalInput").ap()
            for k, v in arrays.items()}
    out = nc.dram_tensor("out", (T, D), F32, kind="ExternalOutput").ap()
    build(nc, **args, out=out)
    r = run_bass_kernel_spmd(nc, [{f"in_{k}": v for k, v in arrays.items()}], core_ids=[0])
    return r.results[0]["out"].reshape(1, T, D)
```
